# Optimizing a Trainium2 kernel written in Bass

```python
import numpy as np
import jax
import jax.numpy as jnp

def _softmax(x, axis=-1):
    return jax.nn.softmax(x, axis=axis)

def _gelu(x):
    return jax.nn.gelu(x, approximate=True)

def _silu(x):
    return jax.nn.silu(x)

def _sigmoid(x):
    return jax.nn.sigmoid(x)

def _layernorm(x, axis=-1, eps=1e-05):
    m = jnp.mean(x, axis=axis, keepdims=True)
    v = jnp.var(x, axis=axis, keepdims=True)
    return (x - m) / jnp.sqrt(v + eps)

def _scatter_add(tgt, idx, src, axis=0):
    return tgt.at[idx].add(src)

def _segment_sum(src, seg, n):
    return jax.ops.segment_sum(src, seg, n)
kernel_name = 'mk_vit_tower_d2_tok_img256_r4_503da7'

def setup_inputs(seed: int=0):
    np.random.seed(seed)
    _w = jnp.asarray

    def _rec_inputs():
        import jax
        import jax.numpy as jnp
        _rk = jax.random.key(seed)
        x = -7.10856e-05 + 0.999911 * jax.random.normal(jax.random.fold_in(_rk, 1), (16, 64, 128, 64), jnp.float32)
        return x
    x = _rec_inputs()

    def _L0_tok_setup():
        import jax, jax.numpy as jnp
        import numpy as np
        PATCH_LEN = 16
        STRIDE = 8
        PAD = 8
        key = jax.random.key(seed)
        k1, k2 = jax.random.split(key)
        x = jax.random.normal(k1, (32, 64, 128, 64), dtype=jnp.float32)
        in_feat = 64 * (PATCH_LEN // 2 + 1) * 2
        W = jax.random.normal(k2, (64, in_feat), dtype=jnp.float32) * 0.02
        return {'x': x, 'W': W}
    _L0_tok_all = _L0_tok_setup()
    _L0_tok_in = {k: v for k, v in _L0_tok_all.items() if k in ('W',)}
    del _L0_tok_all

    def _L0_attn_setup():
        import jax, jax.numpy as jnp
        import numpy as np
        MIDC = 64
        HEADS = 16
        HEADC = MIDC // HEADS
        EPS = 1e-05

        def _layernorm(x, w, b):
            mean = jnp.mean(x, axis=-1, keepdims=True)
            std = jnp.std(x, axis=-1, keepdims=True, ddof=1)
            return w * (x - mean) / (std + EPS) + b
        key = jax.random.key(seed)
        ks = jax.random.split(key, 3)
        B, HW = (8, 4096)
        x = jax.random.normal(ks[0], (B, HW, MIDC), dtype=jnp.float32)
        W_qkv = jax.random.normal(ks[1], (3 * MIDC, MIDC), dtype=jnp.float32) * 0.02
        b_qkv = jnp.zeros((3 * MIDC,), dtype=jnp.float32)
        kln_w = jnp.ones((HEADS, 1, HEADC), dtype=jnp.float32)
        kln_b = jnp.zeros((HEADS, 1, HEADC), dtype=jnp.float32)
        vln_w = jnp.ones((HEADS, 1, HEADC), dtype=jnp.float32)
        vln_b = jnp.zeros((HEADS, 1, HEADC), dtype=jnp.float32)
        W_proj = jax.random.normal(ks[2], (MIDC, MIDC), dtype=jnp.float32) * 0.02
        b_proj = jnp.zeros((MIDC,), dtype=jnp.float32)
        return {'x': x, 'W_qkv': W_qkv, 'b_qkv': b_qkv, 'kln_w': kln_w, 'kln_b': kln_b, 'vln_w': vln_w, 'vln_b': vln_b, 'W_proj': W_proj, 'b_proj': b_proj}
    _L0_attn_all = _L0_attn_setup()
    _L0_attn_in = {k: v for k, v in _L0_attn_all.items() if k in ('W_qkv', 'b_qkv', 'kln_w', 'kln_b', 'vln_w', 'vln_b', 'W_proj', 'b_proj')}
    del _L0_attn_all

    def _L0_ffn_setup():
        import jax, jax.numpy as jnp
        import numpy as np
        E, D, H, TOP_K = (6, 64, 64, 2)
        ROUTER_H = D // 2
        key = jax.random.key(seed)
        ks = jax.random.split(key, 12)
        s = 1.0 / np.sqrt(D)
        sh = 1.0 / np.sqrt(H)
        sr = 1.0 / np.sqrt(ROUTER_H)
        return {'features': jax.random.normal(ks[0], (8, 1024, D), dtype=jnp.float32), 'router_w1': jax.random.uniform(ks[1], (D, ROUTER_H), jnp.float32, -s, s), 'router_b1': jnp.zeros((ROUTER_H,), jnp.float32), 'router_w2': jax.random.uniform(ks[2], (ROUTER_H, E), jnp.float32, -sr, sr), 'router_b2': jnp.zeros((E,), jnp.float32), 'expert_w1': jax.random.uniform(ks[3], (E, D, H), jnp.float32, -s, s), 'expert_b1': jnp.zeros((E, H), jnp.float32), 'expert_w2': jax.random.uniform(ks[4], (E, H, H), jnp.float32, -sh, sh), 'expert_b2': jnp.zeros((E, H), jnp.float32), 'expert_w3': jax.random.uniform(ks[5], (E, H, D), jnp.float32, -sh, sh), 'expert_b3': jnp.zeros((E, D), jnp.float32)}
    _L0_ffn_all = _L0_ffn_setup()
    _L0_ffn_in = {k: v for k, v in _L0_ffn_all.items() if k in ('router_w1', 'router_b1', 'router_w2', 'router_b2', 'expert_w1', 'expert_b1', 'expert_w2', 'expert_b2', 'expert_w3', 'expert_b3')}
    del _L0_ffn_all

    def _L1_attn_setup():
        import jax, jax.numpy as jnp
        import numpy as np
        B, N, D = (8, 512, 64)
        key = jax.random.key(seed)
        k1, k2, k3, k4 = jax.random.split(key, 4)
        s = D ** (-0.5)
        return {'x': jax.random.normal(k1, (B, N, D), dtype=jnp.float32), 'Wq': jax.random.normal(k2, (D, D), dtype=jnp.float32) * s, 'Wk': jax.random.normal(k3, (D, D), dtype=jnp.float32) * s, 'Wv': jax.random.normal(k4, (D, D), dtype=jnp.float32) * s}
    _L1_attn_all = _L1_attn_setup()
    _L1_attn_in = {k: v for k, v in _L1_attn_all.items() if k in ('Wq', 'Wk', 'Wv')}
    del _L1_attn_all

    def _L1_ffn_setup():
        import jax, jax.numpy as jnp
        import numpy as np
        B, S, H, NH, NE = (4, 256, 64, 4, 4)
        D = H // NH
        EPS = 1e-08

        def layernorm(x, g, b):
            m = jnp.mean(x, axis=-1, keepdims=True)
            v = jnp.mean((x - m) ** 2, axis=-1, keepdims=True)
            return (x - m) / jnp.sqrt(v + EPS) * g + b
        key = jax.random.key(seed)
        ks = jax.random.split(key, 18)
        sc = 0.05
        return {'x': jax.random.normal(ks[0], (B, S, H), jnp.float32), 'hl_w': jax.random.normal(ks[1], (NH, D, H), jnp.float32) * sc, 'hl_b': jax.random.normal(ks[2], (NH, D), jnp.float32) * sc, 'wq': jax.random.normal(ks[3], (NH, NE, D, D), jnp.float32) * sc, 'wk': jax.random.normal(ks[4], (NH, D, D), jnp.float32) * sc, 'wv': jax.random.normal(ks[5], (NH, D, D), jnp.float32) * sc, 'gate_w': jax.random.normal(ks[6], (NH, NE, NE * D), jnp.float32) * sc, 'gate_b': jax.random.normal(ks[7], (NH, NE), jnp.float32) * sc, 'ln_g': jnp.ones((D,), jnp.float32), 'ln_b': jnp.zeros((D,), jnp.float32), 'fc1_w': jax.random.normal(ks[8], (D, D), jnp.float32) * sc, 'fc1_b': jax.random.normal(ks[9], (D,), jnp.float32) * sc, 'fc2_w': jax.random.normal(ks[10], (D, D), jnp.float32) * sc, 'fc2_b': jax.random.normal(ks[11], (D,), jnp.float32) * sc, 'fnorm_g': jnp.ones((D,), jnp.float32), 'fnorm_b': jnp.zeros((D,), jnp.float32), 'fgate_w': jax.random.normal(ks[12], (NH, H), jnp.float32) * sc}
    _L1_ffn_all = _L1_ffn_setup()
    _L1_ffn_in = {k: v for k, v in _L1_ffn_all.items() if k in ('hl_w', 'hl_b', 'wq', 'wk', 'wv', 'gate_w', 'gate_b', 'ln_g', 'ln_b', 'fc1_w', 'fc1_b', 'fc2_w', 'fc2_b', 'fnorm_g', 'fnorm_b', 'fgate_w')}
    del _L1_ffn_all
    return {'x': x, 'L0_tok_W': _L0_tok_in['W'], 'L0_attn_W_qkv': _L0_attn_in['W_qkv'], 'L0_attn_b_qkv': _L0_attn_in['b_qkv'], 'L0_attn_kln_w': _L0_attn_in['kln_w'], 'L0_attn_kln_b': _L0_attn_in['kln_b'], 'L0_attn_vln_w': _L0_attn_in['vln_w'], 'L0_attn_vln_b': _L0_attn_in['vln_b'], 'L0_attn_W_proj': _L0_attn_in['W_proj'], 'L0_attn_b_proj': _L0_attn_in['b_proj'], 'L0_ffn_router_w1': _L0_ffn_in['router_w1'], 'L0_ffn_router_b1': _L0_ffn_in['router_b1'], 'L0_ffn_router_w2': _L0_ffn_in['router_w2'], 'L0_ffn_router_b2': _L0_ffn_in['router_b2'], 'L0_ffn_expert_w1': _L0_ffn_in['expert_w1'], 'L0_ffn_expert_b1': _L0_ffn_in['expert_b1'], 'L0_ffn_expert_w2': _L0_ffn_in['expert_w2'], 'L0_ffn_expert_b2': _L0_ffn_in['expert_b2'], 'L0_ffn_expert_w3': _L0_ffn_in['expert_w3'], 'L0_ffn_expert_b3': _L0_ffn_in['expert_b3'], 'L1_attn_Wq': _L1_attn_in['Wq'], 'L1_attn_Wk': _L1_attn_in['Wk'], 'L1_attn_Wv': _L1_attn_in['Wv'], 'L1_ffn_hl_w': _L1_ffn_in['hl_w'], 'L1_ffn_hl_b': _L1_ffn_in['hl_b'], 'L1_ffn_wq': _L1_ffn_in['wq'], 'L1_ffn_wk': _L1_ffn_in['wk'], 'L1_ffn_wv': _L1_ffn_in['wv'], 'L1_ffn_gate_w': _L1_ffn_in['gate_w'], 'L1_ffn_gate_b': _L1_ffn_in['gate_b'], 'L1_ffn_ln_g': _L1_ffn_in['ln_g'], 'L1_ffn_ln_b': _L1_ffn_in['ln_b'], 'L1_ffn_fc1_w': _L1_ffn_in['fc1_w'], 'L1_ffn_fc1_b': _L1_ffn_in['fc1_b'], 'L1_ffn_fc2_w': _L1_ffn_in['fc2_w'], 'L1_ffn_fc2_b': _L1_ffn_in['fc2_b'], 'L1_ffn_fnorm_g': _L1_ffn_in['fnorm_g'], 'L1_ffn_fnorm_b': _L1_ffn_in['fnorm_b'], 'L1_ffn_fgate_w': _L1_ffn_in['fgate_w']}

def reference(x, L0_tok_W, L0_attn_W_qkv, L0_attn_b_qkv, L0_attn_kln_w, L0_attn_kln_b, L0_attn_vln_w, L0_attn_vln_b, L0_attn_W_proj, L0_attn_b_proj, L0_ffn_router_w1, L0_ffn_router_b1, L0_ffn_router_w2, L0_ffn_router_b2, L0_ffn_expert_w1, L0_ffn_expert_b1, L0_ffn_expert_w2, L0_ffn_expert_b2, L0_ffn_expert_w3, L0_ffn_expert_b3, L1_attn_Wq, L1_attn_Wk, L1_attn_Wv, L1_ffn_hl_w, L1_ffn_hl_b, L1_ffn_wq, L1_ffn_wk, L1_ffn_wv, L1_ffn_gate_w, L1_ffn_gate_b, L1_ffn_ln_g, L1_ffn_ln_b, L1_ffn_fc1_w, L1_ffn_fc1_b, L1_ffn_fc2_w, L1_ffn_fc2_b, L1_ffn_fnorm_g, L1_ffn_fnorm_b, L1_ffn_fgate_w):
    import jax
    import jax.numpy as jnp

    def _L0_tok_ref(x, W):
        import jax, jax.numpy as jnp
        import numpy as np
        PATCH_LEN = 16
        STRIDE = 8
        PAD = 8
        B, C, T, V = x.shape
        xp = jnp.pad(x, ((0, 0), (0, 0), (0, PAD), (0, 0)), mode='edge')
        Tp = T + PAD
        N = (Tp - PATCH_LEN) // STRIDE + 1
        idx = jnp.arange(N)[:, None] * STRIDE + jnp.arange(PATCH_LEN)[None, :]
        patches = xp[:, :, idx, :]
        patches = jnp.transpose(patches, (0, 4, 2, 3, 1))
        xf = jnp.fft.rfft(patches, axis=-2, norm='ortho')
        F = xf.shape[-2]
        x_real = xf.real.reshape(B, V, N, F * C)
        x_imag = xf.imag.reshape(B, V, N, F * C)
        x_emb = jnp.concatenate([x_real, x_imag], axis=-1)
        x_emb = x_emb @ W.T
        return x_emb.reshape(B, V * N, -1)

    def _L0_attn_ref(x, W_qkv, b_qkv, kln_w, kln_b, vln_w, vln_b, W_proj, b_proj):
        import jax, jax.numpy as jnp
        import numpy as np
        MIDC = 64
        HEADS = 16
        HEADC = MIDC // HEADS
        EPS = 1e-05

        def _layernorm(x, w, b):
            mean = jnp.mean(x, axis=-1, keepdims=True)
            std = jnp.std(x, axis=-1, keepdims=True, ddof=1)
            return w * (x - mean) / (std + EPS) + b
        B, HW, C = x.shape
        bias = x
        qkv = jnp.einsum('bnc,oc->bno', x, W_qkv) + b_qkv
        qkv = qkv.reshape(B, HW, HEADS, 3 * HEADC).transpose(0, 2, 1, 3)
        q, k, v = jnp.split(qkv, 3, axis=-1)
        k = _layernorm(k, kln_w, kln_b)
        v = _layernorm(v, vln_w, vln_b)
        kv = jnp.einsum('bhnd,bhne->bhde', k, v) / HW
        out = jnp.einsum('bhnd,bhde->bhne', q, kv)
        out = out.transpose(0, 2, 1, 3).reshape(B, HW, C)
        ret = out + bias
        proj = jnp.einsum('bnc,oc->bno', ret, W_proj) + b_proj
        return jax.nn.gelu(proj, approximate=False) + bias

    def _L0_ffn_ref(features, router_w1, router_b1, router_w2, router_b2, expert_w1, expert_b1, expert_w2, expert_b2, expert_w3, expert_b3):
        import jax, jax.numpy as jnp
        import numpy as np
        E, D, H, TOP_K = (6, 64, 64, 2)
        ROUTER_H = D // 2
        rh = jax.nn.relu(features @ router_w1 + router_b1)
        expert_logits = jax.nn.softmax(rh @ router_w2 + router_b2, axis=-1)
        top_w, top_i = jax.lax.top_k(expert_logits, TOP_K)
        routing_weights = jax.nn.softmax(top_w, axis=-1)
        h1 = jax.nn.relu(jnp.einsum('bsd,edh->bseh', features, expert_w1) + expert_b1)
        h2 = jax.nn.relu(jnp.einsum('bseh,ehf->bsef', h1, expert_w2) + expert_b2)
        expert_out = jnp.einsum('bsef,efo->bseo', h2, expert_w3) + expert_b3
        sel = jnp.take_along_axis(expert_out, top_i[:, :, :, None], axis=2)
        combined = jnp.sum(sel * routing_weights[..., None], axis=2)
        return combined

    def _L1_attn_ref(x, Wq, Wk, Wv):
        import jax, jax.numpy as jnp
        import numpy as np
        B, N, D = (8, 512, 64)
        q = jnp.einsum('bnd,ed->bne', x, Wq)
        k = jnp.einsum('bnd,ed->bne', x, Wk)
        v = jnp.einsum('bnd,ed->bne', x, Wv)
        energy = jnp.einsum('bqd,bkd->bqk', q, k)
        scaling = jnp.asarray(x.shape[-1] ** (-0.5), x.dtype)
        att = jax.nn.softmax(energy, axis=-1) * scaling
        out = jnp.einsum('bqk,bkv->bqv', att, v)
        return out

    def _L1_ffn_ref(x, hl_w, hl_b, wq, wk, wv, gate_w, gate_b, ln_g, ln_b, fc1_w, fc1_b, fc2_w, fc2_b, fnorm_g, fnorm_b, fgate_w):
        import jax, jax.numpy as jnp
        import numpy as np
        B, S, H, NH, NE = (4, 256, 64, 4, 4)
        D = H // NH
        EPS = 1e-08

        def layernorm(x, g, b):
            m = jnp.mean(x, axis=-1, keepdims=True)
            v = jnp.mean((x - m) ** 2, axis=-1, keepdims=True)
            return (x - m) / jnp.sqrt(v + EPS) * g + b
        b, s, h = x.shape
        nh, d, _ = wk.shape
        ne = wq.shape[1]
        sx = jnp.einsum('bsh,ndh->bnsd', x, hl_w) + hl_b[None, :, None, :]
        pad = sx == 0
        q = jnp.einsum('bnsd,neod->bneso', sx, wq)
        k = jnp.einsum('bnsd,nod->bnso', sx, wk)
        v = jnp.einsum('bnsd,nod->bnso', sx, wv)
        causal = jnp.where(jnp.tril(jnp.ones((s, s), bool)), 0.0, -jnp.inf).astype(x.dtype)
        scores = jnp.einsum('bnesd,bntd->bnest', q, k) * d ** 0.5 + causal
        att = jax.nn.softmax(scores, axis=-1)
        qkv = jnp.einsum('bnest,bntd->bnesd', att, v)
        qkv = jnp.where(pad[:, :, None], 0.0, qkv)
        out = jnp.transpose(qkv, (0, 1, 3, 2, 4)).reshape(b, nh, s, ne * d)
        gs = jax.nn.softmax(jnp.einsum('bnsf,nef->bnse', out, gate_w) + gate_b[None, :, None, :], axis=-1)
        mixed = jnp.einsum('bnsed,bnse->bnsd', out.reshape(b, nh, s, ne, d), gs)
        resid = sx[jnp.arange(nh), jnp.arange(nh)]
        hn = layernorm(mixed + resid, ln_g, ln_b)
        f_n = jnp.transpose(hn, (0, 2, 1, 3)).reshape(b, s, h)
        fx = f_n.reshape(b, s, nh, d)
        pm = fx == 0
        hx = jnp.where(pm, 0.0, fx @ fc1_w.T + fc1_b)
        hx = jax.nn.relu(hx)
        hx = jnp.where(pm, 0.0, hx @ fc2_w.T + fc2_b)
        hx = layernorm(hx + fx, fnorm_g, fnorm_b)
        fout = hx.reshape(b, s, h)
        fg = jax.nn.softmax(fout @ fgate_w.T, axis=-1)
        return (fout.reshape(b, s, nh, d) * fg[..., None]).reshape(b, s, h)
    h = _L0_tok_ref(x, L0_tok_W)
    h = h + _L0_attn_ref(_layernorm(h, axis=-1), L0_attn_W_qkv, L0_attn_b_qkv, L0_attn_kln_w, L0_attn_kln_b, L0_attn_vln_w, L0_attn_vln_b, L0_attn_W_proj, L0_attn_b_proj)
    h = h + _L0_ffn_ref(_layernorm(h, axis=-1), L0_ffn_router_w1, L0_ffn_router_b1, L0_ffn_router_w2, L0_ffn_router_b2, L0_ffn_expert_w1, L0_ffn_expert_b1, L0_ffn_expert_w2, L0_ffn_expert_b2, L0_ffn_expert_w3, L0_ffn_expert_b3)
    h = h + _L1_attn_ref(_layernorm(h, axis=-1), L1_attn_Wq, L1_attn_Wk, L1_attn_Wv)
    h = h + _L1_ffn_ref(_layernorm(h, axis=-1), L1_ffn_hl_w, L1_ffn_hl_b, L1_ffn_wq, L1_ffn_wk, L1_ffn_wv, L1_ffn_gate_w, L1_ffn_gate_b, L1_ffn_ln_g, L1_ffn_ln_b, L1_ffn_fc1_w, L1_ffn_fc1_b, L1_ffn_fc2_w, L1_ffn_fc2_b, L1_ffn_fnorm_g, L1_ffn_fnorm_b, L1_ffn_fgate_w)
    return h

_drawn_inputs = setup_inputs


def setup_inputs(seed=0):
    import zlib

    import numpy as np

    out = dict(_drawn_inputs(seed))
    spreads = {'L0_attn_b_qkv': (0.0, 0.8),
     'L0_attn_kln_w': (1.0, 0.6),
     'L0_attn_kln_b': (0.0, 0.8),
     'L0_attn_vln_w': (1.0, 0.6),
     'L0_attn_vln_b': (0.0, 0.8),
     'L0_attn_b_proj': (0.0, 0.1),
     'L0_ffn_router_b1': (0.0, 0.275),
     'L0_ffn_router_b2': (0.0, 0.1),
     'L0_ffn_expert_b1': (0.0, 0.8),
     'L0_ffn_expert_b2': (0.0, 0.403),
     'L0_ffn_expert_b3': (0.0, 0.1),
     'L1_ffn_ln_g': (1.0, 0.582),
     'L1_ffn_ln_b': (0.0, 0.462),
     'L1_ffn_fnorm_g': (1.0, 0.2),
     'L1_ffn_fnorm_b': (0.0, 0.449)}
    factors = {'L0_attn_W_qkv': 8.0,
     'L1_ffn_wq': 8.0,
     'L1_ffn_wk': 8.0,
     'L1_ffn_wv': 8.0,
     'L1_ffn_gate_w': 8.0,
     'L1_ffn_gate_b': 8.0,
     'L1_ffn_fc1_w': 8.0,
     'L1_ffn_fc1_b': 8.0,
     'L1_ffn_fc2_w': 8.0,
     'L1_ffn_fc2_b': 4.364}
    for name, (base, spread) in spreads.items():
        noise = np.random.default_rng([zlib.crc32(name.encode()), seed]).standard_normal(out[name].shape)
        drawn = base * np.exp(spread * noise) if base else spread * noise
        out[name] = jnp.asarray(drawn.astype(out[name].dtype))
    for name, factor in factors.items():
        out[name] = (out[name] * factor).astype(out[name].dtype)
    return out
```

```python
from contextlib import ExitStack

import concourse.bass as bass
import numpy as np
from concourse import mybir

F32 = mybir.dt.float32
F32R = mybir.dt.float32r
BF16 = mybir.dt.bfloat16
ALU = mybir.AluOpType
ACT = mybir.ActivationFunctionType
AX_X = mybir.AxisListType.X

P = 128
B, C, T, V = 16, 64, 128, 64
D = 64
PATCH, STRIDE = 16, 8
NP = T // STRIDE
S = V * NP
NT = S // P
NF = PATCH // 2 + 1
E6 = 6
NH, NE, DH = 4, 4, 16
NEG = -1.0e30
PRIME = 32


def columns(table):
    at, where = 0, {}
    for name, rows, cols in table:
        where[name] = (rows, at, cols)
        at += cols
    return where, at


WEIGHTS, W_COLS = columns(
    [("kvT", 128, 65), ("ak", 65, 64), ("av", 65, 64), ("wqT", 65, 65), ("wpT", 64, 64), ("bp", 65, 64),
     ("rw1", 128, 33), ("rb1", 33, 1), ("rw2", 33, E6), ("ew1", 128, E6 * D), ("eb1", 128, 3), ("ew2", 128, 3 * 128), ("eb2", 128, 3),
     ("ew3", 128, 3 * D), ("eb3", 32 + E6, D), ("wqq", 128, 128), ("wkk", 128, 128), ("wv1", 128, 64),
     ])
F_WEIGHTS, F_COLS = columns(
    [("hlT", DH + 1, NH * 65), ("hlmask", 65, NH * 128), ("hlres", 65, NH * DH),
     ("proj", DH + 1, NH * 322), ("gate", 128, NH * 84), ("gate_b", 128, NH * NE),
     ("ln_g", 128, D), ("ln_b", 128, D), ("fc1", 64, 128), ("fc1_b", 64, 1), ("fc2", 65, 64),
     ("fn_g", 128, D), ("fn_b", 128, D), ("fgate", 64, NH)])
CONSTS, C_COLS = columns(
    [("ident", 128, 128), ("center4", 128, 128), ("kvmask", 64, 64), ("iaug", 64, 65), ("dft", 2 * NF, PATCH),
     ("rank", 128, NT * E6), ("pair", 32 + E6, 3 * 128)])


def constants():
    out = np.zeros((P, C_COLS), np.float32)

    def put(name, a):
        rows, at, cols = CONSTS[name]
        out[:rows, at:at + cols] = a

    put("ident", np.eye(128))
    put("center4", np.eye(128) - np.kron(np.eye(32), np.full((4, 4), 0.25)))
    put("kvmask", np.kron(np.eye(16), np.ones((4, 4))) / S)
    put("iaug", np.eye(64, 65))
    t, f = np.arange(PATCH), np.arange(NF)
    angle = 2.0 * np.pi * np.outer(f, t) / PATCH
    dft = np.concatenate([np.cos(angle), -np.sin(angle)]) / np.sqrt(PATCH)
    put("dft", dft.reshape(2 * NF, 2, 2, 4).transpose(0, 2, 3, 1).reshape(2 * NF, PATCH))
    put("rank", np.tile(np.arange(E6, 0, -1), NT))
    pair = np.kron(np.eye(E6), np.ones((1, 64)))
    put("pair", np.concatenate([pair, np.zeros((32 - E6, E6 * 64)), pair]))
    return out


class Step:

    def __init__(self, sem):
        self.sem = sem

    @staticmethod
    def now(q):
        return q + (PRIME + 1)

    @staticmethod
    def before(q, depth):
        return q + (PRIME + 1 - depth)


def prime(engine, steps):
    for s in steps:
        engine.sem_inc(s.sem, PRIME)


class Tower:

    def __init__(self, nc, ctx):
        self.nc, self.ctx = nc, ctx
        self.h = self.sb("h", [P, B, NT * D])
        self.f = self.sb("f", [P, F_COLS])
        self.c = self.sb("c", [P, C_COLS])
        self.neg_half = self.sb("neg_half", [P, NT])

    def sb(self, name, shape, dt=F32):
        return self.ctx.enter_context(self.nc.sbuf_tensor(name, shape, dt))

    def wt(self, name, rows=None, lo=0, n=None):
        r, at, cols = WEIGHTS[name]
        return self.w[0:rows or r, at + lo:at + lo + (n or cols)]

    def fw(self, name, rows=None, lo=0, n=None):
        r, at, cols = F_WEIGHTS[name]
        return self.f[0:rows or r, at + lo:at + lo + (n or cols)]

    def ct(self, name, rows=None, lo=0, n=None):
        r, at, cols = CONSTS[name]
        return self.c[0:rows or r, at + lo:at + lo + (n or cols)]

    def h_at(self, b):
        return self.h[:, bass.ds(b, 1), :].rearrange("p a (t f) -> p (a t) f", f=D)


class Stage:

    def __init__(self, tw, name):
        self.tw, self.nc, self.name, self.ctx, self.sems = tw, tw.nc, name, ExitStack(), []

    def __enter__(self):
        return self

    def __exit__(self, *a):
        self.ctx.close()
        self.nc.clear_and_free_semaphores(self.sems)
        self.nc.all_engine_barrier()

    def sb(self, name, shape, dt=F32):
        return self.ctx.enter_context(self.nc.sbuf_tensor(f"{self.name}_{name}", shape, dt))

    def ps(self, name, shape, dt=F32):
        return self.ctx.enter_context(self.nc.psum_tensor(f"{self.name}_{name}", shape, dt))

    def sem(self, name):
        self.sems.append(self.nc.alloc_semaphore(f"{self.name}_{name}"))
        return self.sems[-1]

    def steps(self, names):
        return [Step(self.sem(n)) for n in names.split()]


def bc(ap, n):
    return ap.unsqueeze(2).to_broadcast([ap.shape[0], ap.shape[1], n])


def load_inputs(tw, weights, f_weights, consts):
    nc = tw.nc
    with Stage(tw, "load") as st:
        arrived = st.sem("arrived")
        with nc.Block() as block:
            @block.sync
            def _(sp):
                sp.dma_start(tw.w[:, :], weights).then_inc(arrived, 16)
                sp.dma_start(tw.c[:, :], consts).then_inc(arrived, 16)
                sp.dma_start(tw.f[:, :], f_weights).then_inc(arrived, 16)
                sp.wait_ge(arrived, 48)

            @block.vector
            def _(dve):
                nc.vector.memset(tw.neg_half[:, :], -0.5)


def tokens(tw, x, tok_w):
    nc, U = tw.nc, 2
    with Stage(tw, "tok") as st:
        rf = st.sb("rf", [2 * NF, D * C])
        wt = st.sb("wt", [P, 8, D])
        xs = [st.sb(f"x{u}", [P, NP + 1, 4, V]) for u in range(U)]
        embT = [st.sb(f"embT{u}", [P, 512]) for u in range(U)]
        ps_e = st.ps("ps_e", [P, U, 512])
        ps_h = st.ps("ps_h", [P, U, 2, 512])
        rf_in, fold_mm, fold_sb = st.sem("rf_in"), st.sem("fold_mm"), st.sem("fold_sb")
        x_in = [st.sem(f"x_in{u}") for u in range(U)]
        emb_mm, emb_sb, tr_mm, h_out = st.steps("emb_mm emb_sb tr_mm h_out")
        xr = x.rearrange("b c (m h s) v -> b h c m (s v)", h=2, s=4)
        with nc.Block() as block:
            @block.sync
            def _(sp):
                sp.dma_start(rf[:, :], tok_w).then_inc(rf_in, 16)
                with sp.Fori(0, B // U) as i:
                    for u in range(U):
                        b = i * U + u
                        sp.wait_ge(emb_mm.sem, emb_mm.before(b, U))
                        for hh in range(2):
                            rows = slice(64 * hh, 64 * hh + 64)
                            sp.dma_start(xs[u][rows, 0:NP, :, :].rearrange("c m s v -> c m (s v)"),
                                         xr[bass.ds(b, 1), hh].rearrange("a c m f -> (a c) m f")
                                         ).then_inc(x_in[u], 16)
                            edge = x[bass.ds(b, 1), :, T - 1, :].rearrange("a c v -> (a c) v")
                            sp.dma_start(xs[u][rows, NP, :, :],
                                         edge.unsqueeze(1).to_broadcast([C, 4, V])).then_inc(x_in[u], 16)

            @block.tensor
            def _(pe):
                prime(pe, [emb_mm, tr_mm])
                pe.wait_ge(rf_in, 16)
                for hh in range(2):
                    for o in range(D):
                        last = nc.tensor.matmul(
                            ps_h[64 * hh:64 * hh + 64, 0, 0, 8 * o:8 * o + 8], rf[:, C * o:C * o + C],
                            tw.ct("dft", lo=8 * hh, n=8), start=True, stop=True, tile_position=(0, 64 * hh))
                last.then_inc(fold_mm, 1)
                pe.wait_ge(fold_sb, 1)
                with pe.Fori(0, B // U) as i:
                    for u in range(U):
                        b = i * U + u
                        pe.wait_ge(x_in[u], (i + 1) * 64)
                        pe.wait_ge(emb_sb.sem, emb_sb.before(b, U))
                        for kk in range(8):
                            s, chunk = kk // 2, kk % 2
                            for vh in range(2):
                                last = nc.tensor.matmul(
                                    ps_e[64 * vh:64 * vh + 64, u, :], wt[:, kk, :],
                                    xs[u][:, chunk:chunk + NP, s, 32 * vh:32 * vh + 32],
                                    start=kk == 0, stop=kk == 7, tile_position=(0, 64 * vh))
                        last.then_inc(emb_mm.sem, 1)
                    for u in range(U):
                        b = i * U + u
                        pe.wait_ge(emb_sb.sem, emb_sb.now(b))
                        pe.wait_ge(h_out.sem, h_out.before(b, U))
                        for vh in range(2):
                            rows = slice(64 * vh, 64 * vh + 64)
                            for t in range(NT // 2):
                                last = nc.tensor.matmul(
                                    ps_h[:, u, vh, D * t:D * t + D], embT[u][rows, P * t:P * t + P],
                                    tw.c[rows, CONSTS["ident"][1] + 64 * vh:CONSTS["ident"][1] + 64 * vh + 64],
                                    start=True, stop=True)
                        last.then_inc(tr_mm.sem, 1)

            @block.scalar
            def _(act):
                prime(act, [emb_sb])
                act.wait_ge(fold_mm, 1)
                nc.scalar.copy(wt[:, :, :], ps_h[:, 0, 0, :].rearrange("p (o k) -> p k o", k=8)).then_inc(fold_sb, 1)
                with act.Fori(0, B // U) as i:
                    for u in range(U):
                        b = i * U + u
                        act.wait_ge(emb_mm.sem, emb_mm.now(b))
                        act.wait_ge(tr_mm.sem, tr_mm.before(b, U))
                        nc.scalar.copy(embT[u][:, :].rearrange("p (v n) -> p v n", n=NP),
                                       ps_e[:, u, :].rearrange("p (n v) -> p v n", n=NP)).then_inc(emb_sb.sem, 1)

            @block.vector
            def _(dve):
                prime(dve, [h_out])
                with dve.Fori(0, B // U) as i:
                    for u in range(U):
                        b = i * U + u
                        dve.wait_ge(tr_mm.sem, tr_mm.now(b))
                        nc.vector.tensor_copy(
                            tw.h[:, bass.ds(b, 1), :].rearrange("p a (g f) -> p (a g) f", g=2),
                            ps_h[:, u, :, 0:256]).then_inc(h_out.sem, 1)


class Norm:

    def __init__(self, st, U):
        self.st, self.nc, self.U = st, st.nc, U
        self.xn = [st.sb(f"xn{u}", [P, NT, D]) for u in range(U)]
        self.xc = [st.sb(f"xc{u}", [P, NT, D]) for u in range(U)]
        self.sq = [st.sb(f"sq{u}", [P, NT, D]) for u in range(U)]
        self.stat = [st.sb(f"stat{u}", [P, 5, NT]) for u in range(U)]
        self.sum, self.mean, self.cent, self.sqr, self.var, self.eps, self.rstd, self.out = st.steps(
            "ln_sum ln_mean ln_cent ln_sqr ln_var ln_eps ln_rstd ln_out")
        self.dve_steps = [self.sum, self.mean, self.cent, self.var, self.eps, self.out]

    def center(self, dve, q, u, xn_used, b=None):
        nc, stat, h = self.nc, self.stat[u], self.st.tw.h_at(q if b is None else b)
        dve.wait_ge(xn_used.sem, xn_used.before(q, self.U))
        nc.vector.reduce_sum(stat[:, 0, :], h, axis=AX_X).then_inc(self.sum.sem, 1)
        dve.wait_ge(self.sum.sem, self.sum.now(q))
        nc.vector.tensor_scalar(stat[:, 1, :], stat[:, 0, :], 1.0 / D, None, ALU.mult).then_inc(self.mean.sem, 1)
        dve.wait_ge(self.mean.sem, self.mean.now(q))
        nc.vector.tensor_tensor(self.xc[u][:, :, :], h, bc(stat[:, 1, :], D),
                                ALU.subtract).then_inc(self.cent.sem, 1)

    def square(self, act, q, u):
        act.wait_ge(self.cent.sem, self.cent.now(q))
        self.nc.scalar.activation(self.sq[u][:, :, :], self.xc[u][:, :, :], ACT.Square).then_inc(self.sqr.sem, 1)

    def variance(self, dve, q, u):
        dve.wait_ge(self.sqr.sem, self.sqr.now(q))
        stat = self.stat[u]
        self.nc.vector.reduce_sum(stat[:, 2, :], self.sq[u][:, :, :], axis=AX_X).then_inc(self.var.sem, 1)
        dve.wait_ge(self.var.sem, self.var.now(q))
        self.nc.vector.tensor_scalar(stat[:, 3, :], stat[:, 2, :], 1.0 / D, 1e-5, ALU.mult,
                                     ALU.add).then_inc(self.eps.sem, 1)

    def inverse_root(self, pool, q, u):
        nc, stat = self.nc, self.stat[u]
        pool.wait_ge(self.eps.sem, self.eps.now(q))
        nc.gpsimd.tensor_tensor(stat[:, 4, :], stat[:, 3, :], self.st.tw.neg_half[:, :],
                                ALU.pow).then_inc(self.rstd.sem, 1)

    def scale(self, dve, q, u):
        dve.wait_ge(self.rstd.sem, self.rstd.now(q))
        self.nc.vector.tensor_tensor(self.xn[u][:, :, :], self.xc[u][:, :, :], bc(self.stat[u][:, 4, :], D),
                                     ALU.mult).then_inc(self.out.sem, 1)

    def scale_twice(self, pool, q, u, xn2, used):
        pool.wait_ge(self.rstd.sem, self.rstd.now(q))
        pool.wait_ge(used.sem, used.before(q, self.U))
        for k in range(2):
            last = self.nc.gpsimd.tensor_tensor(xn2[:, :, k, :], self.xc[u][:, :, :], bc(self.stat[u][:, 4, :], D),
                                                ALU.mult)
        last.then_inc(self.out.sem, 1)

    def transpose(self, pe, q, u, ps_x, done):
        pe.wait_ge(self.out.sem, self.out.now(q))
        for t in range(NT // 2):
            last = self.nc.tensor.transpose(ps_x[:, P * t:P * t + P], self.xn[u][:, 2 * t:2 * t + 2, :],
                                            self.st.tw.ct("ident"))
        last.then_inc(done.sem, 1)

    def features(self, act, xT, ps_x, done):
        for par in range(2):
            last = self.nc.scalar.copy(
                xT[0:D, :].rearrange("p (t e n) -> p e t n", e=2, n=P)[:, par],
                ps_x[D * par:D * par + D, :].rearrange("p (t n) -> p t n", n=P))
        last.then_inc(done.sem, 1)


def linear_attention(tw):
    nc, U = tw.nc, 2
    with Stage(tw, "lin") as st:
        ln = Norm(st, U)
        wkv = st.sb("wkv", [65, 128])
        xT = [st.sb(f"xT{u}", [65, S]) for u in range(U)]
        kv_sq = st.sb("kv_sq", [P, S])
        dev = [st.sb(f"dev{u}", [P, 3, 256]) for u in range(U)]
        z = [st.sb(f"z{u}", [P, 2 * NT, 65]) for u in range(U)]
        small = [st.sb(f"small{u}", [65, 6, 65]) for u in range(U)]
        g = [st.sb(f"g{u}", [P, NT, D]) for u in range(U)]
        g2 = [st.sb(f"g2{u}", [P, NT, D]) for u in range(U)]
        ps_x = st.ps("ps_x", [P, 512])
        ps_kv = st.ps("ps_kv", [P, S])
        ps_s = st.ps("ps_s", [P, U, 512])
        ps_p = st.ps("ps_p", [P, U, 512])
        wkv_mm, wkv_sb = st.sem("wkv_mm"), st.sem("wkv_sb")
        (xT_mm, xT_sb, kv_mm, kv_sqr, kv_ss, kv_sd, kv_eps, kv_r, z_out, gram_mm, gram_sb, a_mm, a_sb, m_mm,
         m_sb, r_mm, r_sb, w_mm, w_sb, p_mm, gelu, g_add, h_add) = st.steps(
            "xT_mm xT_sb kv_mm kv_sqr kv_ss kv_sd kv_eps kv_r z_out gram_mm gram_sb a_mm a_sb m_mm m_sb r_mm r_sb "
            "w_mm w_sb p_mm gelu g_add h_add")
        with nc.Block() as block:
            @block.tensor
            def _(pe):
                prime(pe, [xT_mm, kv_mm, gram_mm, a_mm, m_mm, r_mm, w_mm, p_mm])
                nc.tensor.matmul(ps_s[0:65, 0, 0:128], tw.wt("kvT"), tw.ct("center4"),
                                 start=True, stop=True).then_inc(wkv_mm, 1)
                pe.wait_ge(wkv_sb, 1)
                with pe.Fori(0, B // U) as i:
                    for u in range(U):
                        q = i * U + u
                        pe.wait_ge(xT_sb.sem, xT_sb.before(q, 1))
                        ln.transpose(pe, q, u, ps_x, xT_mm)
                        pe.wait_ge(xT_sb.sem, xT_sb.now(q))
                        pe.wait_ge(z_out.sem, z_out.before(q, 1))
                        for t in range(NT):
                            last = nc.tensor.matmul(ps_kv[:, P * t:P * t + P], xT[u][:, P * t:P * t + P],
                                                    wkv[:, :], start=True, stop=True)
                        last.then_inc(kv_mm.sem, 1)
                    for u in range(U):
                        q = i * U + u
                        pe.wait_ge(z_out.sem, z_out.now(q))
                        pe.wait_ge(w_sb.sem, w_sb.before(q, U))
                        for t in range(NT):
                            last = nc.tensor.matmul(ps_s[0:65, u, 0:65], z[u][:, 2 * t + 1, :], z[u][:, 2 * t, :],
                                                    start=t == 0, stop=t == NT - 1)
                        last.then_inc(gram_mm.sem, 1)
                    for u in range(U):
                        q = i * U + u
                        pe.wait_ge(gram_sb.sem, gram_sb.now(q))
                        nc.tensor.matmul(ps_s[0:65, u, 0:64], small[u][:, 0, :], tw.wt("av"),
                                         start=True, stop=True).then_inc(a_mm.sem, 1)
                    for u in range(U):
                        q = i * U + u
                        pe.wait_ge(a_sb.sem, a_sb.now(q))
                        nc.tensor.matmul(ps_s[0:64, u, 0:64], tw.wt("ak"), small[u][:, 1, 0:64],
                                         start=True, stop=True).then_inc(m_mm.sem, 1)
                    for u in range(U):
                        q = i * U + u
                        pe.wait_ge(m_sb.sem, m_sb.now(q))
                        nc.tensor.matmul(ps_s[0:64, u, 0:65], small[u][:, 2, 0:64], tw.wt("wqT"),
                                         start=True, stop=True).then_inc(r_mm.sem, 1)
                    for u in range(U):
                        q = i * U + u
                        pe.wait_ge(r_sb.sem, r_sb.now(q))
                        nc.tensor.matmul(ps_s[0:65, u, 0:64], small[u][0:64, 3, :], tw.wt("wpT"),
                                         start=True, stop=True).then_inc(w_mm.sem, 1)
                    for u in range(U):
                        q = i * U + u
                        pe.wait_ge(w_sb.sem, w_sb.now(q))
                        pe.wait_ge(gelu.sem, gelu.before(q, U))
                        for t in range(NT):
                            last = nc.tensor.matmul(ps_p[:, u, D * t:D * t + D], xT[u][:, P * t:P * t + P],
                                                    small[u][:, 4, 0:64], start=True, stop=True)
                        last.then_inc(p_mm.sem, 1)

            @block.scalar
            def _(act):
                prime(act, [ln.sqr, xT_sb, kv_sqr, kv_sd, gram_sb, a_sb, gelu])
                act.wait_ge(wkv_mm, 1)
                nc.scalar.copy(wkv[:, :], ps_s[0:65, 0, 0:128]).then_inc(wkv_sb, 1)
                with act.Fori(0, B // U) as i:
                    for u in range(U):
                        ln.square(act, i * U + u, u)
                    for u in range(U):
                        q = i * U + u
                        act.wait_ge(xT_mm.sem, xT_mm.now(q))
                        act.wait_ge(p_mm.sem, p_mm.before(q, U))
                        ln.features(act, xT[u], ps_x, xT_sb)
                        act.wait_ge(kv_mm.sem, kv_mm.now(q))
                        act.wait_ge(kv_ss.sem, kv_ss.before(q, 1))
                        nc.scalar.activation(kv_sq[:, :], ps_kv[:, :], ACT.Square).then_inc(kv_sqr.sem, 1)
                        act.wait_ge(kv_ss.sem, kv_ss.now(q))
                        nc.scalar.activation(dev[u][:, 1, :], dev[u][:, 0, :], ACT.Sqrt,
                                             scale=1.0 / 3.0).then_inc(kv_sd.sem, 1)
                    for u in range(U):
                        q = i * U + u
                        act.wait_ge(gram_mm.sem, gram_mm.now(q))
                        nc.scalar.copy(small[u][:, 0, :], ps_s[0:65, u, 0:65]).then_inc(gram_sb.sem, 1)
                    for u in range(U):
                        q = i * U + u
                        act.wait_ge(a_mm.sem, a_mm.now(q))
                        nc.scalar.copy(small[u][:, 1, 0:64], ps_s[0:65, u, 0:64]).then_inc(a_sb.sem, 1)
                    for u in range(U):
                        q = i * U + u
                        act.wait_ge(p_mm.sem, p_mm.now(q))
                        act.wait_ge(g_add.sem, g_add.before(q, U))
                        nc.scalar.activation(g[u][:, :, :], ps_p[:, u, :].rearrange("p (t f) -> p t f", f=D),
                                             ACT.Gelu).then_inc(gelu.sem, 1)

            @block.vector
            def _(dve):
                prime(dve, ln.dve_steps + [kv_ss, kv_eps, kv_r, z_out, m_sb, r_sb, w_sb])
                for u in range(U):
                    nc.vector.memset(xT[u][64:65, :], 1.0)
                    nc.vector.memset(z[u][:, :, 64:65], 1.0)
                    nc.vector.memset(small[u][64:65, 2, :], 0.0)
                with dve.Fori(0, B // U) as i:
                    for u in range(U):
                        ln.center(dve, i * U + u, u, g_add)
                    for u in range(U):
                        ln.variance(dve, i * U + u, u)
                    for u in range(U):
                        ln.scale(dve, i * U + u, u)
                    for u in range(U):
                        q = i * U + u
                        dve.wait_ge(kv_sqr.sem, kv_sqr.now(q))
                        dve.wait_ge(kv_sd.sem, kv_sd.before(q, U))
                        nc.vector.reduce_sum(dev[u][:, 0, :], kv_sq[:, :].rearrange("p (g j) -> p g j", j=4),
                                             axis=AX_X).then_inc(kv_ss.sem, 1)
                        dve.wait_ge(kv_sd.sem, kv_sd.now(q))
                        nc.vector.tensor_scalar(dev[u][:, 2, :], dev[u][:, 1, :], 1e-5, None,
                                                ALU.add).then_inc(kv_eps.sem, 1)
                        dve.wait_ge(kv_eps.sem, kv_eps.now(q))
                        nc.vector.reciprocal(dev[u][:, 2, :], dev[u][:, 2, :]).then_inc(kv_r.sem, 1)
                        dve.wait_ge(kv_r.sem, kv_r.now(q))
                        dve.wait_ge(gram_mm.sem, gram_mm.before(q, U))
                        nc.vector.tensor_tensor(
                            z[u][:, :, 0:64].rearrange("p t (g j) -> p t g j", j=4),
                            ps_kv[:, :].rearrange("p (t g j) -> p t g j", g=16, j=4),
                            dev[u][:, 2, :].rearrange("p (t g) -> p t g", g=16).unsqueeze(3).to_broadcast(
                                [P, 2 * NT, 16, 4]), ALU.mult).then_inc(z_out.sem, 1)
                    for u in range(U):
                        q = i * U + u
                        dve.wait_ge(m_mm.sem, m_mm.now(q))
                        nc.vector.tensor_tensor(small[u][0:64, 2, 0:64], ps_s[0:64, u, 0:64], tw.ct("kvmask"),
                                                ALU.mult).then_inc(m_sb.sem, 1)
                    for u in range(U):
                        q = i * U + u
                        dve.wait_ge(r_mm.sem, r_mm.now(q))
                        nc.vector.tensor_tensor(small[u][0:64, 3, :], ps_s[0:64, u, 0:65], tw.ct("iaug"),
                                                ALU.add).then_inc(r_sb.sem, 1)
                    for u in range(U):
                        q = i * U + u
                        dve.wait_ge(w_mm.sem, w_mm.now(q))
                        dve.wait_ge(p_mm.sem, p_mm.before(q, U))
                        nc.vector.tensor_tensor(small[u][:, 4, 0:64], ps_s[0:65, u, 0:64], tw.wt("bp"),
                                                ALU.add).then_inc(w_sb.sem, 1)

            @block.gpsimd
            def _(pool):
                prime(pool, [ln.rstd, g_add, h_add])
                with pool.Fori(0, B // U) as i:
                    for u in range(U):
                        ln.inverse_root(pool, i * U + u, u)
                    for u in range(U):
                        q = i * U + u
                        pool.wait_ge(gelu.sem, gelu.now(q))
                        pool.wait_ge(h_add.sem, h_add.before(q, U))
                        nc.gpsimd.tensor_tensor(g2[u][:, :, :], g[u][:, :, :], ln.xn[u][:, :, :],
                                                ALU.add).then_inc(g_add.sem, 1)
                        pool.wait_ge(g_add.sem, g_add.now(q))
                        nc.gpsimd.tensor_tensor(tw.h_at(q), tw.h_at(q), g2[u][:, :, :],
                                                ALU.add).then_inc(h_add.sem, 1)


def routed_ffn(tw):
    nc, U = tw.nc, 2
    PAIRS = E6 // 2
    GR = 32 + E6
    with Stage(tw, "moe") as st:
        ln = Norm(st, U)
        xn2 = [st.sb(f"xn2{u}", [P, NT, 2, D]) for u in range(U)]
        xs = [st.sb(f"xs{u}", [P, S], F32R) for u in range(U)]
        w1 = [st.sb(f"w1{k}", [P, E6 * D], F32R) for k in range(2)]
        wr = [st.sb(f"wr{k}", [P, 33], F32R) for k in range(2)]
        pair = st.sb("pair", [GR, PAIRS * P], F32R)
        rT = st.sb("rT", [33, S])
        route = st.sb("route", [P, 8, NT, E6])
        best = st.sb("best", [P, 8, NT])
        gates = st.sb("gates", [P, NT, GR])
        gT = st.sb("gT", [GR, S], F32R)
        h1 = st.sb("h1", [P, 2, 512])
        h2 = st.sb("h2", [P, E6, 512])
        h2g = st.sb("h2g", [P, E6, 512])
        o = st.sb("o", [P, 512])
        ps_x = st.ps("ps_x", [P, S])
        ps_1 = st.ps("ps_1", [P, 2, 512])
        ps_2 = st.ps("ps_2", [P, 2, 512])
        ps_b = st.ps("ps_b", [P, 512])
        ps_o = st.ps("ps_o", [P, 512])
        split_hi, split_lo, cleared = st.sem("split_hi"), st.sem("split_lo"), st.sem("cleared")
        (x_mm, x_hi, x_lo, r_mm, r_sb, l_mm, l_max, l_sub, l_exp, l_sum, l_rec, prob, max1, eq1, pref1, mp1, sel1,
         rest, max2, eq2, pref2, mp2, sel2, diff, dexp, dsum, wa, wb, g1, g2, gate, gT_mm, gT_hi, gT_lo, h1_mm,
         h1_sb, h2_mm, h2_sb, b_mm, b_mul, o_mm, o_sb, o_tr, h_add) = st.steps(
            "x_mm x_hi x_lo r_mm r_sb l_mm l_max l_sub l_exp l_sum l_rec prob max1 eq1 pref1 mp1 sel1 rest max2 eq2 "
            "pref2 mp2 sel2 diff dexp dsum wa wb g1 g2 gate gT_mm gT_hi gT_lo h1_mm h1_sb h2_mm h2_sb b_mm b_mul "
            "o_mm o_sb o_tr h_add")
        blocks = [(c, p) for c in range(2) for p in range(PAIRS)]
        NB = len(blocks)

        def each_image(engine, body):
            with engine.Fori(0, B // U - 1) as i:
                for u in range(U):
                    body(i * U + u, u, True, True)
            body(B - 2, 0, True, False)
            body(B - 1, 1, False, False)

        with nc.Block() as block:
            @block.tensor
            def _(pe):
                def tokens_t(q, u):
                    pe.wait_ge(gT_lo.sem, gT_lo.before(q, 1))
                    pe.wait_ge(ln.out.sem, ln.out.now(q))
                    for t in range(NT):
                        last = nc.tensor.transpose(ps_x[:, P * t:P * t + P], xn2[u][:, t], tw.ct("ident"))
                    last.then_inc(x_mm.sem, 1)

                def router_hidden(q, u):
                    pe.wait_ge(x_lo.sem, x_lo.now(q))
                    for c in range(2):
                        for k in range(2):
                            last = nc.tensor.matmul(ps_x[0:33, 512 * c:512 * c + 512], wr[k][:, :],
                                                    xs[u][:, 512 * c:512 * c + 512], start=k == 0, stop=k == 1)
                    last.then_inc(r_mm.sem, 1)

                def router_logits(q):
                    pe.wait_ge(r_sb.sem, r_sb.now(q))
                    for t in range(NT):
                        last = nc.tensor.matmul(ps_x[:, E6 * t:E6 * t + E6], rT[:, P * t:P * t + P],
                                                tw.wt("rw2"), start=True, stop=True)
                    last.then_inc(l_mm.sem, 1)

                def first_layer(q, u, j):
                    c, p = blocks[j]
                    pe.wait_ge(h1_sb.sem, h1_sb.before(q * NB + j, 2))
                    for k in range(2):
                        last = nc.tensor.matmul(ps_1[:, j % 2, :], w1[k][:, P * p:P * p + P],
                                                xs[u][:, 512 * c:512 * c + 512], start=k == 0, stop=k == 1)
                    last.then_inc(h1_mm.sem, 1)

                def second_layer(q, j):
                    k, p = q * NB + j, blocks[j][1]
                    pe.wait_ge(h2_sb.sem, h2_sb.before(k, 2))
                    pe.wait_ge(h1_sb.sem, h1_sb.now(k))
                    for e in range(2):
                        last = nc.tensor.matmul(ps_2[64 * e:64 * e + 64, j % 2, :],
                                                tw.wt("ew2", lo=P * p + 64 * e, n=64), h1[:, j % 2, :],
                                                start=True, stop=True, tile_position=(0, 64 * e))
                    last.then_inc(h2_mm.sem, 1)

                def gates_t(q):
                    pe.wait_ge(gate.sem, gate.now(q))
                    for t in range(NT):
                        last = nc.tensor.matmul(ps_x[0:GR, P * t:P * t + P], gates[:, t, :], tw.ct("ident"),
                                                start=True, stop=True)
                    last.then_inc(gT_mm.sem, 1)

                def spread(q, j):
                    c, p = blocks[j]
                    pe.wait_ge(gT_lo.sem, gT_lo.now(q))
                    pe.wait_ge(b_mul.sem, b_mul.before(q * NB + j, 1))
                    nc.tensor.matmul(ps_b[:, :], pair[:, P * p:P * p + P], gT[:, 512 * c:512 * c + 512],
                                     start=True, stop=True).then_inc(b_mm.sem, 1)

                def third_layer(q):
                    pe.wait_ge(h_add.sem, h_add.before(q, 1))
                    for p in range(PAIRS + 1):
                        for c in range(2):
                            if p < PAIRS:
                                pe.wait_ge(b_mul.sem, b_mul.now(q * NB + PAIRS * c + p))
                                w, x = tw.wt("ew3", lo=D * p, n=D), h2g[:, PAIRS * c + p, :]
                            else:
                                w, x = tw.wt("eb3"), gT[:, 512 * c:512 * c + 512].bitcast(F32)
                            last = nc.tensor.matmul(ps_o[64 * c:64 * c + 64, :], w, x, start=p == 0, stop=p == PAIRS,
                                                    tile_position=(0, 64 * c))
                    last.then_inc(o_mm.sem, 1)

                def outputs_t(q):
                    pe.wait_ge(o_sb.sem, o_sb.now(q))
                    for t in range(NT // 2):
                        last = nc.tensor.transpose(ps_o[:, P * t:P * t + P], o[:, P * t:P * t + P], tw.ct("ident"))
                    last.then_inc(o_tr.sem, 1)

                def body(q, u, front, norm):
                    first_layer(q, u, 0)
                    first_layer(q, u, 1)
                    second_layer(q, 0)
                    first_layer(q, u, 2)
                    second_layer(q, 1)
                    gates_t(q)
                    first_layer(q, u, 3)
                    second_layer(q, 2)
                    spread(q, 0)
                    if front:
                        tokens_t(q + 1, 1 - u)
                    first_layer(q, u, 4)
                    second_layer(q, 3)
                    spread(q, 1)
                    first_layer(q, u, 5)
                    second_layer(q, 4)
                    spread(q, 2)
                    if front:
                        router_hidden(q + 1, 1 - u)
                    second_layer(q, 5)
                    spread(q, 3)
                    spread(q, 4)
                    if front:
                        router_logits(q + 1)
                    spread(q, 5)
                    third_layer(q)
                    outputs_t(q)

                prime(pe, [x_mm, r_mm, l_mm, gT_mm, h1_mm, h2_mm, b_mm, o_mm, o_tr])
                pe.wait_ge(split_lo, 2)
                pe.wait_ge(cleared, 1)
                tokens_t(0, 0)
                router_hidden(0, 0)
                router_logits(0)
                each_image(pe, body)

            @block.scalar
            def _(act):
                def tokens_high(q, u):
                    act.wait_ge(x_mm.sem, x_mm.now(q))
                    act.wait_ge(h1_mm.sem, h1_mm.before((q - 1) * NB, 1))
                    nc.scalar.copy(xs[u][:, :], ps_x[:, :]).then_inc(x_hi.sem, 1)

                def router_hidden(q):
                    act.wait_ge(r_mm.sem, r_mm.now(q))
                    act.wait_ge(l_mm.sem, l_mm.before(q, 1))
                    nc.scalar.activation(rT[:, :], ps_x[0:33, :], ACT.Relu, bias=tw.wt("rb1")).then_inc(r_sb.sem, 1)

                def router_exp(q):
                    act.wait_ge(l_sub.sem, l_sub.now(q))
                    nc.scalar.activation(route[:, 1], route[:, 0], ACT.Exp).then_inc(l_exp.sem, 1)

                def best_exp(q):
                    act.wait_ge(diff.sem, diff.now(q))
                    nc.scalar.activation(best[:, 5, :], best[:, 4, :], ACT.Exp).then_inc(dexp.sem, 1)

                def first_relu(q, j):
                    k = q * NB + j
                    act.wait_ge(h1_mm.sem, h1_mm.now(k))
                    act.wait_ge(h2_mm.sem, h2_mm.before(k, 2))
                    nc.scalar.activation(h1[:, j % 2, :], ps_1[:, j % 2, :], ACT.Relu,
                                         bias=tw.wt("eb1", lo=blocks[j][1], n=1)).then_inc(h1_sb.sem, 1)

                def second_relu(q, j):
                    k = q * NB + j
                    act.wait_ge(h2_mm.sem, h2_mm.now(k))
                    act.wait_ge(b_mul.sem, b_mul.before(k, NB))
                    nc.scalar.activation(h2[:, j, :], ps_2[:, j % 2, :], ACT.Relu,
                                         bias=tw.wt("eb2", lo=blocks[j][1], n=1)).then_inc(h2_sb.sem, 1)

                def gates_high(q):
                    act.wait_ge(gT_mm.sem, gT_mm.now(q))
                    act.wait_ge(o_mm.sem, o_mm.before(q, 1))
                    nc.scalar.copy(gT[:, :], ps_x[0:GR, :]).then_inc(gT_hi.sem, 1)

                def outputs(q):
                    act.wait_ge(o_mm.sem, o_mm.now(q))
                    nc.scalar.copy(o[:, :], ps_o[:, :]).then_inc(o_sb.sem, 1)

                def body(q, u, front, norm):
                    first_relu(q, 0)
                    first_relu(q, 1)
                    second_relu(q, 0)
                    first_relu(q, 2)
                    second_relu(q, 1)
                    gates_high(q)
                    first_relu(q, 3)
                    second_relu(q, 2)
                    if front:
                        tokens_high(q + 1, 1 - u)
                    first_relu(q, 4)
                    second_relu(q, 3)
                    first_relu(q, 5)
                    second_relu(q, 4)
                    if front:
                        router_hidden(q + 1)
                    second_relu(q, 5)
                    if front:
                        router_exp(q + 1)
                    outputs(q)
                    if front:
                        best_exp(q + 1)
                    if norm:
                        ln.square(act, q + 2, u)

                prime(act, [ln.sqr, x_hi, r_sb, l_exp, dexp, gT_hi, h1_sb, h2_sb, o_sb])
                for wide, name in ((w1, "ew1"), (wr, "rw1")):
                    nc.scalar.copy(wide[0][:, :], tw.wt(name)).then_inc(split_hi, 1)
                nc.scalar.copy(pair[:, :], tw.ct("pair")).then_inc(cleared, 1)
                ln.square(act, 0, 0)
                ln.square(act, 1, 1)
                tokens_high(0, 0)
                router_hidden(0)
                router_exp(0)
                best_exp(0)
                each_image(act, body)

            @block.vector
            def _(dve):
                rank = tw.ct("rank").rearrange("p (t e) -> p t e", e=E6)

                def then(step, q, op):
                    op.then_inc(step.sem, 1)
                    dve.wait_ge(step.sem, step.now(q))

                def rests(q, hi, lo, tile, ps, r0, rows):
                    dve.wait_ge(hi.sem, hi.now(q))
                    part = tile[r0:r0 + rows, :]
                    nc.vector.tensor_tensor(part, ps[r0:r0 + rows, :], part, ALU.subtract).then_inc(lo.sem, 1)

                def routing(q):
                    r, s = route, best
                    logits = ps_x[:, 0:NT * E6].rearrange("p (t e) -> p t e", e=E6)
                    dve.wait_ge(l_mm.sem, l_mm.now(q))
                    then(l_max, q, nc.vector.reduce_max(s[:, 0, :], logits, axis=AX_X))
                    nc.vector.tensor_tensor(r[:, 0], logits, bc(s[:, 0, :], E6), ALU.subtract).then_inc(l_sub.sem, 1)
                    dve.wait_ge(l_exp.sem, l_exp.now(q))
                    then(l_sum, q, nc.vector.reduce_sum(s[:, 0, :], r[:, 1], axis=AX_X))
                    then(l_rec, q, nc.vector.reciprocal(s[:, 1, :], s[:, 0, :]))
                    then(prob, q, nc.vector.tensor_tensor(r[:, 2], r[:, 1], bc(s[:, 1, :], E6), ALU.mult))
                    then(max1, q, nc.vector.reduce_max(s[:, 2, :], r[:, 2], axis=AX_X))
                    then(eq1, q, nc.vector.tensor_tensor(r[:, 3], r[:, 2], bc(s[:, 2, :], E6), ALU.is_equal))
                    then(pref1, q, nc.vector.tensor_tensor(r[:, 3], r[:, 3], rank, ALU.mult))
                    then(mp1, q, nc.vector.reduce_max(s[:, 0, :], r[:, 3], axis=AX_X))
                    then(sel1, q, nc.vector.tensor_tensor(r[:, 4], r[:, 3], bc(s[:, 0, :], E6), ALU.is_equal))
                    then(rest, q, nc.vector.scalar_tensor_tensor(r[:, 5], r[:, 4], -2.0, r[:, 2], ALU.mult, ALU.add))
                    then(max2, q, nc.vector.reduce_max(s[:, 3, :], r[:, 5], axis=AX_X))
                    nc.vector.tensor_tensor(s[:, 4, :], s[:, 3, :], s[:, 2, :], ALU.subtract).then_inc(diff.sem, 1)
                    then(eq2, q, nc.vector.tensor_tensor(r[:, 6], r[:, 5], bc(s[:, 3, :], E6), ALU.is_equal))
                    then(pref2, q, nc.vector.tensor_tensor(r[:, 6], r[:, 6], rank, ALU.mult))
                    then(mp2, q, nc.vector.reduce_max(s[:, 0, :], r[:, 6], axis=AX_X))
                    then(sel2, q, nc.vector.tensor_tensor(r[:, 7], r[:, 6], bc(s[:, 0, :], E6), ALU.is_equal))
                    dve.wait_ge(dexp.sem, dexp.now(q))
                    then(dsum, q, nc.vector.tensor_scalar(s[:, 6, :], s[:, 5, :], 1.0, None, ALU.add))
                    then(wa, q, nc.vector.reciprocal(s[:, 6, :], s[:, 6, :]))
                    then(wb, q, nc.vector.tensor_tensor(s[:, 7, :], s[:, 5, :], s[:, 6, :], ALU.mult))
                    then(g1, q, nc.vector.tensor_tensor(r[:, 4], r[:, 4], bc(s[:, 6, :], E6), ALU.mult))
                    then(g2, q, nc.vector.tensor_tensor(r[:, 7], r[:, 7], bc(s[:, 7, :], E6), ALU.mult))
                    dve.wait_ge(gT_mm.sem, gT_mm.before(q, 1))
                    for k in range(2):
                        last = nc.vector.tensor_tensor(gates[:, :, 32 * k:32 * k + E6], r[:, 4], r[:, 7], ALU.add)
                    last.then_inc(gate.sem, 1)

                def weigh(q, j):
                    k = q * NB + j
                    dve.wait_ge(h2_sb.sem, h2_sb.now(k))
                    dve.wait_ge(b_mm.sem, b_mm.now(k))
                    dve.wait_ge(o_mm.sem, o_mm.before(q, 1))
                    nc.vector.tensor_tensor(h2g[:, j, :], h2[:, j, :], ps_b[:, :], ALU.mult).then_inc(b_mul.sem, 1)

                def add(q):
                    dve.wait_ge(o_tr.sem, o_tr.now(q))
                    h = tw.h_at(q).rearrange("p (c t) f -> p t c f", c=2)
                    nc.vector.tensor_tensor(h, h, ps_o[:, :].rearrange("p (t c f) -> p t c f", c=2, f=D),
                                            ALU.add).then_inc(h_add.sem, 1)

                def body(q, u, front, norm):
                    rests(q, gT_hi, gT_lo, gT, ps_x, 32, E6)
                    weigh(q, 0)
                    if front:
                        rests(q + 1, x_hi, x_lo, xs[1 - u], ps_x, 64, 64)
                    for j in range(1, NB):
                        weigh(q, j)
                    if norm:
                        ln.center(dve, q + 2, u, ln.out)
                    if front:
                        routing(q + 1)
                    if norm:
                        ln.variance(dve, q + 2, u)
                    add(q)

                prime(dve, ln.dve_steps[:-1] + [
                    x_lo, l_max, l_sub, l_sum, l_rec, prob, max1, eq1, pref1, mp1, sel1, rest, max2, eq2, pref2, mp2,
                    sel2, diff, dsum, wa, wb, g1, g2, gate, gT_lo, b_mul, h_add])
                dve.wait_ge(split_hi, 2)
                for wide, name in ((w1, "ew1"), (wr, "rw1")):
                    nc.vector.tensor_tensor(wide[1][:, :], tw.wt(name), wide[0][:, :], ALU.subtract
                                            ).then_inc(split_lo, 1)
                nc.vector.memset(gates[:, :, :], 0.0)
                for q in range(2):
                    ln.center(dve, q, q, ln.out)
                for q in range(2):
                    ln.variance(dve, q, q)
                rests(0, x_hi, x_lo, xs[0], ps_x, 64, 64)
                routing(0)
                each_image(dve, body)

            @block.gpsimd
            def _(pool):
                def finish(q, u):
                    ln.inverse_root(pool, q, u)
                    ln.scale_twice(pool, q, u, xn2[u], x_mm)

                prime(pool, [ln.rstd, ln.out])
                finish(0, 0)
                finish(1, 1)
                each_image(pool, lambda q, u, front, norm: finish(q + 2, u) if norm else None)


def softmax_attention(tw):
    nc, U = tw.nc, 3
    with Stage(tw, "att") as st:
        ln = Norm(st, 1)
        xn2 = st.sb("xn2", [P, NT, 2, D])
        xs = st.sb("xs", [P, S], F32R)
        split = {name: [st.sb(f"{name}{k}", [P, cols], F32R) for k in range(2)]
                 for name, cols in (("wqq", 128), ("wkk", 128), ("wv1", D))}
        qs = [st.sb(f"qs{u}", [P, S], F32R) for u in range(U)]
        qm = [st.sb(f"qm{u}", [P, S], F32R) for u in range(U)]
        kh = [st.sb(f"kh{u}", [P, S], F32R) for u in range(U)]
        kl = [st.sb(f"kl{u}", [P, S], F32R) for u in range(U)]
        v = [st.sb(f"v{u}", [P, NT, 65]) for u in range(U)]
        neg_max = st.sb("neg_max", [P, NT])
        probs = st.sb("probs", [P, 4, S])
        oT = st.sb("oT", [65, S])
        inv = st.sb("inv", [P, 2, NT])
        o = st.sb("o", [P, NT, D])
        ps_x = st.ps("ps_x", [P, S])
        ps_s = st.ps("ps_s", [P, 2, S])
        ps_o = st.ps("ps_o", [P, S])
        split_hi, split_lo, zeros, ones = (st.sem(n) for n in ("split_hi", "split_lo", "zeros", "ones"))
        (x_mm, x_hi, x_lo, q_mm, q_hi, q_m, q_lo, k_mm, k_hi, k_lo, v_mm, v_sb, m_zero, s1_mm, s1_max, m_mm, m_sb,
         s2_mm, s2_exp, pv_mm, oT_sb, o_tr, rec, rec8, o_sb, h_add) = st.steps(
            "x_mm x_hi x_lo q_mm q_hi q_m q_lo k_mm k_hi k_lo v_mm v_sb m_zero s1_mm s1_max m_mm m_sb "
            "s2_mm s2_exp pv_mm oT_sb o_tr rec rec8 o_sb h_add")

        def each_image(engine, body):
            body(0, 0, 3, True)
            with engine.Fori(0, (B - 4) // U) as i:
                for u in range(U):
                    body(i * U + u + 1, (u + 1) % U, 3, False)
            for q in range(B - 3, B):
                body(q, q % U, B - 1 - q, False)

        with nc.Block() as block:
            @block.tensor
            def _(pe):
                def tokens_t(q, freed):
                    pe.wait_ge(*freed)
                    pe.wait_ge(ln.out.sem, ln.out.now(q))
                    for t in range(NT):
                        last = nc.tensor.transpose(ps_x[:, P * t:P * t + P], xn2[:, t], tw.ct("ident"))
                    last.then_inc(x_mm.sem, 1)

                def project(name, done):
                    for c in range(2):
                        for k in range(2):
                            last = nc.tensor.matmul(ps_x[:, 512 * c:512 * c + 512], split[name][k][:, :],
                                                    xs[:, 512 * c:512 * c + 512], start=k == 0, stop=k == 1)
                    last.then_inc(done.sem, 1)

                def queries(q):
                    pe.wait_ge(x_lo.sem, x_lo.now(q))
                    project("wqq", q_mm)

                def keys(q):
                    pe.wait_ge(q_m.sem, q_m.now(q))
                    pe.wait_ge(q_lo.sem, q_lo.now(q))
                    project("wkk", k_mm)

                def values_of(q):
                    pe.wait_ge(k_lo.sem, k_lo.now(q))
                    for t in range(NT):
                        for k in range(2):
                            last = nc.tensor.matmul(ps_x[:, D * t:D * t + D], xs[:, P * t:P * t + P],
                                                    split["wv1"][k][:, :], start=k == 0, stop=k == 1)
                    last.then_inc(v_mm.sem, 1)

                def scores(q, u, t):
                    if t == 0:
                        pe.wait_ge(m_zero.sem, m_zero.now(q))
                        pe.wait_ge(k_lo.sem, k_lo.now(q))
                    pe.wait_ge(s1_max.sem, s1_max.before(q * NT + t, 1))
                    for c in range(2):
                        cols = slice(512 * c, 512 * c + 512)
                        nc.tensor.matmul(ps_s[:, 0, cols], qs[u][:, P * t:P * t + P], kh[u][:, cols],
                                         start=True, stop=False)
                        last = nc.tensor.matmul(ps_s[:, 0, cols], qm[u][:, P * t:P * t + P], kl[u][:, cols],
                                                start=False, stop=True)
                    last.then_inc(s1_mm.sem, 1)

                def scores_t(q, u, t):
                    if t == 0:
                        pe.wait_ge(m_sb.sem, m_sb.now(q))
                    pe.wait_ge(s2_exp.sem, s2_exp.before(q * NT + t, 1))
                    for c in range(2):
                        cols = slice(512 * c, 512 * c + 512)
                        nc.tensor.matmul(ps_s[:, 1, cols], kh[u][:, P * t:P * t + P], qs[u][:, cols],
                                         start=True, stop=False)
                        last = nc.tensor.matmul(ps_s[:, 1, cols], kl[u][:, P * t:P * t + P], qm[u][:, cols],
                                                start=False, stop=True)
                    last.then_inc(s2_mm.sem, 1)

                def weighed(q, u, t):
                    pe.wait_ge(s2_exp.sem, s2_exp.now(q * NT + t))
                    if t == 0:
                        pe.wait_ge(oT_sb.sem, oT_sb.before(q, 1))
                    for c in range(2):
                        cols = slice(512 * c, 512 * c + 512)
                        last = nc.tensor.matmul(ps_o[0:65, cols], v[u][:, t, :], probs[:, t % 4, cols],
                                                start=t == 0, stop=t == NT - 1)
                    last.then_inc(pv_mm.sem, 1)

                def maxima(q, freed):
                    pe.wait_ge(*freed)
                    pe.wait_ge(s1_max.sem, s1_max.now(q * NT + NT - 1))
                    for t in range(NT):
                        last = nc.tensor.matmul(ps_x[0:1, P * t:P * t + P], neg_max[:, t:t + 1], tw.ct("ident"),
                                                start=True, stop=True)
                    last.then_inc(m_mm.sem, 1)

                def outputs(q):
                    pe.wait_ge(oT_sb.sem, oT_sb.now(q))
                    for t in range(NT):
                        last = nc.tensor.transpose(ps_x[:, P * t:P * t + 65], oT[:, P * t:P * t + P],
                                                   tw.c[0:65, CONSTS["ident"][1]:CONSTS["ident"][1] + 65])
                    last.then_inc(o_tr.sem, 1)

                def body(q, u, ahead, first):
                    for t in range(NT):
                        if ahead >= 1:
                            scores(q + 1, (u + 1) % U, t)
                        scores_t(q, u, t)
                        if t >= 1:
                            weighed(q, u, t - 1)
                        if t == 1 and not first:
                            outputs(q - 1)
                        if ahead >= 2:
                            if t == 2:
                                tokens_t(q + 2, (o_sb.sem, o_sb.before(q, 1)))
                            elif t == 3:
                                queries(q + 2)
                            elif t == 4:
                                keys(q + 2)
                            elif t == 5:
                                values_of(q + 2)
                    weighed(q, u, NT - 1)
                    if ahead >= 2:
                        maxima(q + 1, (v_sb.sem, v_sb.now(q + 2)))
                    elif ahead == 1:
                        maxima(q + 1, (o_sb.sem, o_sb.before(q, 1)))

                prime(pe, [x_mm, q_mm, k_mm, v_mm, s1_mm, m_mm, s2_mm, pv_mm, o_tr])
                pe.wait_ge(split_lo, 3)
                pe.wait_ge(ones, 1)
                for q in range(2):
                    tokens_t(q, (v_sb.sem, v_sb.before(q, 1)))
                    queries(q)
                    keys(q)
                    values_of(q)
                for t in range(NT):
                    scores(0, 0, t)
                maxima(0, (v_sb.sem, v_sb.now(1)))
                each_image(pe, body)
                pe.wait_ge(o_sb.sem, o_sb.now(B - 2))
                outputs(B - 1)

            @block.scalar
            def _(act):
                def tokens_high(q):
                    act.wait_ge(x_mm.sem, x_mm.now(q))
                    act.wait_ge(v_mm.sem, v_mm.before(q, 1))
                    nc.scalar.copy(xs[:, :], ps_x[:, :]).then_inc(x_hi.sem, 1)

                def queries(q, u):
                    act.wait_ge(q_mm.sem, q_mm.now(q))
                    act.wait_ge(s2_mm.sem, s2_mm.before((q - U + 1) * NT, 1))
                    nc.scalar.copy(qs[u][:, :], ps_x[:, :]).then_inc(q_hi.sem, 1)
                    nc.scalar.copy(qm[u][0:D, :], ps_x[0:D, :]).then_inc(q_m.sem, 1)

                def keys(q, u):
                    act.wait_ge(k_mm.sem, k_mm.now(q))
                    nc.scalar.copy(kh[u][:, :], ps_x[:, :]).then_inc(k_hi.sem, 1)

                def values_of(q, u):
                    act.wait_ge(v_mm.sem, v_mm.now(q))
                    act.wait_ge(pv_mm.sem, pv_mm.before((q - U + 1) * NT, 1))
                    nc.scalar.copy(v[u][:, :, 0:D], ps_x[:, 0:512].rearrange("p (t f) -> p t f", f=D)
                                   ).then_inc(v_sb.sem, 1)

                def maxima(q, u):
                    act.wait_ge(m_mm.sem, m_mm.now(q))
                    nc.scalar.copy(qm[u][D:D + 1, :], ps_x[0:1, :]).then_inc(m_sb.sem, 1)

                def body(q, u, ahead, first):
                    w = (u + 2) % U
                    for t in range(NT):
                        k = q * NT + t
                        act.wait_ge(s2_mm.sem, s2_mm.now(k))
                        act.wait_ge(pv_mm.sem, pv_mm.before(k, 4))
                        nc.scalar.activation(probs[:, t % 4, :], ps_s[:, 1, :], ACT.Exp).then_inc(s2_exp.sem, 1)
                        if ahead >= 2:
                            if t == 2:
                                tokens_high(q + 2)
                            elif t == 3:
                                queries(q + 2, w)
                            elif t == 4:
                                keys(q + 2, w)
                            elif t == 5:
                                values_of(q + 2, w)
                        if ahead >= 3 and t == 6:
                            ln.square(act, q + 3, 0)
                    if ahead >= 1:
                        maxima(q + 1, (u + 1) % U)

                prime(act, [ln.sqr, x_hi, q_hi, q_m, k_hi, v_sb, m_sb, s2_exp])
                for hi, lo in split.items():
                    nc.scalar.copy(lo[0][:, :], tw.wt(hi)).then_inc(split_hi, 1)
                for q in range(2):
                    ln.square(act, q, 0)
                    tokens_high(q)
                    queries(q, q)
                    keys(q, q)
                    values_of(q, q)
                ln.square(act, 2, 0)
                maxima(0, 0)
                each_image(act, body)

            @block.vector
            def _(dve):
                def rest(q, hi, lo, tile, high, r0):
                    dve.wait_ge(hi.sem, hi.now(q))
                    nc.vector.tensor_tensor(tile[r0:r0 + D, :], ps_x[r0:r0 + D, :], high[r0:r0 + D, :],
                                            ALU.subtract).then_inc(lo.sem, 1)

                def rest_of_queries(q, u):
                    rest(q, q_hi, q_lo, qs[u], qs[u], D)
                    nc.vector.memset(qm[u][D:D + 1, :].bitcast(F32), 0.0).then_inc(m_zero.sem, 1)

                def maximum(q, t):
                    if t == 0:
                        dve.wait_ge(m_mm.sem, m_mm.before(q, 1))
                    dve.wait_ge(s1_mm.sem, s1_mm.now(q * NT + t))
                    nc.vector.tensor_reduce(neg_max[:, t:t + 1], ps_s[:, 0, :], axis=AX_X, op=ALU.max, negate=True
                                            ).then_inc(s1_max.sem, 1)

                def gather(q):
                    dve.wait_ge(pv_mm.sem, pv_mm.now(q * NT + NT - 1))
                    dve.wait_ge(o_tr.sem, o_tr.before(q, 1))
                    nc.vector.tensor_copy(oT[:, :], ps_o[0:65, :]).then_inc(oT_sb.sem, 1)

                def outputs(q):
                    pt = ps_x[:, :].rearrange("p (t f) -> p t f", f=P)
                    dve.wait_ge(o_tr.sem, o_tr.now(q))
                    nc.vector.reciprocal(inv[:, 0, :], pt[:, :, 64]).then_inc(rec.sem, 1)
                    dve.wait_ge(rec.sem, rec.now(q))
                    nc.vector.tensor_scalar(inv[:, 1, :], inv[:, 0, :], float(D) ** -0.5, None, ALU.mult
                                            ).then_inc(rec8.sem, 1)
                    dve.wait_ge(rec8.sem, rec8.now(q))
                    dve.wait_ge(h_add.sem, h_add.before(q, 1))
                    nc.vector.tensor_tensor(o[:, :, :], pt[:, :, 0:64], bc(inv[:, 1, :], D), ALU.mult
                                            ).then_inc(o_sb.sem, 1)

                def body(q, u, ahead, first):
                    w = (u + 2) % U
                    for t in range(NT):
                        if ahead >= 1:
                            maximum(q + 1, t)
                        if t == 1 and not first:
                            outputs(q - 1)
                        if ahead >= 2:
                            if t == 2:
                                rest(q + 2, x_hi, x_lo, xs, xs, D)
                            elif t == 3:
                                rest_of_queries(q + 2, w)
                            elif t == 4:
                                rest(q + 2, k_hi, k_lo, kl[w], kh[w], 0)
                        if ahead >= 3:
                            if t == 5:
                                ln.center(dve, q + 3, 0, ln.out)
                            elif t == 7:
                                ln.variance(dve, q + 3, 0)
                    gather(q)

                prime(dve, ln.dve_steps[:-1] + [x_lo, q_lo, k_lo, m_zero, s1_max, oT_sb, rec, rec8, o_sb])
                for u in range(U):
                    nc.vector.memset(qm[u][D:P, :].bitcast(F32), 0.0)
                    last = nc.vector.memset(kl[u][D:P, :].bitcast(F32), 0.0)
                last.then_inc(zeros, 1)
                dve.wait_ge(zeros, 1)
                for u in range(U):
                    nc.vector.memset(v[u][:, :, D:D + 1], 1.0)
                    last = nc.vector.memset(kl[u][D:D + 1, :].bitcast(F32), 1.0)
                last.then_inc(ones, 1)
                dve.wait_ge(split_hi, 3)
                for name, parts in split.items():
                    nc.vector.tensor_tensor(parts[1][:, :], tw.wt(name), parts[0][:, :], ALU.subtract
                                            ).then_inc(split_lo, 1)
                for q in range(2):
                    ln.center(dve, q, 0, ln.out)
                    ln.variance(dve, q, 0)
                    rest(q, x_hi, x_lo, xs, xs, D)
                    rest_of_queries(q, q)
                    rest(q, k_hi, k_lo, kl[q], kh[q], 0)
                ln.center(dve, 2, 0, ln.out)
                ln.variance(dve, 2, 0)
                for t in range(NT):
                    maximum(0, t)
                each_image(dve, body)
                outputs(B - 1)

            @block.gpsimd
            def _(pool):
                def normalise(q):
                    ln.inverse_root(pool, q, 0)
                    ln.scale_twice(pool, q, 0, xn2, x_mm)

                def add(q):
                    pool.wait_ge(o_sb.sem, o_sb.now(q))
                    nc.gpsimd.tensor_tensor(tw.h_at(q), tw.h_at(q), o[:, :, :], ALU.add).then_inc(h_add.sem, 1)

                def body(q, u, ahead, first):
                    if not first:
                        add(q - 1)
                    if ahead >= 3:
                        normalise(q + 3)

                prime(pool, [ln.rstd, ln.out, h_add])
                for q in range(2):
                    normalise(q)
                normalise(2)
                each_image(pool, body)
                add(B - 1)


KEY_STEPS = [(c, kb) for c in range(2) for kb in range(4 * c + 4)]
QUERY_STEPS = [(qb, c) for qb in range(NT) for c in range(qb // 4 + 1)]
NSTEP = len(KEY_STEPS)
NTILE = 2 * NSTEP
assert len(QUERY_STEPS) == NSTEP and NTILE % 3 == 0 and NSTEP % 3 == 0

SLOT_ITEMS = {1: ("m", 1), 3: ("r", 1), 5: ("k", 0), 7: ("k", 1), 9: ("q", 0), 11: ("q", 1), 12: ("m", 0),
              13: ("r", 0), 14: ("q", 2), 16: ("q", 3), 19: ("mask", 0), 23: ("mask", 1)}
EXTRA_ITEMS = {(0, 0): ("v", 0), (0, 4): ("v", 1), (1, 17): ("fxT", 0), (1, 21): ("x", 0), (2, 15): ("f1", 0),
               (2, 17): ("f1", 1), (2, 21): ("f2", 0), (3, 17): ("foT", 0), (3, 21): ("fg", 0)}
TAIL_KINDS = ("fxT", "f1", "f2", "foT", "fg")


def items_of(n, first, last):
    out = {}
    for p in range(NTILE):
        item = EXTRA_ITEMS.get((n, p)) or SLOT_ITEMS.get(p)
        if item is None:
            continue
        kind, j = item
        if first and (kind in TAIL_KINDS or (n == 0 and item == ("r", 1))):
            continue
        if last and (kind == "x" or (n >= 2 and kind in "k q mask".split()) or (n == 3 and item == ("m", 0))):
            continue
        out[p] = item
    return out


def expert_attention(tw, out):
    nc = tw.nc
    with Stage(tw, "exp") as st:
        wc = st.sb("wc", [65, NH, 322])
        resid = st.sb("resid", [P, NH, NT, DH])
        ln = Norm(st, 1)
        xT = st.sb("xT", [65, S])
        x_mm, x_sb = st.steps("x_mm x_sb")
        head_inputs(st, ln, xT, wc, resid, x_mm, x_sb)
        causal_heads(st, ln, xT, wc, resid, x_mm, x_sb, out)


def head_inputs(st, ln, xT, wc, resid, x_mm, x_sb):
    nc, tw = st.nc, st.tw
    with Stage(tw, "hin") as sc:
        ps_w = sc.ps("ps_w", [P, 512])
        ps_x = sc.ps("ps_x", [P, 512])
        ps_r = sc.ps("ps_r", [P, 512])
        w_mm, w_sb, r_mm, r_sb = sc.sem("w_mm"), sc.sem("w_sb"), sc.sem("r_mm"), sc.sem("r_sb")
        ones = sc.sem("ones")
        with nc.Block() as block:
            @block.tensor
            def _(pe):
                prime(pe, [x_mm])
                for n in range(NH):
                    if n:
                        pe.wait_ge(w_sb, n)
                    nc.tensor.matmul(ps_w[0:65, 0:322], tw.fw("hlT", lo=65 * n, n=65),
                                     tw.fw("proj", lo=322 * n, n=322), start=True, stop=True).then_inc(w_mm, 1)
                pe.wait_ge(ones, 1)
                for n in range(NH):
                    ln.transpose(pe, n, 0, ps_x, x_mm)
                    pe.wait_ge(x_sb.sem, x_sb.now(n))
                    if n:
                        pe.wait_ge(r_sb, n)
                    for t in range(NT):
                        last = nc.tensor.matmul(ps_r[:, DH * t:DH * t + DH], xT[:, P * t:P * t + P],
                                                tw.fw("hlres", lo=DH * n, n=DH), start=True, stop=True)
                    last.then_inc(r_mm, 1)

            @block.scalar
            def _(act):
                prime(act, [ln.sqr, x_sb])
                for n in range(NH):
                    act.wait_ge(w_mm, n + 1)
                    nc.scalar.copy(wc[:, n, :], ps_w[0:65, 0:322]).then_inc(w_sb, 1)
                for n in range(NH):
                    ln.square(act, n, 0)
                    act.wait_ge(x_mm.sem, x_mm.now(n))
                    if n:
                        act.wait_ge(r_mm, n)
                    ln.features(act, xT, ps_x, x_sb)

            @block.vector
            def _(dve):
                prime(dve, ln.dve_steps)
                nc.vector.memset(xT[64:65, :], 1.0).then_inc(ones, 1)
                for n in range(NH):
                    ln.center(dve, n, 0, x_mm)
                    ln.variance(dve, n, 0)
                    ln.scale(dve, n, 0)
                    dve.wait_ge(r_mm, n + 1)
                    nc.vector.tensor_copy(resid[:, n], ps_r[:, 0:NT * DH].rearrange("p (t f) -> p t f", f=DH)
                                          ).then_inc(r_sb, 1)

            @block.gpsimd
            def _(pool):
                prime(pool, [ln.rstd])
                for n in range(NH):
                    ln.inverse_root(pool, n, 0)


def causal_heads(st, ln, xT, wc, resid, x_mm, x_sb, out):
    nc, tw = st.nc, st.tw
    LN_BASE = NH
    q_in = [[st.sb(f"q{n}{j}", [98, S], F32R) for j in range(2)] for n in range(NH)]
    k_in = [[st.sb(f"k{n}{e}", [98, S], F32R) for e in range(2)] for n in range(NH)]
    live = [st.sb(f"live{n}", [P, S], BF16) for n in range(NH)]
    v = st.sb("v", [P, NT, NH, 32])
    neg_max = st.sb("neg_max", [P, 2, NE, NT])
    m_cols = st.sb("m_cols", [P, 4, 2, 64], F32R)
    ident_r = st.sb("ident_r", [P, P], F32R)
    probs = st.sb("probs", [P, 3, NE, 512])
    oT = st.sb("oT", [P, 2, 512])
    r = st.sb("r", [P, NH, NT, 84])
    ident_b = st.sb("ident_b", [P, P], BF16)
    mask_q = st.sb("mask_q", [P, P], BF16)
    mask_k = st.sb("mask_k", [P, P], BF16)
    tri = st.sb("tri", [P, P])
    inv = st.sb("inv", [P, NT, NE])
    gl = st.sb("gl", [P, NT, NE, NE])
    lg = st.sb("lg", [P, 3, NT, NE])
    gz = st.sb("gz", [P, 3, NT])
    cf = st.sb("cf", [P, 2, NT, NE])
    weighed = st.sb("weighed", [P, NT, NE, DH])
    mix = st.sb("mix", [P, NT, NH, DH])
    t_stat = st.sb("t_stat", [P, 2, 4, NT * NH])
    t_half = st.sb("t_half", [P, NT * NH])
    t_c = st.sb("t_c", [P, NT, D])
    t_sq = st.sb("t_sq", [P, NT, D])
    fx = st.sb("fx", [P, NT, D])
    y = st.sb("y", [P, NT, D])
    fT = st.sb("fT", [64, S])
    hx = st.sb("hx", [65, S])
    fg = st.sb("fg", [P, 3, NT, NH])
    fz = st.sb("fz", [P, 2, NT])
    o = st.sb("o", [P, NT, D])
    ring = [st.ps(f"ring{i}", [P, 2, 512]) for i in range(3)]
    ps_o = st.ps("ps_o", [P, 512])
    ps_m = st.ps("ps_m", [P, 512])

    names = ("s1_mm s2_mm pv_mm k_mm q_mm mask_mm m_mm r_mm v_mm fxT_mm f1_mm f2_mm foT_mm fg_mm "
             "s1_max k_lo q_lo mask_sb m_cols o_sb y_sb fg_sub "
             "s2_exp k_hi q_hi m_sb r_sb v_sb fxT_sb f1_sb foT_sb "
             "k_in0 k_in1 k_one stored consts_v consts_p n_tri "
             "g_inv g_mul g_sum g_bias g_max g_sub g_exp g_z g_rz g_cf g_cfz g_w g_mix g_res "
             "n_sum n_mean n_cent n_sq n_var n_eps n_root n_out n_g n_b f1_live y_add "
             "z_max z_sum z_rec z_exp z_w z_o z_add")
    s = {name: st.sem(name) for name in names.split()}

    def wait(engine, name, value):
        if isinstance(value, int) and value <= 0:
            return
        engine.wait_ge(s[name], value)

    def heads(tile):
        return tile[:, :, :].rearrange("p t (n f) -> p (t n) f", f=DH)

    def read(engine, n, b, item):
        kind, j = item
        g = NH * b + n
        if kind == "m":
            wait(engine, "m_sb", 2 * (g + 1) + (0 if j else 1))
        elif kind == "r":
            wait(engine, "r_sb", 2 * (g if j else g + 1) - (0 if j else 1))
        elif kind == "k":
            wait(engine, "k_lo", 2 * (g + 2) + j + 1)
        elif kind == "q":
            wait(engine, "q_lo", 4 * (g + 2) + j + 1)
        elif kind == "mask":
            wait(engine, "mask_sb", 2 * (g + 2) + j + 1)
        elif kind == "v":
            wait(engine, "v_sb", 2 * b + j + 1)
        elif kind == "x":
            engine.wait_ge(x_sb.sem, x_sb.now(b + 1 + LN_BASE))
        elif kind == "fxT":
            wait(engine, "fxT_sb", b)
        elif kind == "f1":
            wait(engine, "f1_sb", 2 * (b - 1) + j + 1)
        elif kind == "f2":
            wait(engine, "y_sb", b)
        elif kind == "foT":
            wait(engine, "foT_sb", b)
        elif kind == "fg":
            wait(engine, "fg_sub", b)

    with nc.Block() as block:
        @block.sync
        def _(sp):
            wait(sp, "consts_v", 1)
            for n in range(NH):
                sp.dma_start(k_in[n][1][97:98, :].bitcast(F32), hx[64:65, :]).then_inc(s["k_one"], 16)
            wait(sp, "k_one", 16 * NH)

            def second_keys(g, n):
                wait(sp, "k_lo", 2 * (g + 1))
                sp.dma_start(k_in[n][1][16:96, :].bitcast(F32), k_in[n][0][0:80, :].bitcast(F32)).then_inc(s[f"k_in{n % 2}"], 16)

            def results(b):
                wait(sp, "z_add", b + 1)
                sp.dma_start(out[bass.ds(b, 1)].rearrange("a (t p) f -> p (a t) f", p=P), o[:, :, :]
                             ).then_inc(s["stored"], 16)

            second_keys(0, 0)
            second_keys(1, 1)

            def body(b, first, last):
                for n in range(NH):
                    g = NH * b + n
                    items = items_of(n, first, last)
                    for p in sorted(items):
                        if items[p] == ("k", 1):
                            second_keys(g + 2, (n + 2) % NH)
                if not first:
                    results(b - 1)

            body(0, True, False)
            with sp.Fori(1, B - 1) as b:
                body(b, False, False)
            body(B - 1, False, True)
            results(B - 1)
            wait(sp, "stored", 16 * B)

        @block.tensor
        def _(pe):
            def query_tile(g, n, p):
                (qb, c), j = QUERY_STEPS[p // 2], p % 2
                w = min(512, P * (qb + 1) - 512 * c)
                slot = ring[(2 * p + 1) % 3]
                diagonal = P * qb < 512 * c + w
                for e in range(2):
                    last = nc.tensor.matmul(slot[:, e, 0:w], q_in[n][j][0:96, P * qb:P * qb + P],
                                            k_in[n][e][0:96, 512 * c:512 * c + w], start=True, stop=not diagonal)
                    if diagonal:
                        last = nc.tensor.matmul(slot[:, e, w - P:w], ident_b[:, :], mask_q[:, :],
                                                start=False, stop=True)
                last.then_inc(s["s1_mm"], 1)

            def key_tile(g, n, p):
                (c, kb), j = KEY_STEPS[p // 2], p % 2
                q0 = max(512 * c, P * kb)
                w = 512 * (c + 1) - q0
                slot = ring[(2 * p) % 3]
                diagonal = q0 == P * kb
                for e in range(2):
                    last = nc.tensor.matmul(slot[:, e, 0:w], k_in[n][e][:, P * kb:P * kb + P],
                                            q_in[n][j][:, q0:q0 + w], start=True, stop=not diagonal)
                    if diagonal:
                        last = nc.tensor.matmul(slot[:, e, 0:P], ident_b[:, :], mask_k[:, :],
                                                start=False, stop=True)
                last.then_inc(s["s2_mm"], 1)

            def values(g, n, step):
                c, kb = KEY_STEPS[step]
                q0 = max(512 * c, P * kb)
                w = 512 * (c + 1) - q0
                wait(pe, "s2_exp", NTILE * g + 2 * step + 2)
                if kb == 0:
                    wait(pe, "o_sb", 2 * g + c)
                for e in range(NE):
                    last = nc.tensor.matmul(ps_o[32 * e:32 * e + 32, q0 - 512 * c:512], v[:, kb, n, :],
                                            probs[:, step % 3, e, 0:w], start=kb == 0, stop=kb == 4 * c + 3,
                                            tile_position=(0, 32 * e))
                last.then_inc(s["pv_mm"], 1)

            def project(kind, g, n, j):
                c = j % 2
                cols = xT[:, 512 * c:512 * c + 512]
                if kind == "k":
                    nc.tensor.matmul(ps_m[0:98, :], wc[:, n, 192:290], cols, start=True, stop=True
                                     ).then_inc(s["k_mm"], 1)
                elif kind == "q":
                    nc.tensor.matmul(ps_m[0:96, :], wc[:, n, 96 * (j // 2):96 * (j // 2) + 96], cols,
                                     start=True, stop=True).then_inc(s["q_mm"], 1)
                else:
                    nc.tensor.matmul(ps_m[:, :], tw.fw("hlmask", lo=128 * n, n=128), cols,
                                     start=True, stop=True).then_inc(s["mask_mm"], 1)

            def maxima(g, half):
                wait(pe, "m_cols", 2 * g + half + 1)
                for t in range(4):
                    last = nc.tensor.matmul(ps_m[0:66, P * t:P * t + P],
                                            m_cols[:, t].rearrange("p j c -> p (j c)")[:, 0:66], ident_r[:, :],
                                            start=True, stop=True)
                last.then_inc(s["m_mm"], 1)

            def token_rows(g, n, c):
                wait(pe, "o_sb", 2 * g + c + 1)
                for t in range(4):
                    last = nc.tensor.matmul(ps_m[:, 84 * t:84 * t + 84], oT[:, c, P * t:P * t + P],
                                            tw.fw("gate", lo=84 * n, n=84), start=True, stop=True)
                last.then_inc(s["r_mm"], 1)

            def turn(src, done):
                for t in range(NT // 2):
                    last = nc.tensor.transpose(ps_m[:, P * t:P * t + P], src[:, 2 * t:2 * t + 2, :], tw.ct("ident"))
                last.then_inc(s[done], 1)

            def tail(kind, b, j):
                if kind == "fxT":
                    wait(pe, "n_b", 2 * b + 1)
                    turn(fx, "fxT_mm")
                elif kind == "f1":
                    wait(pe, "fxT_sb", b + 1)
                    nc.tensor.matmul(ps_m[:, :], tw.fw("fc1"), fT[:, 512 * j:512 * j + 512],
                                     start=True, stop=True).then_inc(s["f1_mm"], 1)
                elif kind == "f2":
                    wait(pe, "f1_live", b + 1)
                    for t in range(NT):
                        last = nc.tensor.matmul(ps_m[:, D * t:D * t + D], hx[:, P * t:P * t + P], tw.fw("fc2"),
                                                start=True, stop=True)
                    last.then_inc(s["f2_mm"], 1)
                elif kind == "foT":
                    wait(pe, "n_b", 2 * b + 2)
                    turn(y, "foT_mm")
                else:
                    wait(pe, "foT_sb", b + 1)
                    for t in range(NT):
                        last = nc.tensor.matmul(ps_m[:, NH * t:NH * t + NH], fT[:, P * t:P * t + P],
                                                tw.fw("fgate"), start=True, stop=True)
                    last.then_inc(s["fg_mm"], 1)

            def image_features(b):
                ln.transpose(pe, b + LN_BASE, 0, ps_m, x_mm)

            def small(b, n, item):
                kind, j = item
                g = NH * b + n
                if kind in ("k", "q", "mask"):
                    if kind == "k" and n in (2,):
                        pe.wait_ge(x_sb.sem, x_sb.now(b + 1 + LN_BASE))
                    project(kind, g + 2, (n + 2) % NH, j)
                elif kind == "m":
                    maxima(g if j else g + 1, j)
                elif kind == "r":
                    token_rows(g - 1 if j else g, (n - 1) % NH if j else n, j)
                elif kind == "v":
                    for t in range(4):
                        last = nc.tensor.matmul(ps_m[:, P * t:P * t + P], xT[:, P * (4 * j + t):P * (4 * j + t) + P],
                                                wc[:, :, 290:322], start=True, stop=True)
                    last.then_inc(s["v_mm"], 1)
                elif kind == "x":
                    image_features(b + 1)
                else:
                    tail(kind, b - 1, j)

            wait(pe, "consts_v", 1)
            wait(pe, "consts_p", 1)
            wait(pe, "k_one", 16 * NH)
            image_features(0)
            prev = None
            for g in range(2):
                for item in [("k", 0), ("k", 1), ("q", 0), ("q", 1), ("q", 2), ("q", 3), ("mask", 0), ("mask", 1)]:
                    if prev is None:
                        pe.wait_ge(x_sb.sem, x_sb.now(LN_BASE))
                    else:
                        read(pe, *prev)
                    project(item[0], g, g, item[1])
                    prev = (g - 2, 0, item)
            wait(pe, "k_in0", 16)
            for p in range(NTILE):
                wait(pe, "s1_max", p - 2)
                query_tile(0, 0, p)
            read(pe, *prev)
            maxima(0, 0)
            prev = (-1, 0, ("m", 0))

            def body(b, first, last, prev):
                for n in range(NH):
                    g = NH * b + n
                    items = items_of(n, first, last)
                    more = not (last and n == NH - 1)
                    for p in range(NTILE):
                        if p == 0:
                            wait(pe, "m_sb", 2 * g + 1)
                        elif p == 8:
                            wait(pe, "m_sb", 2 * g + 2)
                        if more:
                            wait(pe, "s1_max", NTILE * (g + 1) + p - 1)
                        else:
                            if p < 2:
                                wait(pe, "s1_max", NTILE * (g + 1) + p - 1 if p == 0 else NTILE * (g + 1))
                            wait(pe, "s2_exp", NTILE * g + max(p - 2, 0))
                        key_tile(g, n, p)
                        if more:
                            if p == 0:
                                wait(pe, f"k_in{(n + 1) % 2}", 16 * (2 * b + (n + 1) // 2 + 1))
                                wait(pe, "q_lo", 4 * (g + 2))
                            wait(pe, "s2_exp", NTILE * g + p)
                            query_tile(g + 1, (n + 1) % NH, p)
                        if p % 2 == 0:
                            if p > 0:
                                if n == 0 and p == 2:
                                    wait(pe, "v_sb", 2 * b + 1)
                                if n == 0 and p == 18:
                                    wait(pe, "v_sb", 2 * b + 2)
                                values(g, n, p // 2 - 1)
                            elif not (first and n == 0):
                                values(g - 1, (n - 1) % NH, NSTEP - 1)
                        if p in items:
                            read(pe, *prev)
                            small(b, n, items[p])
                            prev = (n, b, items[p])
                return prev

            body(0, True, False, prev)
            with pe.Fori(1, B - 1) as b:
                body(b, False, False, (NH - 1, b - 1, ("mask", 1)))
            prev = body(B - 1, False, True, (NH - 1, B - 2, ("mask", 1)))
            g = NH * B - 1
            values(g, NH - 1, NSTEP - 1)
            for item in [("r", 1), ("fxT", 0), ("f1", 0), ("f1", 1), ("f2", 0), ("foT", 0), ("fg", 0)]:
                read(pe, *prev)
                small(B, 0, item)
                prev = (0, B, item)

        @block.scalar
        def _(act):
            def probabilities(g, p):
                (c, kb), j, step = KEY_STEPS[p // 2], p % 2, p // 2
                w = 512 * (c + 1) - max(512 * c, P * kb)
                wait(act, "s2_mm", NTILE * g + p + 1)
                if j == 0:
                    wait(act, "pv_mm", NSTEP * g + step - 2)
                nc.scalar.activation(probs[:, step % 3, 2 * j:2 * j + 2, 0:w], ring[(2 * p) % 3][:, :, 0:w], ACT.Exp,
                                     scale=float(DH) ** 0.5).then_inc(s["s2_exp"], 1)

            def high(kind, g, n, j):
                cols = slice(512 * (j % 2), 512 * (j % 2) + 512)
                if kind == "k":
                    wait(act, "k_mm", 2 * g + j + 1)
                    nc.scalar.copy(k_in[n][0][:, cols], ps_m[0:98, :]).then_inc(s["k_hi"], 1)
                else:
                    wait(act, "q_mm", 4 * g + j + 1)
                    nc.scalar.copy(q_in[n][j // 2][0:96, cols], ps_m[0:96, :]).then_inc(s["q_hi"], 1)

            def maxima(g, n, half):
                wait(act, "m_mm", 2 * g + half + 1)
                for j in range(2):
                    last = nc.scalar.copy(q_in[n][j][96:98, 512 * half:512 * half + 512], ps_m[64 * j:64 * j + 2, :])
                last.then_inc(s["m_sb"], 1)

            def token_rows(g, n, c):
                wait(act, "r_mm", 2 * g + c + 1)
                wait(act, "g_w", g - 3)
                nc.scalar.copy(r[:, n, 4 * c:4 * c + 4, :], ps_m[:, 0:336].rearrange("p (t f) -> p t f", f=84)
                               ).then_inc(s["r_sb"], 1)

            def gate_exp(g):
                wait(act, "g_sub", g + 1)
                nc.scalar.activation(lg[:, 2], lg[:, 1], ACT.Exp).then_inc(s["g_exp"], 1)

            def turned(name, b):
                wait(act, name + "_mm", b + 1)
                for par in range(2):
                    last = nc.scalar.copy(fT[:, :].rearrange("p (t e n) -> p e t n", e=2, n=P)[:, par],
                                          ps_m[D * par:D * par + D, :].rearrange("p (t n) -> p t n", n=P))
                last.then_inc(s[name + "_sb"], 1)

            def hidden(b, j):
                wait(act, "f1_mm", 2 * b + j + 1)
                nc.scalar.activation(hx[0:64, 512 * j:512 * j + 512], ps_m[0:64, :], ACT.Relu,
                                     bias=tw.fw("fc1_b")).then_inc(s["f1_sb"], 1)

            def head_gate_exp(b):
                wait(act, "fg_sub", b + 1)
                nc.scalar.activation(fg[:, 1], fg[:, 0], ACT.Exp).then_inc(s["z_exp"], 1)

            def image_features(b):
                act.wait_ge(x_mm.sem, x_mm.now(b + LN_BASE))
                ln.features(act, xT, ps_m, x_sb)

            def small(b, n, item):
                kind, j = item
                g = NH * b + n
                if kind in ("k", "q"):
                    high(kind, g + 2, (n + 2) % NH, j)
                elif kind == "m":
                    maxima(g if j else g + 1, n if j else (n + 1) % NH, j)
                elif kind == "r":
                    token_rows(g - 1 if j else g, (n - 1) % NH if j else n, j)
                elif kind == "v":
                    wait(act, "v_mm", 2 * b + j + 1)
                    nc.scalar.copy(v[:, 4 * j:4 * j + 4, :, :], ps_m[:, :].rearrange("p (t n f) -> p t n f", n=NH, f=32)
                                   ).then_inc(s["v_sb"], 1)
                elif kind == "x":
                    image_features(b + 1)
                elif kind in ("fxT", "foT"):
                    turned(kind, b - 1)
                elif kind == "f1":
                    hidden(b - 1, j)

            ln.square(act, LN_BASE, 0)
            image_features(0)
            for g in range(2):
                for item in [("k", 0), ("k", 1), ("q", 0), ("q", 1), ("q", 2), ("q", 3)]:
                    high(item[0], g, g, item[1])
            maxima(0, 0, 0)

            def body(b, first, last):
                for n in range(NH):
                    g = NH * b + n
                    items = items_of(n, first, last)
                    for p in range(NTILE):
                        probabilities(g, p)
                        if p in items:
                            small(b, n, items[p])
                        if p == 13 and not (first and n == 0):
                            gate_exp(g - 1)
                        if n == 0 and p == 5 and not last:
                            ln.square(act, b + 1 + LN_BASE, 0)
                        if n == 3 and p == 22 and not first:
                            head_gate_exp(b - 1)

            body(0, True, False)
            with act.Fori(1, B - 1) as b:
                body(b, False, False)
            body(B - 1, False, True)
            token_rows(NH * B - 1, NH - 1, 1)
            gate_exp(NH * B - 1)
            turned("fxT", B - 1)
            hidden(B - 1, 0)
            hidden(B - 1, 1)
            turned("foT", B - 1)
            head_gate_exp(B - 1)

        @block.vector
        def _(dve):
            def then(name, count, op):
                op.then_inc(s[name], 1)
                wait(dve, name, count)

            def maximum(g, p):
                (qb, c), j = QUERY_STEPS[p // 2], p % 2
                w = min(512, P * (qb + 1) - 512 * c)
                wait(dve, "s1_mm", NTILE * g + p + 1)
                nc.vector.tensor_reduce(neg_max[:, c, 2 * j:2 * j + 2, qb], ring[(2 * p + 1) % 3][:, :, 0:w],
                                        axis=AX_X, op=ALU.max, negate=True).then_inc(s["s1_max"], 1)

            def columns_of(x):
                return x.rearrange("p (j e) t -> p t j e", e=2)

            def early_maxima(g):
                wait(dve, "s1_max", NTILE * g + 8)
                wait(dve, "m_mm", 2 * g)
                nc.vector.tensor_copy(m_cols[:, :, :, 0:2], columns_of(neg_max[:, 0, :, 0:4])).then_inc(s["m_cols"], 1)

            def late_maxima(g):
                wait(dve, "s1_max", NTILE * (g + 1))
                wait(dve, "m_mm", 2 * g + 1)
                nc.vector.tensor_tensor(m_cols[:, :, :, 0:2], columns_of(neg_max[:, 0, :, 4:8]),
                                        columns_of(neg_max[:, 1, :, 4:8]), ALU.min).then_inc(s["m_cols"], 1)

            def outputs(g, n, c):
                wait(dve, "pv_mm", NSTEP * g + (4 if c == 0 else NSTEP))
                wait(dve, "r_mm", 2 * (g - 1) + c + 1)
                nc.vector.tensor_tensor(oT[:, c, :], ps_o[:, :], live[n][:, 512 * c:512 * c + 512],
                                        ALU.mult).then_inc(s["o_sb"], 1)

            def rest(kind, g, n, j):
                cols = slice(512 * (j % 2), 512 * (j % 2) + 512)
                if kind == "k":
                    wait(dve, "k_hi", 2 * g + j + 1)
                    part = k_in[n][0][64:96, cols]
                    nc.vector.tensor_tensor(part, ps_m[64:96, :], part, ALU.subtract).then_inc(s["k_lo"], 1)
                elif kind == "q":
                    wait(dve, "q_hi", 4 * g + j + 1)
                    part = q_in[n][j // 2][32:64, cols]
                    nc.vector.tensor_tensor(part, ps_m[32:64, :], part, ALU.subtract).then_inc(s["q_lo"], 1)
                else:
                    wait(dve, "mask_mm", 2 * g + j + 1)
                    nc.vector.tensor_scalar(live[n][:, cols], ps_m[:, :], 0.0, None, ALU.not_equal
                                            ).then_inc(s["mask_sb"], 1)

            def gate_inverse(g, n):
                wait(dve, "r_sb", 2 * g + 2)
                nc.vector.reciprocal(inv[:, :, :], r[:, n, :, 64:68]).then_inc(s["g_inv"], 1)

            def gate_logits(g, n):
                wait(dve, "g_mul", g + 1)
                then("g_sum", g + 1, nc.vector.reduce_sum(lg[:, 0], gl[:, :, :, :], axis=AX_X))
                then("g_bias", g + 1, nc.vector.tensor_tensor(
                    lg[:, 0], lg[:, 0], tw.fw("gate_b", lo=NE * n, n=NE).unsqueeze(1).to_broadcast([P, NT, NE]), ALU.add))
                then("g_max", g + 1, nc.vector.reduce_max(gz[:, 0, :], lg[:, 0], axis=AX_X))
                nc.vector.tensor_tensor(lg[:, 1], lg[:, 0], bc(gz[:, 0, :], NE), ALU.subtract).then_inc(s["g_sub"], 1)

            def gate_norm(g):
                wait(dve, "g_exp", g + 1)
                then("g_z", g + 1, nc.vector.reduce_sum(gz[:, 1, :], lg[:, 2], axis=AX_X))
                nc.vector.reciprocal(gz[:, 2, :], gz[:, 1, :]).then_inc(s["g_rz"], 1)

            def gate_mix(g, n, b):
                wait(dve, "g_w", g + 1)
                if n == 0:
                    wait(dve, "n_cent", 2 * b - 1)
                nc.vector.reduce_sum(mix[:, :, n, :], weighed[:, :, :, :].rearrange("p t e f -> p t f e"),
                                     axis=AX_X).then_inc(s["g_mix"], 1)

            def norm_mean(src, k):
                then("n_sum", k + 1, nc.vector.reduce_sum(t_stat[:, 0, 0, :], src, axis=AX_X))
                nc.vector.tensor_scalar(t_stat[:, 0, 1, :], t_stat[:, 0, 0, :], 1.0 / DH, None, ALU.mult
                                        ).then_inc(s["n_mean"], 1)

            def norm_var(k):
                wait(dve, "n_sq", k + 1)
                then("n_var", k + 1, nc.vector.reduce_sum(t_stat[:, 1, 0, :], heads(t_sq), axis=AX_X))
                nc.vector.tensor_scalar(t_stat[:, 1, 1, :], t_stat[:, 1, 0, :], 1.0 / DH, 1e-8, ALU.mult,
                                        ALU.add).then_inc(s["n_eps"], 1)

            def live_hidden(b):
                wait(dve, "f1_sb", 2 * b + 2)
                nc.vector.scalar_tensor_tensor(hx[0:64, :], fT[:, :], 0.0, hx[0:64, :], ALU.not_equal,
                                               ALU.mult).then_inc(s["f1_live"], 1)

            def live_out(b):
                wait(dve, "f2_mm", b + 1)
                wait(dve, "z_o", b)
                nc.vector.scalar_tensor_tensor(y[:, :, :].rearrange("p t f -> p (t f)"),
                                               fx[:, :, :].rearrange("p t f -> p (t f)"), 0.0, ps_m[:, :],
                                               ALU.not_equal, ALU.mult).then_inc(s["y_sb"], 1)

            def head_gate(b):
                wait(dve, "fg_mm", b + 1)
                logits = ps_m[:, 0:NT * NH].rearrange("p (t n) -> p t n", n=NH)
                then("z_max", b + 1, nc.vector.reduce_max(fz[:, 0, :], logits, axis=AX_X))
                nc.vector.tensor_tensor(fg[:, 0], logits, bc(fz[:, 0, :], NH), ALU.subtract).then_inc(s["fg_sub"], 1)

            def head_gate_norm(b):
                wait(dve, "z_exp", b + 1)
                then("z_sum", b + 1, nc.vector.reduce_sum(fz[:, 0, :], fg[:, 1], axis=AX_X))
                nc.vector.reciprocal(fz[:, 1, :], fz[:, 0, :]).then_inc(s["z_rec"], 1)

            def small(b, n, item):
                kind, j = item
                if kind in ("k", "q", "mask"):
                    rest(kind, NH * b + n + 2, (n + 2) % NH, j)
                elif kind == "f2":
                    live_out(b - 1)
                elif kind == "fg":
                    head_gate(b - 1)

            mixed = mix[:, :, :, :].rearrange("p t n f -> p (t n) f")
            for n in range(NH):
                nc.vector.memset(k_in[n][1][:, :].bitcast(F32), 0.0)
            nc.vector.memset(t_half[:, :], -0.5)
            nc.vector.memset(hx[64:65, :], 1.0)
            nc.vector.memset(m_cols[:, :, :, :].bitcast(F32), 0.0)
            nc.vector.tensor_copy(ident_r[:, :], tw.ct("ident"))
            nc.vector.tensor_copy(ident_b[:, :], tw.ct("ident")).then_inc(s["consts_v"], 1)
            ln.center(dve, LN_BASE, 0, x_mm, b=0)
            ln.variance(dve, LN_BASE, 0)
            ln.scale(dve, LN_BASE, 0)
            for g in range(2):
                for item in [("k", 0), ("k", 1), ("q", 0), ("q", 1), ("q", 2), ("q", 3), ("mask", 0), ("mask", 1)]:
                    rest(item[0], g, g, item[1])
            for p in range(NTILE):
                maximum(0, p)
            early_maxima(0)
            late_maxima(0)

            def body(b, first, last):
                for n in range(NH):
                    g = NH * b + n
                    head_before = not (first and n == 0)
                    items = items_of(n, first, last)
                    more = not (last and n == NH - 1)
                    for p in range(NTILE):
                        if more:
                            maximum(g + 1, p)
                            if p == 8:
                                early_maxima(g + 1)
                        if p in items:
                            small(b, n, items[p])
                        if p == 0 and head_before:
                            outputs(g - 1, (n - 1) % NH, 1)
                        if p == 9:
                            outputs(g, n, 0)
                        if head_before:
                            if p == 6:
                                gate_inverse(g - 1, (n - 1) % NH)
                            elif p == 12:
                                gate_logits(g - 1, (n - 1) % NH)
                            elif p == 15:
                                gate_norm(g - 1)
                            elif p == 19:
                                gate_mix(g - 1, (n - 1) % NH, b)
                        if n == 0 and not last:
                            if p == 2:
                                ln.center(dve, b + 1 + LN_BASE, 0, x_mm, b=b + 1)
                            elif p == 8:
                                ln.variance(dve, b + 1 + LN_BASE, 0)
                            elif p == 14:
                                ln.scale(dve, b + 1 + LN_BASE, 0)
                        if not first:
                            if (n, p) == (0, 22):
                                wait(dve, "g_res", NH * b)
                                norm_mean(mixed, 2 * (b - 1))
                            elif (n, p) == (1, 3):
                                norm_var(2 * (b - 1))
                            elif (n, p) == (2, 19):
                                live_hidden(b - 1)
                            elif (n, p) == (3, 1):
                                wait(dve, "y_add", b)
                                norm_mean(heads(y), 2 * (b - 1) + 1)
                            elif (n, p) == (3, 5):
                                norm_var(2 * (b - 1) + 1)
                            elif (n, p) == (3, 23):
                                head_gate_norm(b - 1)
                    if more:
                        late_maxima(g + 1)

            body(0, True, False)
            with dve.Fori(1, B - 1) as b:
                body(b, False, False)
            body(B - 1, False, True)
            g, b = NH * B - 1, B - 1
            outputs(g, NH - 1, 1)
            gate_inverse(g, NH - 1)
            gate_logits(g, NH - 1)
            gate_norm(g)
            gate_mix(g, NH - 1, b)
            wait(dve, "g_res", NH * B)
            norm_mean(mixed, 2 * b)
            norm_var(2 * b)
            live_hidden(b)
            live_out(b)
            wait(dve, "y_add", B)
            norm_mean(heads(y), 2 * b + 1)
            norm_var(2 * b + 1)
            head_gate(b)
            head_gate_norm(b)

        @block.gpsimd
        def _(pool):
            def then(name, count, op):
                op.then_inc(s[name], 1)
                wait(pool, name, count)

            def gate_products(g, n):
                wait(pool, "g_inv", g + 1)
                nc.gpsimd.tensor_tensor(
                    gl[:, :, :, :], r[:, n, :, 68:84].rearrange("p t (e f) -> p t e f", f=NE),
                    inv[:, :, :].unsqueeze(2).to_broadcast([P, NT, NE, NE]), ALU.mult).then_inc(s["g_mul"], 1)

            def gate_weights(g, n):
                wait(pool, "g_exp", g + 1)
                then("g_cf", g + 1, nc.gpsimd.tensor_tensor(cf[:, 0], lg[:, 2], inv[:, :, :], ALU.mult))
                wait(pool, "g_rz", g + 1)
                then("g_cfz", g + 1, nc.gpsimd.tensor_tensor(cf[:, 1], cf[:, 0], bc(gz[:, 2, :], NE), ALU.mult))
                nc.gpsimd.tensor_tensor(
                    weighed[:, :, :, :], r[:, n, :, 0:64].rearrange("p t (e f) -> p t e f", f=DH),
                    cf[:, 1].unsqueeze(3).to_broadcast([P, NT, NE, DH]), ALU.mult).then_inc(s["g_w"], 1)
                wait(pool, "g_mix", g + 1)
                nc.gpsimd.tensor_tensor(mix[:, :, n, :], mix[:, :, n, :], resid[:, n], ALU.add).then_inc(s["g_res"], 1)

            def norm(src, dst, gain, bias, k, ready):
                ready()
                wait(pool, "n_mean", k + 1)
                then("n_cent", k + 1, nc.gpsimd.tensor_tensor(heads(t_c), src, bc(t_stat[:, 0, 1, :], DH), ALU.subtract))
                nc.gpsimd.tensor_tensor(t_sq[:, :, :], t_c[:, :, :], t_c[:, :, :], ALU.mult).then_inc(s["n_sq"], 1)
                wait(pool, "n_eps", k + 1)
                then("n_root", k + 1, nc.gpsimd.tensor_tensor(t_stat[:, 1, 2, :], t_stat[:, 1, 1, :], t_half[:, :], ALU.pow))
                then("n_out", k + 1, nc.gpsimd.tensor_tensor(heads(dst), heads(t_c), bc(t_stat[:, 1, 2, :], DH), ALU.mult))
                for name, w, op in (("n_g", gain, ALU.mult), ("n_b", bias, ALU.add)):
                    then(name, k + 1, nc.gpsimd.tensor_tensor(
                        dst[:, :, :], dst[:, :, :], tw.fw(w).unsqueeze(1).to_broadcast([P, NT, D]), op))

            def norm_mixed(b):
                norm(mix[:, :, :, :].rearrange("p t n f -> p (t n) f"), fx, "ln_g", "ln_b", 2 * b,
                     lambda: wait(pool, "y_sb", b))

            def norm_out(b):
                wait(pool, "y_sb", b + 1)
                then("y_add", b + 1, nc.gpsimd.tensor_tensor(y[:, :, :], y[:, :, :], fx[:, :, :], ALU.add))
                norm(heads(y), y, "fn_g", "fn_b", 2 * b + 1, lambda: None)

            def finish(b):
                wait(pool, "z_rec", b + 1)
                then("z_w", b + 1, nc.gpsimd.tensor_tensor(fg[:, 2], fg[:, 1], bc(fz[:, 1, :], NH), ALU.mult))
                wait(pool, "stored", 16 * b)
                then("z_o", b + 1, nc.gpsimd.tensor_tensor(
                    heads(o), heads(y), bc(fg[:, 2].rearrange("p t n -> p (t n)"), DH), ALU.mult))
                nc.gpsimd.tensor_tensor(o[:, :, :], o[:, :, :], tw.h_at(b), ALU.add).then_inc(s["z_add"], 1)

            nc.gpsimd.memset(tri[:, :], 0.0).then_inc(s["n_tri"], 1)
            wait(pool, "n_tri", 1)
            nc.gpsimd.affine_select(out=mask_q[:, :], in_=tri[:, :], pattern=[[-1, P]], compare_op=ALU.is_ge,
                                    fill=NEG, base=0, channel_multiplier=1)
            nc.gpsimd.affine_select(out=mask_k[:, :], in_=tri[:, :], pattern=[[1, P]], compare_op=ALU.is_ge,
                                    fill=NEG, base=0, channel_multiplier=-1).then_inc(s["consts_p"], 1)
            ln.inverse_root(pool, LN_BASE, 0)

            def body(b, first, last):
                for n in range(NH):
                    g = NH * b + n
                    if n == 1 and not first:
                        norm_mixed(b - 1)
                    if n == 3 and not first:
                        norm_out(b - 1)
                    if not (first and n == 0):
                        gate_products(g - 1, (n - 1) % NH)
                    if n == 0 and not last:
                        ln.inverse_root(pool, b + 1 + LN_BASE, 0)
                    if not (first and n == 0):
                        gate_weights(g - 1, (n - 1) % NH)
                    if n == 3 and not first:
                        finish(b - 1)

            body(0, True, False)
            with pool.Fori(1, B - 1) as b:
                body(b, False, False)
            body(B - 1, False, True)
            gate_products(NH * B - 1, NH - 1)
            gate_weights(NH * B - 1, NH - 1)
            norm_mixed(B - 1)
            norm_out(B - 1)
            finish(B - 1)


def program(nc, x, tok_w, weights, f_weights, consts, out):
    with ExitStack() as ctx:
        tw = Tower(nc, ctx)
        with nc.sbuf_tensor("w", [P, W_COLS], F32) as tw.w:
            load_inputs(tw, weights, f_weights, consts)
            tokens(tw, x, tok_w)
            linear_attention(tw)
            routed_ffn(tw)
            softmax_attention(tw)
        expert_attention(tw, out)


def pack(x):
    packed = [np.zeros((P, W_COLS), np.float32), np.zeros((P, F_COLS), np.float32)]

    def put(name, a, lo=0, row=0):
        a = np.asarray(a, np.float32)
        out, table = (packed[0], WEIGHTS) if name in WEIGHTS else (packed[1], F_WEIGHTS)
        at = table[name][1] + lo
        out[row:row + a.shape[0], at:at + a.shape[1]] = a

    qkv = np.asarray(x["L0_attn_W_qkv"]).reshape(16, 12, D)
    qkv_b = np.asarray(x["L0_attn_b_qkv"]).reshape(16, 12)
    part = [qkv[:, 4 * j:4 * j + 4].reshape(64, D) for j in range(3)]
    part_b = [qkv_b[:, 4 * j:4 * j + 4].reshape(64, 1) for j in range(3)]
    put("kvT", np.concatenate([part[1], part[2]]))
    put("kvT", np.concatenate([part_b[1], part_b[2]]), lo=64)
    for name, w, b in (("ak", "L0_attn_kln_w", "L0_attn_kln_b"), ("av", "L0_attn_vln_w", "L0_attn_vln_b")):
        for j, v in enumerate(np.asarray(x[w]).reshape(64)):
            put(name, v.reshape(1, 1), lo=j, row=j)
        put(name, np.asarray(x[b]).reshape(1, 64), row=64)
    put("wqT", part[0])
    put("wqT", part_b[0], lo=64)
    put("wpT", np.asarray(x["L0_attn_W_proj"]).T)
    put("bp", np.asarray(x["L0_attn_b_proj"]).reshape(1, 64), row=64)
    for k in range(2):
        put("rw1", x["L0_ffn_router_w1"], row=64 * k)
        put("eb3", x["L0_ffn_expert_b3"], row=32 * k)
    put("rb1", np.asarray(x["L0_ffn_router_b1"]).reshape(32, 1))
    put("rb1", np.ones((1, 1)), row=32)
    put("rw2", x["L0_ffn_router_w2"])
    put("rw2", np.asarray(x["L0_ffn_router_b2"]).reshape(1, E6), row=32)
    for e in range(E6):
        for k in range(2):
            put("ew1", x["L0_ffn_expert_w1"][e], lo=64 * e, row=64 * k)
        put("eb1", np.asarray(x["L0_ffn_expert_b1"][e]).reshape(64, 1), lo=e // 2, row=64 * (e % 2))
        put("ew2", x["L0_ffn_expert_w2"][e], lo=64 * e, row=64 * (e % 2))
        put("eb2", np.asarray(x["L0_ffn_expert_b2"][e]).reshape(64, 1), lo=e // 2, row=64 * (e % 2))
        put("ew3", x["L0_ffn_expert_w3"][e], lo=64 * (e // 2), row=64 * (e % 2))
    for j in range(2):
        for k in range(2):
            put("wqq", np.asarray(x["L1_attn_Wq"]).T, lo=64 * j, row=64 * k)
            put("wkk", np.asarray(x["L1_attn_Wk"]).T, lo=64 * j, row=64 * k)
        put("wv1", np.asarray(x["L1_attn_Wv"]).T, row=64 * j)
    one = np.ones((1, 1))
    for n in range(NH):
        hl_w, hl_b = np.asarray(x["L1_ffn_hl_w"][n]), np.asarray(x["L1_ffn_hl_b"][n])
        put("hlT", hl_w, lo=65 * n)
        put("hlT", hl_b.reshape(DH, 1), lo=65 * n + 64)
        put("hlT", one, lo=65 * n + 64, row=DH)
        put("hlres", hl_w.T, lo=DH * n)
        put("hlres", hl_b.reshape(1, DH), lo=DH * n, row=64)
        at = 322 * n
        for e in range(NE):
            put("hlmask", hl_w.T, lo=128 * n + 32 * e)
            put("hlmask", hl_b.reshape(1, DH), lo=128 * n + 32 * e, row=64)
            put("hlmask", one, lo=128 * n + 32 * e + DH, row=64)
            for g in range(3):
                put("proj", np.asarray(x["L1_ffn_wq"][n, e]).T, lo=at + 96 * (e // 2) + 32 * g + DH * (e % 2))
        for g in range(3):
            put("proj", np.asarray(x["L1_ffn_wk"][n]).T, lo=at + 192 + 32 * g)
        put("proj", one, lo=at + 192 + 96, row=DH)
        put("proj", np.asarray(x["L1_ffn_wv"][n]).T, lo=at + 290)
        put("proj", one, lo=at + 290 + DH, row=DH)
        for e in range(NE):
            put("gate", np.eye(DH), lo=84 * n + DH * e, row=32 * e)
            put("gate", one, lo=84 * n + 64 + e, row=32 * e + DH)
            for f in range(NE):
                put("gate", np.asarray(x["L1_ffn_gate_w"][n, e, DH * f:DH * f + DH]).reshape(DH, 1),
                    lo=84 * n + 68 + NE * e + f, row=32 * f)
        put("fgate", np.asarray(x["L1_ffn_fgate_w"]).T)
        put("fc1", np.asarray(x["L1_ffn_fc1_w"]).T, lo=DH * n, row=DH * n)
        put("fc1_b", np.asarray(x["L1_ffn_fc1_b"]).reshape(DH, 1), row=DH * n)
        put("fc2", np.asarray(x["L1_ffn_fc2_w"]).T, lo=DH * n, row=DH * n)
        put("fc2", np.asarray(x["L1_ffn_fc2_b"]).reshape(1, DH), lo=DH * n, row=64)
        for name, w in (("ln_g", "ln_g"), ("ln_b", "ln_b"), ("fn_g", "fnorm_g"), ("fn_b", "fnorm_b")):
            put(name, np.broadcast_to(np.asarray(x["L1_ffn_" + w]), (P, DH)), lo=DH * n)
    put("gate_b", np.broadcast_to(np.asarray(x["L1_ffn_gate_b"]).reshape(NH * NE), (P, NH * NE)))
    return packed


def kernel(**inputs):
    import concourse.bacc as bacc
    from concourse.bass_utils import run_bass_kernel_spmd

    nc = bacc.Bacc("TRN2", target_bir_lowering=False, num_devices=1)
    weights, f_weights = pack(inputs)
    arrays = {
        "x": np.ascontiguousarray(inputs["x"]),
        "tok_w": np.ascontiguousarray(
            np.asarray(inputs["L0_tok_W"]).reshape(D, 2 * NF, C).transpose(1, 0, 2).reshape(2 * NF, D * C)),
        "weights": weights,
        "f_weights": f_weights,
        "consts": constants(),
    }
    args = {n: nc.dram_tensor(n, a.shape, mybir.dt.from_np(a.dtype), kind="ExternalInput").ap()
            for n, a in arrays.items()}
    out = nc.dram_tensor("out", (B, S, D), F32, kind="ExternalOutput").ap()
    program(nc, out=out, **args)
    return run_bass_kernel_spmd(nc, [arrays], core_ids=[0]).results[0]["out"]
```

```python
from contextlib import ExitStack

import concourse.bass as bass
import numpy as np
from concourse import mybir

F32 = mybir.dt.float32
F32R = mybir.dt.float32r
BF16 = mybir.dt.bfloat16
ALU = mybir.AluOpType
ACT = mybir.ActivationFunctionType
AX_X = mybir.AxisListType.X

P = 128
B, C, T, V = 16, 64, 128, 64
D = 64
PATCH, STRIDE = 16, 8
NP = T // STRIDE
S = V * NP
NT = S // P
NF = PATCH // 2 + 1
E6 = 6
NH, NE, DH = 4, 4, 16
NEG = -1.0e30
PRIME = 32


def columns(table):
    at, where = 0, {}
    for name, rows, cols in table:
        where[name] = (rows, at, cols)
        at += cols
    return where, at


WEIGHTS, W_COLS = columns(
    [("kvT", 128, 65), ("ak", 65, 64), ("av", 65, 64), ("wqT", 65, 65), ("wpT", 64, 64), ("bp", 65, 64),
     ("rw1", 128, 33), ("rb1", 33, 1), ("rw2", 33, E6), ("ew1", 128, E6 * D), ("eb1", 128, 3), ("ew2", 128, 3 * 128), ("eb2", 128, 3),
     ("ew3", 128, 3 * D), ("eb3", 32 + E6, D), ("wqq", 128, 128), ("wkk", 128, 128), ("wv1", 128, 64),
     ])
H_WEIGHTS, H_COLS = columns(
    [("hl_w", DH, NH * 128), ("hl_b", DH + 1, NH * 128), ("hlmask", 128, NH * 128), ("hlmask_b", 128, NH),
     ("hlres", 65, NH * DH), ("proj", DH + 1, NH * 322)])
F_WEIGHTS, F_COLS = columns(
    [("gate", 128, NH * 84), ("gate_b", 128, NH * NE),
     ("ln_g", 128, D), ("ln_b", 128, D), ("fc1", 64, 128), ("fc1_b", 64, 1), ("fc2", 65, 64),
     ("fn_g", 128, D), ("fn_b", 128, D), ("fgate", 64, NH)])
CONSTS, C_COLS = columns(
    [("ident", 128, 128), ("center4", 128, 128), ("kvmask", 64, 64), ("iaug", 64, 65), ("dft", 2 * NF, PATCH),
     ("rank", 128, NT * E6), ("pair", 32 + E6, 3 * 128)])


def constants():
    out = np.zeros((P, C_COLS), np.float32)

    def put(name, a):
        rows, at, cols = CONSTS[name]
        out[:rows, at:at + cols] = a

    put("ident", np.eye(128))
    put("center4", np.eye(128) - np.kron(np.eye(32), np.full((4, 4), 0.25)))
    put("kvmask", np.kron(np.eye(16), np.ones((4, 4))) / S)
    put("iaug", np.eye(64, 65))
    t, f = np.arange(PATCH), np.arange(NF)
    angle = 2.0 * np.pi * np.outer(f, t) / PATCH
    dft = np.concatenate([np.cos(angle), -np.sin(angle)]) / np.sqrt(PATCH)
    put("dft", dft.reshape(2 * NF, 2, 2, 4).transpose(0, 2, 3, 1).reshape(2 * NF, PATCH))
    put("rank", np.tile(np.arange(E6, 0, -1), NT))
    pair = np.kron(np.eye(E6), np.ones((1, 64)))
    put("pair", np.concatenate([pair, np.zeros((32 - E6, E6 * 64)), pair]))
    return out


class Step:

    def __init__(self, sem):
        self.sem = sem

    @staticmethod
    def now(q):
        return q + (PRIME + 1)

    @staticmethod
    def before(q, depth):
        return q + (PRIME + 1 - depth)


def prime(engine, steps):
    for s in steps:
        engine.sem_inc(s.sem, PRIME)


class Tower:

    def __init__(self, nc, ctx):
        self.nc, self.ctx = nc, ctx
        self.h = self.sb("h", [P, B, NT * D])
        self.f = self.sb("f", [P, F_COLS])
        self.c = self.sb("c", [P, C_COLS])
        self.neg_half = self.sb("neg_half", [P, NT])

    def sb(self, name, shape, dt=F32):
        return self.ctx.enter_context(self.nc.sbuf_tensor(name, shape, dt))

    def wt(self, name, rows=None, lo=0, n=None):
        r, at, cols = WEIGHTS[name]
        return self.w[0:rows or r, at + lo:at + lo + (n or cols)]

    def fw(self, name, rows=None, lo=0, n=None):
        r, at, cols = F_WEIGHTS[name]
        return self.f[0:rows or r, at + lo:at + lo + (n or cols)]

    def hw(self, name, rows=None, lo=0, n=None):
        r, at, cols = H_WEIGHTS[name]
        return self.hd[0:rows or r, at + lo:at + lo + (n or cols)]

    def ct(self, name, rows=None, lo=0, n=None):
        r, at, cols = CONSTS[name]
        return self.c[0:rows or r, at + lo:at + lo + (n or cols)]

    def h_at(self, b):
        return self.h[:, bass.ds(b, 1), :].rearrange("p a (t f) -> p (a t) f", f=D)


class Stage:

    def __init__(self, tw, name):
        self.tw, self.nc, self.name, self.ctx, self.sems = tw, tw.nc, name, ExitStack(), []

    def __enter__(self):
        return self

    def __exit__(self, *a):
        self.ctx.close()
        self.nc.clear_and_free_semaphores(self.sems)
        self.nc.all_engine_barrier()

    def sb(self, name, shape, dt=F32):
        return self.ctx.enter_context(self.nc.sbuf_tensor(f"{self.name}_{name}", shape, dt))

    def ps(self, name, shape, dt=F32):
        return self.ctx.enter_context(self.nc.psum_tensor(f"{self.name}_{name}", shape, dt))

    def sem(self, name):
        self.sems.append(self.nc.alloc_semaphore(f"{self.name}_{name}"))
        return self.sems[-1]

    def steps(self, names):
        return [Step(self.sem(n)) for n in names.split()]


def bc(ap, n):
    return ap.unsqueeze(2).to_broadcast([ap.shape[0], ap.shape[1], n])


def load_inputs(tw, weights, f_weights, consts):
    nc = tw.nc
    with Stage(tw, "load") as st:
        arrived = st.sem("arrived")
        with nc.Block() as block:
            @block.sync
            def _(sp):
                sp.dma_start(tw.w[:, :], weights).then_inc(arrived, 16)
                sp.dma_start(tw.c[:, :], consts).then_inc(arrived, 16)
                sp.dma_start(tw.f[:, :], f_weights).then_inc(arrived, 16)
                sp.wait_ge(arrived, 48)

            @block.vector
            def _(dve):
                nc.vector.memset(tw.neg_half[:, :], -0.5)


def tokens(tw, x, tok_w):
    nc, U, K = tw.nc, 4, 2
    with Stage(tw, "tok") as st:
        rf = st.sb("rf", [2 * NF, D * C])
        wt = st.sb("wt", [P, 8, D])
        xs = [st.sb(f"x{u}", [P, NP + 1, 4, V]) for u in range(U)]
        embT = [st.sb(f"embT{u}", [P, 512]) for u in range(K)]
        ps_e = st.ps("ps_e", [P, K, 512])
        ps_h = st.ps("ps_h", [P, K, 2, 512])
        rf_in, fold_mm, fold_sb = st.sem("rf_in"), st.sem("fold_mm"), st.sem("fold_sb")
        x_in = [st.sem(f"x_in{u}") for u in range(U)]
        emb_mm, emb_sb, tr_mm, h_out = st.steps("emb_mm emb_sb tr_mm h_out")
        xr = x.rearrange("b c (m h s) v -> b h c m (s v)", h=2, s=4)
        with nc.Block() as block:
            @block.sync
            def _(sp):
                sp.dma_start(rf[:, :], tok_w).then_inc(rf_in, 16)
                with sp.Fori(0, B // U) as i:
                    for u in range(U):
                        b = i * U + u
                        sp.wait_ge(emb_mm.sem, emb_mm.before(b, U))
                        for hh in range(2):
                            rows = slice(64 * hh, 64 * hh + 64)
                            sp.dma_start(xs[u][rows, 0:NP, :, :].rearrange("c m s v -> c m (s v)"),
                                         xr[bass.ds(b, 1), hh].rearrange("a c m f -> (a c) m f")
                                         ).then_inc(x_in[u], 16)
                            edge = x[bass.ds(b, 1), :, T - 1, :].rearrange("a c v -> (a c) v")
                            sp.dma_start(xs[u][rows, NP, :, :],
                                         edge.unsqueeze(1).to_broadcast([C, 4, V])).then_inc(x_in[u], 16)

            @block.tensor
            def _(pe):
                prime(pe, [emb_mm, tr_mm])
                pe.wait_ge(rf_in, 16)
                for hh in range(2):
                    for o in range(D):
                        last = nc.tensor.matmul(
                            ps_h[64 * hh:64 * hh + 64, 0, 0, 8 * o:8 * o + 8], rf[:, C * o:C * o + C],
                            tw.ct("dft", lo=8 * hh, n=8), start=True, stop=True, tile_position=(0, 64 * hh))
                last.then_inc(fold_mm, 1)
                pe.wait_ge(fold_sb, 1)
                def embed(b, u):
                    k = u % K
                    pe.wait_ge(emb_sb.sem, emb_sb.before(b, K))
                    for kk in range(8):
                        s, chunk = kk // 2, kk % 2
                        for vh in range(2):
                            last = nc.tensor.matmul(
                                ps_e[64 * vh:64 * vh + 64, k, :], wt[:, kk, :],
                                xs[u][:, chunk:chunk + NP, s, 32 * vh:32 * vh + 32],
                                start=kk == 0, stop=kk == 7, tile_position=(0, 64 * vh))
                    last.then_inc(emb_mm.sem, 1)

                def token_major(b, u):
                    k = u % K
                    pe.wait_ge(emb_sb.sem, emb_sb.now(b))
                    pe.wait_ge(h_out.sem, h_out.before(b, K))
                    for vh in range(2):
                        rows = slice(64 * vh, 64 * vh + 64)
                        for t in range(NT // 2):
                            last = nc.tensor.matmul(
                                ps_h[:, k, vh, D * t:D * t + D], embT[k][rows, P * t:P * t + P],
                                tw.c[rows, CONSTS["ident"][1] + 64 * vh:CONSTS["ident"][1] + 64 * vh + 64],
                                start=True, stop=True)
                    last.then_inc(tr_mm.sem, 1)

                with pe.Fori(0, B // U) as i:
                    for u in range(U):
                        pe.wait_ge(x_in[u], (i + 1) * 64)
                        embed(i * U + u, u)
                        if u:
                            token_major(i * U + u - 1, u - 1)
                    token_major(i * U + U - 1, U - 1)

            @block.scalar
            def _(act):
                prime(act, [emb_sb])
                act.wait_ge(fold_mm, 1)
                nc.scalar.copy(wt[:, :, :], ps_h[:, 0, 0, :].rearrange("p (o k) -> p k o", k=8)).then_inc(fold_sb, 1)
                with act.Fori(0, B // U) as i:
                    for u in range(U):
                        b = i * U + u
                        act.wait_ge(emb_mm.sem, emb_mm.now(b))
                        act.wait_ge(tr_mm.sem, tr_mm.before(b, K))
                        nc.scalar.copy(embT[u % K][:, :].rearrange("p (v n) -> p v n", n=NP),
                                       ps_e[:, u % K, :].rearrange("p (n v) -> p v n", n=NP)).then_inc(emb_sb.sem, 1)

            @block.vector
            def _(dve):
                prime(dve, [h_out])
                with dve.Fori(0, B // U) as i:
                    for u in range(U):
                        b = i * U + u
                        dve.wait_ge(tr_mm.sem, tr_mm.now(b))
                        nc.vector.tensor_copy(
                            tw.h[:, bass.ds(b, 1), :].rearrange("p a (g f) -> p (a g) f", g=2),
                            ps_h[:, u % K, :, 0:256]).then_inc(h_out.sem, 1)


class Norm:

    def __init__(self, st, U, xn=None):
        self.st, self.nc, self.U = st, st.nc, U
        self.xn = xn or [st.sb(f"xn{u}", [P, NT, D]) for u in range(U)]
        self.xc = [st.sb(f"xc{u}", [P, NT, D]) for u in range(U)]
        self.sq = [st.sb(f"sq{u}", [P, NT, D]) for u in range(U)]
        self.stat = [st.sb(f"stat{u}", [P, 5, NT]) for u in range(U)]
        self.sum, self.mean, self.cent, self.sqr, self.var, self.eps, self.rstd, self.out = st.steps(
            "ln_sum ln_mean ln_cent ln_sqr ln_var ln_eps ln_rstd ln_out")
        self.dve_steps = [self.sum, self.mean, self.cent, self.var, self.eps, self.out]

    def center(self, dve, q, u, xn_used, b=None):
        nc, stat, h = self.nc, self.stat[u], self.st.tw.h_at(q if b is None else b)
        dve.wait_ge(xn_used.sem, xn_used.before(q, self.U))
        nc.vector.reduce_sum(stat[:, 0, :], h, axis=AX_X).then_inc(self.sum.sem, 1)
        dve.wait_ge(self.sum.sem, self.sum.now(q))
        nc.vector.tensor_scalar(stat[:, 1, :], stat[:, 0, :], 1.0 / D, None, ALU.mult).then_inc(self.mean.sem, 1)
        dve.wait_ge(self.mean.sem, self.mean.now(q))
        nc.vector.tensor_tensor(self.xc[u][:, :, :], h, bc(stat[:, 1, :], D),
                                ALU.subtract).then_inc(self.cent.sem, 1)

    def square(self, act, q, u):
        act.wait_ge(self.cent.sem, self.cent.now(q))
        self.nc.scalar.activation(self.sq[u][:, :, :], self.xc[u][:, :, :], ACT.Square).then_inc(self.sqr.sem, 1)

    def variance(self, dve, q, u):
        dve.wait_ge(self.sqr.sem, self.sqr.now(q))
        stat = self.stat[u]
        self.nc.vector.reduce_sum(stat[:, 2, :], self.sq[u][:, :, :], axis=AX_X).then_inc(self.var.sem, 1)
        dve.wait_ge(self.var.sem, self.var.now(q))
        self.nc.vector.tensor_scalar(stat[:, 3, :], stat[:, 2, :], 1.0 / D, 1e-5, ALU.mult,
                                     ALU.add).then_inc(self.eps.sem, 1)

    def inverse_root(self, pool, q, u):
        nc, stat = self.nc, self.stat[u]
        pool.wait_ge(self.eps.sem, self.eps.now(q))
        nc.gpsimd.tensor_tensor(stat[:, 4, :], stat[:, 3, :], self.st.tw.neg_half[:, :],
                                ALU.pow).then_inc(self.rstd.sem, 1)

    def scale(self, dve, q, u):
        dve.wait_ge(self.rstd.sem, self.rstd.now(q))
        self.nc.vector.tensor_tensor(self.xn[u][:, :, :], self.xc[u][:, :, :], bc(self.stat[u][:, 4, :], D),
                                     ALU.mult).then_inc(self.out.sem, 1)

    def scale_twice(self, pool, q, u, xn2, used=None):
        pool.wait_ge(self.rstd.sem, self.rstd.now(q))
        if used:
            pool.wait_ge(used.sem, used.before(q, self.U))
        for k in range(2):
            last = self.nc.gpsimd.tensor_tensor(xn2[:, :, k, :], self.xc[u][:, :, :], bc(self.stat[u][:, 4, :], D),
                                                ALU.mult)
        last.then_inc(self.out.sem, 1)

    def transpose(self, pe, q, u, ps_x, done):
        pe.wait_ge(self.out.sem, self.out.now(q))
        for t in range(NT // 2):
            last = self.nc.tensor.transpose(ps_x[:, P * t:P * t + P], self.xn[u][:, 2 * t:2 * t + 2, :],
                                            self.st.tw.ct("ident"))
        last.then_inc(done.sem, 1)

    def features(self, act, xT, ps_x, done):
        for par in range(2):
            last = self.nc.scalar.copy(
                xT[0:D, :].rearrange("p (t e n) -> p e t n", e=2, n=P)[:, par],
                ps_x[D * par:D * par + D, :].rearrange("p (t n) -> p t n", n=P))
        last.then_inc(done.sem, 1)


def linear_attention(tw):
    nc, U, R = tw.nc, 2, 4
    with Stage(tw, "lin") as st:
        ln = Norm(st, R)
        wkv = st.sb("wkv", [65, 128])
        xT = [st.sb(f"xT{r}", [65, S]) for r in range(R)]
        z = [st.sb(f"z{r}", [P, 2 * NT, 65]) for r in range(R)]
        kv_sq = [st.sb(f"kv_sq{u}", [P, S]) for u in range(U)]
        dev = [st.sb(f"dev{u}", [P, 3, 256]) for u in range(U)]
        small = [st.sb(f"small{u}", [65, 6, 65]) for u in range(U)]
        g = [st.sb(f"g{u}", [P, NT, D]) for u in range(U)]
        g2 = [st.sb(f"g2{u}", [P, NT, D]) for u in range(U)]
        ps_x = st.ps("ps_x", [P, 512])
        ps_kv = st.ps("ps_kv", [P, U, S])
        ps_s = st.ps("ps_s", [P, U, 512])
        ps_p = st.ps("ps_p", [P, 512])
        wkv_mm, wkv_sb = st.sem("wkv_mm"), st.sem("wkv_sb")
        (xT_mm, xT_sb, kv_mm, kv_sqr, kv_ss, kv_sd, kv_eps, kv_r, z_out, gram_mm, gram_sb, a_mm, a_sb, m_mm,
         m_sb, r_mm, r_sb, w_mm, w_sb, p_mm, gelu, g_add, h_add) = st.steps(
            "xT_mm xT_sb kv_mm kv_sqr kv_ss kv_sd kv_eps kv_r z_out gram_mm gram_sb a_mm a_sb m_mm m_sb r_mm r_sb "
            "w_mm w_sb p_mm gelu g_add h_add")

        def each_pair(engine, body):
            body(None, 0, 1)
            with engine.Fori(0, B // R - 1) as i:
                for half in range(2):
                    q = i * R + U * half
                    body(q, q + U, half)
            body(B - 2 * U, B - U, 0)
            body(B - U, None, 1)

        with nc.Block() as block:
            @block.tensor
            def _(pe):
                def tokens_t(q, r):
                    pe.wait_ge(xT_sb.sem, xT_sb.before(q, 1))
                    ln.transpose(pe, q, r, ps_x, xT_mm)

                def keys_values(q, r, u):
                    pe.wait_ge(xT_sb.sem, xT_sb.now(q))
                    pe.wait_ge(z_out.sem, z_out.before(q, U))
                    for t in range(NT):
                        last = nc.tensor.matmul(ps_kv[:, u, P * t:P * t + P], xT[r][:, P * t:P * t + P],
                                                wkv[:, :], start=True, stop=True)
                    last.then_inc(kv_mm.sem, 1)

                def gram(q, r, u):
                    pe.wait_ge(z_out.sem, z_out.now(q))
                    pe.wait_ge(w_sb.sem, w_sb.before(q, U))
                    for t in range(NT):
                        last = nc.tensor.matmul(ps_s[0:65, u, 0:65], z[r][:, 2 * t + 1, :], z[r][:, 2 * t, :],
                                                start=t == 0, stop=t == NT - 1)
                    last.then_inc(gram_mm.sem, 1)

                def link(q, u, ready, out, lhsT, rhs, done):
                    pe.wait_ge(ready.sem, ready.now(q))
                    nc.tensor.matmul(out, lhsT, rhs, start=True, stop=True).then_inc(done.sem, 1)

                def apply(q, r, u):
                    pe.wait_ge(w_sb.sem, w_sb.now(q))
                    pe.wait_ge(gelu.sem, gelu.before(q, 1))
                    for t in range(NT):
                        last = nc.tensor.matmul(ps_p[:, D * t:D * t + D], xT[r][:, P * t:P * t + P],
                                                small[u][:, 4, 0:64], start=True, stop=True)
                    last.then_inc(p_mm.sem, 1)

                def body(q, nxt, half):
                    mine, other = U * half, U * (1 - half)
                    if q is not None:
                        for u in range(U):
                            gram(q + u, mine + u, u)
                        for u in range(U):
                            link(q + u, u, gram_sb, ps_s[0:65, u, 0:64], small[u][:, 0, :], tw.wt("av"), a_mm)
                    if nxt is not None:
                        tokens_t(nxt, other)
                    if q is not None:
                        for u in range(U):
                            link(q + u, u, a_sb, ps_s[0:64, u, 0:64], tw.wt("ak"), small[u][:, 1, 0:64], m_mm)
                    if nxt is not None:
                        keys_values(nxt, other, 0)
                        tokens_t(nxt + 1, other + 1)
                    if q is not None:
                        for u in range(U):
                            link(q + u, u, m_sb, ps_s[0:64, u, 0:65], small[u][:, 2, 0:64], tw.wt("wqT"), r_mm)
                    if nxt is not None:
                        keys_values(nxt + 1, other + 1, 1)
                    if q is not None:
                        for u in range(U):
                            link(q + u, u, r_sb, ps_s[0:65, u, 0:64], small[u][0:64, 3, :], tw.wt("wpT"), w_mm)
                        for u in range(U):
                            apply(q + u, mine + u, u)

                prime(pe, [xT_mm, kv_mm, gram_mm, a_mm, m_mm, r_mm, w_mm, p_mm])
                nc.tensor.matmul(ps_s[0:65, 0, 0:128], tw.wt("kvT"), tw.ct("center4"),
                                 start=True, stop=True).then_inc(wkv_mm, 1)
                pe.wait_ge(wkv_sb, 1)
                each_pair(pe, body)

            @block.scalar
            def _(act):
                def tokens_sb(q, r):
                    act.wait_ge(xT_mm.sem, xT_mm.now(q))
                    act.wait_ge(p_mm.sem, p_mm.before(q, R))
                    ln.features(act, xT[r], ps_x, xT_sb)

                def squares(q, u):
                    act.wait_ge(kv_mm.sem, kv_mm.now(q))
                    act.wait_ge(kv_ss.sem, kv_ss.before(q, U))
                    nc.scalar.activation(kv_sq[u][:, :], ps_kv[:, u, :], ACT.Square).then_inc(kv_sqr.sem, 1)

                def deviation(q, u):
                    act.wait_ge(kv_ss.sem, kv_ss.now(q))
                    nc.scalar.activation(dev[u][:, 1, :], dev[u][:, 0, :], ACT.Sqrt, scale=1.0 / 3.0
                                         ).then_inc(kv_sd.sem, 1)

                def copied(q, u, ready, k, cols, done):
                    act.wait_ge(ready.sem, ready.now(q))
                    nc.scalar.copy(small[u][:, k, 0:cols], ps_s[0:65, u, 0:cols]).then_inc(done.sem, 1)

                def body(q, nxt, half):
                    other = U * (1 - half)
                    if nxt is not None:
                        for u in range(U):
                            ln.square(act, nxt + u, other + u)
                    if q is not None:
                        for u in range(U):
                            copied(q + u, u, gram_mm, 0, 65, gram_sb)
                        for u in range(U):
                            copied(q + u, u, a_mm, 1, 64, a_sb)
                    if nxt is not None:
                        tokens_sb(nxt, other)
                        squares(nxt, 0)
                        tokens_sb(nxt + 1, other + 1)
                        squares(nxt + 1, 1)
                        deviation(nxt, 0)
                        deviation(nxt + 1, 1)
                    if q is not None:
                        for u in range(U):
                            act.wait_ge(p_mm.sem, p_mm.now(q + u))
                            act.wait_ge(g_add.sem, g_add.before(q + u, U))
                            nc.scalar.activation(g[u][:, :, :], ps_p[:, :].rearrange("p (t f) -> p t f", f=D),
                                                 ACT.Gelu).then_inc(gelu.sem, 1)

                prime(act, [ln.sqr, xT_sb, kv_sqr, kv_sd, gram_sb, a_sb, gelu])
                act.wait_ge(wkv_mm, 1)
                nc.scalar.copy(wkv[:, :], ps_s[0:65, 0, 0:128]).then_inc(wkv_sb, 1)
                each_pair(act, body)

            @block.vector
            def _(dve):
                def sum_squares(q, u):
                    dve.wait_ge(kv_sqr.sem, kv_sqr.now(q))
                    dve.wait_ge(kv_sd.sem, kv_sd.before(q, U))
                    nc.vector.reduce_sum(dev[u][:, 0, :], kv_sq[u][:, :].rearrange("p (g j) -> p g j", j=4),
                                         axis=AX_X).then_inc(kv_ss.sem, 1)

                def normalise(q, r, u):
                    dve.wait_ge(kv_sd.sem, kv_sd.now(q))
                    nc.vector.tensor_scalar(dev[u][:, 2, :], dev[u][:, 1, :], 1e-5, None,
                                            ALU.add).then_inc(kv_eps.sem, 1)
                    dve.wait_ge(kv_eps.sem, kv_eps.now(q))
                    nc.vector.reciprocal(dev[u][:, 2, :], dev[u][:, 2, :]).then_inc(kv_r.sem, 1)
                    dve.wait_ge(kv_r.sem, kv_r.now(q))
                    dve.wait_ge(gram_mm.sem, gram_mm.before(q, R))
                    nc.vector.tensor_tensor(
                        z[r][:, :, 0:64].rearrange("p t (g j) -> p t g j", j=4),
                        ps_kv[:, u, :].rearrange("p (t g j) -> p t g j", g=16, j=4),
                        dev[u][:, 2, :].rearrange("p (t g) -> p t g", g=16).unsqueeze(3).to_broadcast(
                            [P, 2 * NT, 16, 4]), ALU.mult).then_inc(z_out.sem, 1)

                def combined(q, u, ready, rows, k, cols, src, other, op, done):
                    dve.wait_ge(ready.sem, ready.now(q))
                    nc.vector.tensor_tensor(small[u][0:rows, k, 0:cols], src, other, op).then_inc(done.sem, 1)

                def body(q, nxt, half):
                    other = U * (1 - half)
                    if nxt is not None:
                        for u in range(U):
                            ln.center(dve, nxt + u, other + u, g_add)
                        for u in range(U):
                            ln.variance(dve, nxt + u, other + u)
                        for u in range(U):
                            ln.scale(dve, nxt + u, other + u)
                    if q is not None:
                        for u in range(U):
                            combined(q + u, u, m_mm, 64, 2, 64, ps_s[0:64, u, 0:64], tw.ct("kvmask"), ALU.mult, m_sb)
                    if nxt is not None:
                        sum_squares(nxt, 0)
                    if q is not None:
                        for u in range(U):
                            combined(q + u, u, r_mm, 64, 3, 65, ps_s[0:64, u, 0:65], tw.ct("iaug"), ALU.add, r_sb)
                    if q is not None:
                        for u in range(U):
                            dve.wait_ge(p_mm.sem, p_mm.before(q + u, U))
                            combined(q + u, u, w_mm, 65, 4, 64, ps_s[0:65, u, 0:64], tw.wt("bp"), ALU.add, w_sb)
                    if nxt is not None:
                        sum_squares(nxt + 1, 1)
                        for u in range(U):
                            normalise(nxt + u, other + u, u)

                prime(dve, ln.dve_steps + [kv_ss, kv_eps, kv_r, z_out, m_sb, r_sb, w_sb])
                for r in range(R):
                    nc.vector.memset(xT[r][64:65, :], 1.0)
                    nc.vector.memset(z[r][:, :, 64:65], 1.0)
                for u in range(U):
                    nc.vector.memset(small[u][64:65, 2, :], 0.0)
                each_pair(dve, body)

            @block.gpsimd
            def _(pool):
                def body(q, nxt, half):
                    if nxt is not None:
                        for u in range(U):
                            ln.inverse_root(pool, nxt + u, U * (1 - half) + u)
                    if q is not None:
                        for u in range(U):
                            pool.wait_ge(gelu.sem, gelu.now(q + u))
                            pool.wait_ge(h_add.sem, h_add.before(q + u, U))
                            nc.gpsimd.tensor_tensor(g2[u][:, :, :], g[u][:, :, :], ln.xn[U * half + u][:, :, :],
                                                    ALU.add).then_inc(g_add.sem, 1)
                            pool.wait_ge(g_add.sem, g_add.now(q + u))
                            nc.gpsimd.tensor_tensor(tw.h_at(q + u), tw.h_at(q + u), g2[u][:, :, :],
                                                    ALU.add).then_inc(h_add.sem, 1)

                prime(pool, [ln.rstd, g_add, h_add])
                each_pair(pool, body)


def routed_ffn(tw):
    nc, U = tw.nc, 2
    PAIRS = E6 // 2
    GR = 32 + E6
    with Stage(tw, "moe") as st:
        ln = Norm(st, U)
        xn2 = [st.sb(f"xn2{u}", [P, NT, 2, D]) for u in range(U)]
        xs = [st.sb(f"xs{u}", [P, S], F32R) for u in range(U)]
        w1 = [st.sb(f"w1{k}", [P, E6 * D], F32R) for k in range(2)]
        wr = [st.sb(f"wr{k}", [P, 33], F32R) for k in range(2)]
        pair = st.sb("pair", [GR, PAIRS * P], F32R)
        rT = st.sb("rT", [33, S])
        route = st.sb("route", [P, 8, NT, E6])
        best = st.sb("best", [P, 8, NT])
        gates = st.sb("gates", [P, NT, GR])
        gT = st.sb("gT", [GR, S], F32R)
        h1 = st.sb("h1", [P, 2, 512])
        h2 = st.sb("h2", [P, E6, 512])
        h2g = st.sb("h2g", [P, E6, 512])
        o = st.sb("o", [P, 512])
        ps_x = st.ps("ps_x", [P, S])
        ps_1 = st.ps("ps_1", [P, 2, 512])
        ps_2 = st.ps("ps_2", [P, 2, 512])
        ps_b = st.ps("ps_b", [P, 512])
        ps_o = st.ps("ps_o", [P, 512])
        split_hi, split_lo, cleared = st.sem("split_hi"), st.sem("split_lo"), st.sem("cleared")
        (x_mm, x_hi, x_lo, r_mm, r_sb, l_mm, l_max, l_sub, l_exp, l_sum, l_rec, prob, max1, eq1, pref1, mp1, sel1,
         rest, max2, eq2, pref2, mp2, sel2, diff, dexp, dsum, wa, wb, g1, g2, gate, gT_mm, gT_hi, gT_lo, h1_mm,
         h1_sb, h2_mm, h2_sb, b_mm, b_mul, o_mm, o_sb, o_tr, h_add) = st.steps(
            "x_mm x_hi x_lo r_mm r_sb l_mm l_max l_sub l_exp l_sum l_rec prob max1 eq1 pref1 mp1 sel1 rest max2 eq2 "
            "pref2 mp2 sel2 diff dexp dsum wa wb g1 g2 gate gT_mm gT_hi gT_lo h1_mm h1_sb h2_mm h2_sb b_mm b_mul "
            "o_mm o_sb o_tr h_add")
        blocks = [(c, p) for c in range(2) for p in range(PAIRS)]
        NB = len(blocks)

        def each_image(engine, body):
            with engine.Fori(0, B // U - 1) as i:
                for u in range(U):
                    body(i * U + u, u, True, True)
            body(B - 2, 0, True, False)
            body(B - 1, 1, False, False)

        with nc.Block() as block:
            @block.tensor
            def _(pe):
                def tokens_t(q, u):
                    pe.wait_ge(gT_lo.sem, gT_lo.before(q, 1))
                    pe.wait_ge(ln.out.sem, ln.out.now(q))
                    for t in range(NT):
                        last = nc.tensor.transpose(ps_x[:, P * t:P * t + P], xn2[u][:, t], tw.ct("ident"))
                    last.then_inc(x_mm.sem, 1)

                def router_hidden(q, u):
                    pe.wait_ge(x_lo.sem, x_lo.now(q))
                    for c in range(2):
                        for k in range(2):
                            last = nc.tensor.matmul(ps_x[0:33, 512 * c:512 * c + 512], wr[k][:, :],
                                                    xs[u][:, 512 * c:512 * c + 512], start=k == 0, stop=k == 1)
                    last.then_inc(r_mm.sem, 1)

                def router_logits(q):
                    pe.wait_ge(r_sb.sem, r_sb.now(q))
                    for t in range(NT):
                        last = nc.tensor.matmul(ps_x[:, E6 * t:E6 * t + E6], rT[:, P * t:P * t + P],
                                                tw.wt("rw2"), start=True, stop=True)
                    last.then_inc(l_mm.sem, 1)

                def first_layer(q, u, j):
                    c, p = blocks[j]
                    pe.wait_ge(h1_sb.sem, h1_sb.before(q * NB + j, 2))
                    for k in range(2):
                        last = nc.tensor.matmul(ps_1[:, j % 2, :], w1[k][:, P * p:P * p + P],
                                                xs[u][:, 512 * c:512 * c + 512], start=k == 0, stop=k == 1)
                    last.then_inc(h1_mm.sem, 1)

                def second_layer(q, j):
                    k, p = q * NB + j, blocks[j][1]
                    pe.wait_ge(h2_sb.sem, h2_sb.before(k, 2))
                    pe.wait_ge(h1_sb.sem, h1_sb.now(k))
                    for e in range(2):
                        last = nc.tensor.matmul(ps_2[64 * e:64 * e + 64, j % 2, :],
                                                tw.wt("ew2", lo=P * p + 64 * e, n=64), h1[:, j % 2, :],
                                                start=True, stop=True, tile_position=(0, 64 * e))
                    last.then_inc(h2_mm.sem, 1)

                def gates_t(q):
                    pe.wait_ge(gate.sem, gate.now(q))
                    for t in range(NT):
                        last = nc.tensor.matmul(ps_x[0:GR, P * t:P * t + P], gates[:, t, :], tw.ct("ident"),
                                                start=True, stop=True)
                    last.then_inc(gT_mm.sem, 1)

                def spread(q, j):
                    c, p = blocks[j]
                    pe.wait_ge(gT_lo.sem, gT_lo.now(q))
                    pe.wait_ge(b_mul.sem, b_mul.before(q * NB + j, 1))
                    nc.tensor.matmul(ps_b[:, :], pair[:, P * p:P * p + P], gT[:, 512 * c:512 * c + 512],
                                     start=True, stop=True).then_inc(b_mm.sem, 1)

                def third_layer(q):
                    pe.wait_ge(h_add.sem, h_add.before(q, 1))
                    for p in range(PAIRS + 1):
                        for c in range(2):
                            if p < PAIRS:
                                pe.wait_ge(b_mul.sem, b_mul.now(q * NB + PAIRS * c + p))
                                w, x = tw.wt("ew3", lo=D * p, n=D), h2g[:, PAIRS * c + p, :]
                            else:
                                w, x = tw.wt("eb3"), gT[:, 512 * c:512 * c + 512].bitcast(F32)
                            last = nc.tensor.matmul(ps_o[64 * c:64 * c + 64, :], w, x, start=p == 0, stop=p == PAIRS,
                                                    tile_position=(0, 64 * c))
                    last.then_inc(o_mm.sem, 1)

                def outputs_t(q):
                    pe.wait_ge(o_sb.sem, o_sb.now(q))
                    for t in range(NT // 2):
                        last = nc.tensor.transpose(ps_o[:, P * t:P * t + P], o[:, P * t:P * t + P], tw.ct("ident"))
                    last.then_inc(o_tr.sem, 1)

                def body(q, u, front, norm):
                    first_layer(q, u, 0)
                    first_layer(q, u, 1)
                    second_layer(q, 0)
                    first_layer(q, u, 2)
                    second_layer(q, 1)
                    gates_t(q)
                    first_layer(q, u, 3)
                    second_layer(q, 2)
                    spread(q, 0)
                    if front:
                        tokens_t(q + 1, 1 - u)
                    first_layer(q, u, 4)
                    second_layer(q, 3)
                    spread(q, 1)
                    first_layer(q, u, 5)
                    second_layer(q, 4)
                    spread(q, 2)
                    if front:
                        router_hidden(q + 1, 1 - u)
                    second_layer(q, 5)
                    spread(q, 3)
                    spread(q, 4)
                    if front:
                        router_logits(q + 1)
                    spread(q, 5)
                    third_layer(q)
                    outputs_t(q)

                prime(pe, [x_mm, r_mm, l_mm, gT_mm, h1_mm, h2_mm, b_mm, o_mm, o_tr])
                pe.wait_ge(split_lo, 2)
                pe.wait_ge(cleared, 1)
                tokens_t(0, 0)
                router_hidden(0, 0)
                router_logits(0)
                each_image(pe, body)

            @block.scalar
            def _(act):
                def tokens_high(q, u):
                    act.wait_ge(x_mm.sem, x_mm.now(q))
                    act.wait_ge(h1_mm.sem, h1_mm.before((q - 1) * NB, 1))
                    nc.scalar.copy(xs[u][:, :], ps_x[:, :]).then_inc(x_hi.sem, 1)

                def router_hidden(q):
                    act.wait_ge(r_mm.sem, r_mm.now(q))
                    act.wait_ge(l_mm.sem, l_mm.before(q, 1))
                    nc.scalar.activation(rT[:, :], ps_x[0:33, :], ACT.Relu, bias=tw.wt("rb1")).then_inc(r_sb.sem, 1)

                def router_exp(q):
                    act.wait_ge(l_sub.sem, l_sub.now(q))
                    nc.scalar.activation(route[:, 1], route[:, 0], ACT.Exp).then_inc(l_exp.sem, 1)

                def best_exp(q):
                    act.wait_ge(diff.sem, diff.now(q))
                    nc.scalar.activation(best[:, 5, :], best[:, 4, :], ACT.Exp).then_inc(dexp.sem, 1)

                def first_relu(q, j):
                    k = q * NB + j
                    act.wait_ge(h1_mm.sem, h1_mm.now(k))
                    act.wait_ge(h2_mm.sem, h2_mm.before(k, 2))
                    nc.scalar.activation(h1[:, j % 2, :], ps_1[:, j % 2, :], ACT.Relu,
                                         bias=tw.wt("eb1", lo=blocks[j][1], n=1)).then_inc(h1_sb.sem, 1)

                def second_relu(q, j):
                    k = q * NB + j
                    act.wait_ge(h2_mm.sem, h2_mm.now(k))
                    act.wait_ge(b_mul.sem, b_mul.before(k, NB))
                    nc.scalar.activation(h2[:, j, :], ps_2[:, j % 2, :], ACT.Relu,
                                         bias=tw.wt("eb2", lo=blocks[j][1], n=1)).then_inc(h2_sb.sem, 1)

                def gates_high(q):
                    act.wait_ge(gT_mm.sem, gT_mm.now(q))
                    act.wait_ge(o_mm.sem, o_mm.before(q, 1))
                    nc.scalar.copy(gT[:, :], ps_x[0:GR, :]).then_inc(gT_hi.sem, 1)

                def outputs(q):
                    act.wait_ge(o_mm.sem, o_mm.now(q))
                    nc.scalar.copy(o[:, :], ps_o[:, :]).then_inc(o_sb.sem, 1)

                def body(q, u, front, norm):
                    first_relu(q, 0)
                    first_relu(q, 1)
                    second_relu(q, 0)
                    first_relu(q, 2)
                    second_relu(q, 1)
                    gates_high(q)
                    first_relu(q, 3)
                    second_relu(q, 2)
                    if front:
                        tokens_high(q + 1, 1 - u)
                    first_relu(q, 4)
                    second_relu(q, 3)
                    first_relu(q, 5)
                    second_relu(q, 4)
                    if front:
                        router_hidden(q + 1)
                    second_relu(q, 5)
                    if front:
                        router_exp(q + 1)
                    outputs(q)
                    if front:
                        best_exp(q + 1)
                    if norm:
                        ln.square(act, q + 2, u)

                prime(act, [ln.sqr, x_hi, r_sb, l_exp, dexp, gT_hi, h1_sb, h2_sb, o_sb])
                for wide, name in ((w1, "ew1"), (wr, "rw1")):
                    nc.scalar.copy(wide[0][:, :], tw.wt(name)).then_inc(split_hi, 1)
                nc.scalar.copy(pair[:, :], tw.ct("pair")).then_inc(cleared, 1)
                ln.square(act, 0, 0)
                ln.square(act, 1, 1)
                tokens_high(0, 0)
                router_hidden(0)
                router_exp(0)
                best_exp(0)
                each_image(act, body)

            @block.vector
            def _(dve):
                rank = tw.ct("rank").rearrange("p (t e) -> p t e", e=E6)

                def then(step, q, op):
                    op.then_inc(step.sem, 1)
                    dve.wait_ge(step.sem, step.now(q))

                def rests(q, hi, lo, tile, ps, r0, rows):
                    dve.wait_ge(hi.sem, hi.now(q))
                    part = tile[r0:r0 + rows, :]
                    nc.vector.tensor_tensor(part, ps[r0:r0 + rows, :], part, ALU.subtract).then_inc(lo.sem, 1)

                def routing(q):
                    r, s = route, best
                    logits = ps_x[:, 0:NT * E6].rearrange("p (t e) -> p t e", e=E6)
                    dve.wait_ge(l_mm.sem, l_mm.now(q))
                    then(l_max, q, nc.vector.reduce_max(s[:, 0, :], logits, axis=AX_X))
                    nc.vector.tensor_tensor(r[:, 0], logits, bc(s[:, 0, :], E6), ALU.subtract).then_inc(l_sub.sem, 1)
                    dve.wait_ge(l_exp.sem, l_exp.now(q))
                    then(l_sum, q, nc.vector.reduce_sum(s[:, 0, :], r[:, 1], axis=AX_X))
                    then(l_rec, q, nc.vector.reciprocal(s[:, 1, :], s[:, 0, :]))
                    then(prob, q, nc.vector.tensor_tensor(r[:, 2], r[:, 1], bc(s[:, 1, :], E6), ALU.mult))
                    then(max1, q, nc.vector.reduce_max(s[:, 2, :], r[:, 2], axis=AX_X))
                    then(eq1, q, nc.vector.tensor_tensor(r[:, 3], r[:, 2], bc(s[:, 2, :], E6), ALU.is_equal))
                    then(pref1, q, nc.vector.tensor_tensor(r[:, 3], r[:, 3], rank, ALU.mult))
                    then(mp1, q, nc.vector.reduce_max(s[:, 0, :], r[:, 3], axis=AX_X))
                    then(sel1, q, nc.vector.tensor_tensor(r[:, 4], r[:, 3], bc(s[:, 0, :], E6), ALU.is_equal))
                    then(rest, q, nc.vector.scalar_tensor_tensor(r[:, 5], r[:, 4], -2.0, r[:, 2], ALU.mult, ALU.add))
                    then(max2, q, nc.vector.reduce_max(s[:, 3, :], r[:, 5], axis=AX_X))
                    nc.vector.tensor_tensor(s[:, 4, :], s[:, 3, :], s[:, 2, :], ALU.subtract).then_inc(diff.sem, 1)
                    then(eq2, q, nc.vector.tensor_tensor(r[:, 6], r[:, 5], bc(s[:, 3, :], E6), ALU.is_equal))
                    then(pref2, q, nc.vector.tensor_tensor(r[:, 6], r[:, 6], rank, ALU.mult))
                    then(mp2, q, nc.vector.reduce_max(s[:, 0, :], r[:, 6], axis=AX_X))
                    then(sel2, q, nc.vector.tensor_tensor(r[:, 7], r[:, 6], bc(s[:, 0, :], E6), ALU.is_equal))
                    dve.wait_ge(dexp.sem, dexp.now(q))
                    then(dsum, q, nc.vector.tensor_scalar(s[:, 6, :], s[:, 5, :], 1.0, None, ALU.add))
                    then(wa, q, nc.vector.reciprocal(s[:, 6, :], s[:, 6, :]))
                    then(wb, q, nc.vector.tensor_tensor(s[:, 7, :], s[:, 5, :], s[:, 6, :], ALU.mult))
                    then(g1, q, nc.vector.tensor_tensor(r[:, 4], r[:, 4], bc(s[:, 6, :], E6), ALU.mult))
                    then(g2, q, nc.vector.tensor_tensor(r[:, 7], r[:, 7], bc(s[:, 7, :], E6), ALU.mult))
                    dve.wait_ge(gT_mm.sem, gT_mm.before(q, 1))
                    for k in range(2):
                        last = nc.vector.tensor_tensor(gates[:, :, 32 * k:32 * k + E6], r[:, 4], r[:, 7], ALU.add)
                    last.then_inc(gate.sem, 1)

                def weigh(q, j):
                    k = q * NB + j
                    dve.wait_ge(h2_sb.sem, h2_sb.now(k))
                    dve.wait_ge(b_mm.sem, b_mm.now(k))
                    dve.wait_ge(o_mm.sem, o_mm.before(q, 1))
                    nc.vector.tensor_tensor(h2g[:, j, :], h2[:, j, :], ps_b[:, :], ALU.mult).then_inc(b_mul.sem, 1)

                def add(q):
                    dve.wait_ge(o_tr.sem, o_tr.now(q))
                    h = tw.h_at(q).rearrange("p (c t) f -> p t c f", c=2)
                    nc.vector.tensor_tensor(h, h, ps_o[:, :].rearrange("p (t c f) -> p t c f", c=2, f=D),
                                            ALU.add).then_inc(h_add.sem, 1)

                def body(q, u, front, norm):
                    rests(q, gT_hi, gT_lo, gT, ps_x, 32, E6)
                    weigh(q, 0)
                    if front:
                        rests(q + 1, x_hi, x_lo, xs[1 - u], ps_x, 64, 64)
                    for j in range(1, NB):
                        weigh(q, j)
                    if norm:
                        ln.center(dve, q + 2, u, ln.out)
                    if front:
                        routing(q + 1)
                    if norm:
                        ln.variance(dve, q + 2, u)
                    add(q)

                prime(dve, ln.dve_steps[:-1] + [
                    x_lo, l_max, l_sub, l_sum, l_rec, prob, max1, eq1, pref1, mp1, sel1, rest, max2, eq2, pref2, mp2,
                    sel2, diff, dsum, wa, wb, g1, g2, gate, gT_lo, b_mul, h_add])
                dve.wait_ge(split_hi, 2)
                for wide, name in ((w1, "ew1"), (wr, "rw1")):
                    nc.vector.tensor_tensor(wide[1][:, :], tw.wt(name), wide[0][:, :], ALU.subtract
                                            ).then_inc(split_lo, 1)
                nc.vector.memset(gates[:, :, :], 0.0)
                for q in range(2):
                    ln.center(dve, q, q, ln.out)
                for q in range(2):
                    ln.variance(dve, q, q)
                rests(0, x_hi, x_lo, xs[0], ps_x, 64, 64)
                routing(0)
                each_image(dve, body)

            @block.gpsimd
            def _(pool):
                def finish(q, u):
                    ln.inverse_root(pool, q, u)
                    ln.scale_twice(pool, q, u, xn2[u], x_mm)

                prime(pool, [ln.rstd, ln.out])
                finish(0, 0)
                finish(1, 1)
                each_image(pool, lambda q, u, front, norm: finish(q + 2, u) if norm else None)


def softmax_attention(tw):
    nc, U = tw.nc, 3
    with Stage(tw, "att") as st:
        ln = Norm(st, 1)
        xn2 = st.sb("xn2", [P, NT, 2, D])
        xs = st.sb("xs", [P, S], F32R)
        split = {name: [st.sb(f"{name}{k}", [P, cols], F32R) for k in range(2)]
                 for name, cols in (("wqq", 128), ("wkk", 128), ("wv1", D))}
        qs = [st.sb(f"qs{u}", [P, S], F32R) for u in range(U)]
        qm = [st.sb(f"qm{u}", [P, S], F32R) for u in range(U)]
        kh = [st.sb(f"kh{u}", [P, S], F32R) for u in range(U)]
        kl = [st.sb(f"kl{u}", [P, S], F32R) for u in range(U)]
        v = [st.sb(f"v{u}", [P, NT, 65]) for u in range(U)]
        neg_max = st.sb("neg_max", [P, NT])
        probs = st.sb("probs", [P, 4, S])
        oT = st.sb("oT", [65, S])
        inv = st.sb("inv", [P, 2, NT])
        o = st.sb("o", [P, NT, D])
        ps_x = st.ps("ps_x", [P, S])
        ps_s = st.ps("ps_s", [P, 2, S])
        ps_o = st.ps("ps_o", [P, S])
        split_hi, split_lo, zeros, ones = (st.sem(n) for n in ("split_hi", "split_lo", "zeros", "ones"))
        (x_mm, x_hi, x_lo, q_mm, q_hi, q_m, q_lo, k_mm, k_hi, k_lo, v_mm, v_sb, m_zero, s1_mm, s1_max, m_mm, m_sb,
         s2_mm, s2_exp, pv_mm, oT_sb, o_tr, rec, rec8, o_sb, h_add) = st.steps(
            "x_mm x_hi x_lo q_mm q_hi q_m q_lo k_mm k_hi k_lo v_mm v_sb m_zero s1_mm s1_max m_mm m_sb "
            "s2_mm s2_exp pv_mm oT_sb o_tr rec rec8 o_sb h_add")

        def each_image(engine, body):
            body(0, 0, 3, True)
            with engine.Fori(0, (B - 4) // U) as i:
                for u in range(U):
                    body(i * U + u + 1, (u + 1) % U, 3, False)
            for q in range(B - 3, B):
                body(q, q % U, B - 1 - q, False)

        with nc.Block() as block:
            @block.tensor
            def _(pe):
                def tokens_t(q, freed):
                    pe.wait_ge(*freed)
                    pe.wait_ge(ln.out.sem, ln.out.now(q))
                    for t in range(NT):
                        last = nc.tensor.transpose(ps_x[:, P * t:P * t + P], xn2[:, t], tw.ct("ident"))
                    last.then_inc(x_mm.sem, 1)

                def project(name, done):
                    for c in range(2):
                        for k in range(2):
                            last = nc.tensor.matmul(ps_x[:, 512 * c:512 * c + 512], split[name][k][:, :],
                                                    xs[:, 512 * c:512 * c + 512], start=k == 0, stop=k == 1)
                    last.then_inc(done.sem, 1)

                def queries(q):
                    pe.wait_ge(x_lo.sem, x_lo.now(q))
                    project("wqq", q_mm)

                def keys(q):
                    pe.wait_ge(q_m.sem, q_m.now(q))
                    pe.wait_ge(q_lo.sem, q_lo.now(q))
                    project("wkk", k_mm)

                def values_of(q):
                    pe.wait_ge(k_lo.sem, k_lo.now(q))
                    for t in range(NT):
                        for k in range(2):
                            last = nc.tensor.matmul(ps_x[:, D * t:D * t + D], xs[:, P * t:P * t + P],
                                                    split["wv1"][k][:, :], start=k == 0, stop=k == 1)
                    last.then_inc(v_mm.sem, 1)

                def scores(q, u, t):
                    if t == 0:
                        pe.wait_ge(m_zero.sem, m_zero.now(q))
                        pe.wait_ge(k_lo.sem, k_lo.now(q))
                    pe.wait_ge(s1_max.sem, s1_max.before(q * NT + t, 1))
                    for c in range(2):
                        cols = slice(512 * c, 512 * c + 512)
                        nc.tensor.matmul(ps_s[:, 0, cols], qs[u][:, P * t:P * t + P], kh[u][:, cols],
                                         start=True, stop=False)
                        last = nc.tensor.matmul(ps_s[:, 0, cols], qm[u][:, P * t:P * t + P], kl[u][:, cols],
                                                start=False, stop=True)
                    last.then_inc(s1_mm.sem, 1)

                def scores_t(q, u, t):
                    if t == 0:
                        pe.wait_ge(m_sb.sem, m_sb.now(q))
                    pe.wait_ge(s2_exp.sem, s2_exp.before(q * NT + t, 1))
                    for c in range(2):
                        cols = slice(512 * c, 512 * c + 512)
                        nc.tensor.matmul(ps_s[:, 1, cols], kh[u][:, P * t:P * t + P], qs[u][:, cols],
                                         start=True, stop=False)
                        last = nc.tensor.matmul(ps_s[:, 1, cols], kl[u][:, P * t:P * t + P], qm[u][:, cols],
                                                start=False, stop=True)
                    last.then_inc(s2_mm.sem, 1)

                def weighed(q, u, t):
                    pe.wait_ge(s2_exp.sem, s2_exp.now(q * NT + t))
                    if t == 0:
                        pe.wait_ge(oT_sb.sem, oT_sb.before(q, 1))
                    for c in range(2):
                        cols = slice(512 * c, 512 * c + 512)
                        last = nc.tensor.matmul(ps_o[0:65, cols], v[u][:, t, :], probs[:, t % 4, cols],
                                                start=t == 0, stop=t == NT - 1)
                    last.then_inc(pv_mm.sem, 1)

                def maxima(q, freed):
                    pe.wait_ge(*freed)
                    pe.wait_ge(s1_max.sem, s1_max.now(q * NT + NT - 1))
                    for t in range(NT):
                        last = nc.tensor.matmul(ps_x[0:1, P * t:P * t + P], neg_max[:, t:t + 1], tw.ct("ident"),
                                                start=True, stop=True)
                    last.then_inc(m_mm.sem, 1)

                def outputs(q):
                    pe.wait_ge(oT_sb.sem, oT_sb.now(q))
                    for t in range(NT):
                        last = nc.tensor.transpose(ps_x[:, P * t:P * t + 65], oT[:, P * t:P * t + P],
                                                   tw.c[0:65, CONSTS["ident"][1]:CONSTS["ident"][1] + 65])
                    last.then_inc(o_tr.sem, 1)

                def body(q, u, ahead, first):
                    for t in range(NT):
                        if ahead >= 1:
                            scores(q + 1, (u + 1) % U, t)
                        scores_t(q, u, t)
                        if t >= 1:
                            weighed(q, u, t - 1)
                        if t == 1 and not first:
                            outputs(q - 1)
                        if ahead >= 2:
                            if t == 2:
                                tokens_t(q + 2, (o_sb.sem, o_sb.before(q, 1)))
                            elif t == 3:
                                queries(q + 2)
                            elif t == 4:
                                keys(q + 2)
                            elif t == 5:
                                values_of(q + 2)
                    weighed(q, u, NT - 1)
                    if ahead >= 2:
                        maxima(q + 1, (v_sb.sem, v_sb.now(q + 2)))
                    elif ahead == 1:
                        maxima(q + 1, (o_sb.sem, o_sb.before(q, 1)))

                prime(pe, [x_mm, q_mm, k_mm, v_mm, s1_mm, m_mm, s2_mm, pv_mm, o_tr])
                for q in range(2):
                    tokens_t(q, (v_sb.sem, v_sb.before(q, 1)))
                    if q == 0:
                        pe.wait_ge(split_lo, 3)
                        pe.wait_ge(ones, 1)
                    queries(q)
                    keys(q)
                    values_of(q)
                for t in range(NT):
                    scores(0, 0, t)
                maxima(0, (v_sb.sem, v_sb.now(1)))
                each_image(pe, body)
                pe.wait_ge(o_sb.sem, o_sb.now(B - 2))
                outputs(B - 1)

            @block.scalar
            def _(act):
                def tokens_high(q):
                    act.wait_ge(x_mm.sem, x_mm.now(q))
                    act.wait_ge(v_mm.sem, v_mm.before(q, 1))
                    nc.scalar.copy(xs[:, :], ps_x[:, :]).then_inc(x_hi.sem, 1)

                def queries(q, u):
                    act.wait_ge(q_mm.sem, q_mm.now(q))
                    act.wait_ge(s2_mm.sem, s2_mm.before((q - U + 1) * NT, 1))
                    nc.scalar.copy(qs[u][:, :], ps_x[:, :]).then_inc(q_hi.sem, 1)
                    nc.scalar.copy(qm[u][0:D, :], ps_x[0:D, :]).then_inc(q_m.sem, 1)

                def keys(q, u):
                    act.wait_ge(k_mm.sem, k_mm.now(q))
                    nc.scalar.copy(kh[u][:, :], ps_x[:, :]).then_inc(k_hi.sem, 1)

                def values_of(q, u):
                    act.wait_ge(v_mm.sem, v_mm.now(q))
                    act.wait_ge(pv_mm.sem, pv_mm.before((q - U + 1) * NT, 1))
                    nc.scalar.copy(v[u][:, :, 0:D], ps_x[:, 0:512].rearrange("p (t f) -> p t f", f=D)
                                   ).then_inc(v_sb.sem, 1)

                def maxima(q, u):
                    act.wait_ge(m_mm.sem, m_mm.now(q))
                    nc.scalar.copy(qm[u][D:D + 1, :], ps_x[0:1, :]).then_inc(m_sb.sem, 1)

                def body(q, u, ahead, first):
                    w = (u + 2) % U
                    for t in range(NT):
                        k = q * NT + t
                        act.wait_ge(s2_mm.sem, s2_mm.now(k))
                        act.wait_ge(pv_mm.sem, pv_mm.before(k, 4))
                        nc.scalar.activation(probs[:, t % 4, :], ps_s[:, 1, :], ACT.Exp).then_inc(s2_exp.sem, 1)
                        if ahead >= 2:
                            if t == 2:
                                tokens_high(q + 2)
                            elif t == 3:
                                queries(q + 2, w)
                            elif t == 4:
                                keys(q + 2, w)
                            elif t == 5:
                                values_of(q + 2, w)
                        if ahead >= 3 and t == 6:
                            ln.square(act, q + 3, 0)
                    if ahead >= 1:
                        maxima(q + 1, (u + 1) % U)

                prime(act, [ln.sqr, x_hi, q_hi, q_m, k_hi, v_sb, m_sb, s2_exp])
                for hi, lo in split.items():
                    nc.scalar.copy(lo[0][:, :], tw.wt(hi)).then_inc(split_hi, 1)
                for q in range(2):
                    ln.square(act, q, 0)
                    tokens_high(q)
                    queries(q, q)
                    keys(q, q)
                    values_of(q, q)
                ln.square(act, 2, 0)
                maxima(0, 0)
                each_image(act, body)

            @block.vector
            def _(dve):
                def rest(q, hi, lo, tile, high, r0):
                    dve.wait_ge(hi.sem, hi.now(q))
                    nc.vector.tensor_tensor(tile[r0:r0 + D, :], ps_x[r0:r0 + D, :], high[r0:r0 + D, :],
                                            ALU.subtract).then_inc(lo.sem, 1)

                def rest_of_queries(q, u):
                    rest(q, q_hi, q_lo, qs[u], qs[u], D)
                    nc.vector.memset(qm[u][D:D + 1, :].bitcast(F32), 0.0).then_inc(m_zero.sem, 1)

                def maximum(q, t):
                    if t == 0:
                        dve.wait_ge(m_mm.sem, m_mm.before(q, 1))
                    dve.wait_ge(s1_mm.sem, s1_mm.now(q * NT + t))
                    nc.vector.tensor_reduce(neg_max[:, t:t + 1], ps_s[:, 0, :], axis=AX_X, op=ALU.max, negate=True
                                            ).then_inc(s1_max.sem, 1)

                def gather(q):
                    dve.wait_ge(pv_mm.sem, pv_mm.now(q * NT + NT - 1))
                    dve.wait_ge(o_tr.sem, o_tr.before(q, 1))
                    nc.vector.tensor_copy(oT[:, :], ps_o[0:65, :]).then_inc(oT_sb.sem, 1)

                def outputs(q):
                    pt = ps_x[:, :].rearrange("p (t f) -> p t f", f=P)
                    dve.wait_ge(o_tr.sem, o_tr.now(q))
                    nc.vector.reciprocal(inv[:, 0, :], pt[:, :, 64]).then_inc(rec.sem, 1)
                    dve.wait_ge(rec.sem, rec.now(q))
                    nc.vector.tensor_scalar(inv[:, 1, :], inv[:, 0, :], float(D) ** -0.5, None, ALU.mult
                                            ).then_inc(rec8.sem, 1)
                    dve.wait_ge(rec8.sem, rec8.now(q))
                    dve.wait_ge(h_add.sem, h_add.before(q, 1))
                    nc.vector.tensor_tensor(o[:, :, :], pt[:, :, 0:64], bc(inv[:, 1, :], D), ALU.mult
                                            ).then_inc(o_sb.sem, 1)

                def body(q, u, ahead, first):
                    w = (u + 2) % U
                    for t in range(NT):
                        if ahead >= 1:
                            maximum(q + 1, t)
                        if t == 1 and not first:
                            outputs(q - 1)
                        if ahead >= 2:
                            if t == 2:
                                rest(q + 2, x_hi, x_lo, xs, xs, D)
                            elif t == 3:
                                rest_of_queries(q + 2, w)
                            elif t == 4:
                                rest(q + 2, k_hi, k_lo, kl[w], kh[w], 0)
                        if ahead >= 3:
                            if t == 5:
                                ln.center(dve, q + 3, 0, ln.out)
                            elif t == 7:
                                ln.variance(dve, q + 3, 0)
                    gather(q)

                prime(dve, ln.dve_steps[:-1] + [x_lo, q_lo, k_lo, m_zero, s1_max, oT_sb, rec, rec8, o_sb])
                for q in range(2):
                    ln.center(dve, q, 0, ln.out)
                    if q == 0:
                        dve.wait_ge(split_hi, 3)
                        for name, parts in split.items():
                            nc.vector.tensor_tensor(parts[1][:, :], tw.wt(name), parts[0][:, :], ALU.subtract
                                                    ).then_inc(split_lo, 1)
                    ln.variance(dve, q, 0)
                    if q == 0:
                        for u in range(U):
                            nc.vector.memset(qm[u][D:P, :].bitcast(F32), 0.0)
                            last = nc.vector.memset(kl[u][D:P, :].bitcast(F32), 0.0)
                        last.then_inc(zeros, 1)
                        dve.wait_ge(zeros, 1)
                        for u in range(U):
                            nc.vector.memset(v[u][:, :, D:D + 1], 1.0)
                            last = nc.vector.memset(kl[u][D:D + 1, :].bitcast(F32), 1.0)
                        last.then_inc(ones, 1)
                    rest(q, x_hi, x_lo, xs, xs, D)
                    rest_of_queries(q, q)
                    rest(q, k_hi, k_lo, kl[q], kh[q], 0)
                ln.center(dve, 2, 0, ln.out)
                ln.variance(dve, 2, 0)
                for t in range(NT):
                    maximum(0, t)
                each_image(dve, body)
                outputs(B - 1)

            @block.gpsimd
            def _(pool):
                def normalise(q):
                    ln.inverse_root(pool, q, 0)
                    ln.scale_twice(pool, q, 0, xn2, x_mm)

                def add(q):
                    pool.wait_ge(o_sb.sem, o_sb.now(q))
                    nc.gpsimd.tensor_tensor(tw.h_at(q), tw.h_at(q), o[:, :, :], ALU.add).then_inc(h_add.sem, 1)

                def body(q, u, ahead, first):
                    if not first:
                        add(q - 1)
                    if ahead >= 3:
                        normalise(q + 3)

                prime(pool, [ln.rstd, ln.out, h_add])
                for q in range(2):
                    normalise(q)
                normalise(2)
                each_image(pool, body)
                add(B - 1)


KEY_STEPS = [(0, 0), (0, 3), (0, 1), (0, 2), (1, 0), (1, 7), (1, 1), (1, 6), (1, 2), (1, 5), (1, 3), (1, 4)]
QUERY_STEPS = [(3, 0), (0, 0), (7, 0), (1, 0), (4, 0), (2, 0), (5, 0), (4, 1), (6, 0), (5, 1), (7, 1), (6, 1)]
EARLY = 2 * 6
assert sorted(KEY_STEPS) == [(c, kb) for c in range(2) for kb in range(4 * c + 4)]
assert sorted(QUERY_STEPS) == [(qb, c) for qb in range(NT) for c in range(qb // 4 + 1)]
assert all(qb >= 4 for qb, c in QUERY_STEPS[EARLY // 2:])
NSTEP = len(KEY_STEPS)
NTILE = 2 * NSTEP
assert len(QUERY_STEPS) == NSTEP and NTILE % 3 == 0 and NSTEP % 3 == 0

SLOT_ITEMS = {1: ("m", 1), 3: ("r", 1), 5: ("k", 0), 7: ("k", 1), 9: ("q", 0), 11: ("q", 1), 13: ("q", 2),
              15: ("q", 3), 17: ("r", 0), 19: ("m", 0), 21: ("mask", 0), 23: ("mask", 1)}
EXTRA_ITEMS = {(0, 0): ("v", 0), (0, 4): ("v", 1), (1, 18): ("fxT", 0), (2, 0): ("x", 0), (2, 4): ("x", 1),
               (2, 18): ("f1", 0), (2, 20): ("f1", 1), (3, 2): ("f2", 0), (3, 18): ("foT", 0), (3, 22): ("fg", 0)}
GATE_AT = (12, 13, 14, 15, 18, 19)
MIXED_AT, OUT_AT = (0, 1, 4, 5), (6, 7, 9, 10)
TAIL_KINDS = ("fxT", "f1", "f2", "foT", "fg")


def items_of(n, first, last):
    out = {}
    for p in range(NTILE):
        item = EXTRA_ITEMS.get((n, p)) or SLOT_ITEMS.get(p)
        if item is None:
            continue
        kind, j = item
        if first and (kind in TAIL_KINDS or (n == 0 and item == ("r", 1))):
            continue
        if last and (kind == "x" or (n >= 2 and kind in "k q mask".split()) or (n == 3 and item == ("m", 0))):
            continue
        out[p] = item
    return out


def expert_attention(tw, out):
    nc = tw.nc
    with Stage(tw, "exp") as st:
        wx = [st.sb(f"wx{k}", [P, NH, 322], F32R) for k in range(2)]
        wm = [st.sb(f"wm{k}", [P, NH, P], F32R) for k in range(2)]
        wb = st.sb("wb", [98, NH, 3])
        v_bias = st.sb("v_bias", [P, NH, 32])
        no_feature = st.sb("no_feature", [P, NH])
        resid = st.sb("resid", [P, NH, NT, DH])
        xn2 = st.sb("xn2", [P, NT, 2, D])
        ln = Norm(st, 1, xn=[None])
        head_inputs(st, wx, wm, wb, v_bias, no_feature, resid)
        causal_heads(st, ln, xn2, wx, wm, wb, v_bias, no_feature, resid, out)


def head_inputs(st, wx, wm, wb, v_bias, no_feature, resid):
    nc, tw = st.nc, st.tw
    with Stage(tw, "hin") as sc:
        tw.hd = sc.sb("hd", [P, H_COLS])
        ln = Norm(sc, NH)
        xT = [sc.sb(f"xT{n}", [65, S]) for n in range(NH)]
        ps_w = sc.ps("ps_w", [P, 512])
        ps_b = sc.ps("ps_b", [P, 512])
        ps_x = sc.ps("ps_x", [P, 2, 512])
        ps_r = sc.ps("ps_r", [P, 2, 512])
        (loaded, b_mm, b_sb, w_mm, w_hi, w_lo, r_mm, r_sb, ones, m_hi) = (
            sc.sem(n) for n in "loaded b_mm b_sb w_mm w_hi w_lo r_mm r_sb ones m_hi".split())
        x_mm, x_sb = sc.steps("x_mm x_sb")
        with nc.Block() as block:
            @block.sync
            def _(sp):
                sp.dma_start(tw.hd[:, :], tw.head_weights).then_inc(loaded, 16)
                sp.wait_ge(loaded, 16)

            @block.tensor
            def _(pe):
                prime(pe, [x_mm])
                pe.wait_ge(loaded, 16)
                for n in range(NH):
                    bias = tw.hw("hl_b", lo=P * n, n=P)
                    for m, lo, cols in ((0, 0, 96), (1, 96, 96), (2, 192, 98)):
                        nc.tensor.matmul(ps_b[0:cols, 3 * n + m:3 * n + m + 1], tw.hw("proj", lo=322 * n + lo, n=cols),
                                         bias[:, 0:1], start=True, stop=True)
                    last = nc.tensor.matmul(ps_b[:, 128 + 32 * n:160 + 32 * n], bias,
                                            tw.hw("proj", lo=322 * n + 290, n=32), start=True, stop=True)
                last.then_inc(b_mm, 1)
                for n in range(NH):
                    if n:
                        pe.wait_ge(w_lo, n)
                    nc.tensor.matmul(ps_w[:, 0:322], tw.hw("hl_w", lo=P * n, n=P),
                                     tw.hw("proj", rows=DH, lo=322 * n, n=322), start=True, stop=True
                                     ).then_inc(w_mm, 1)
                pe.wait_ge(ones, 1)
                for n in range(NH):
                    pe.wait_ge(x_sb.sem, x_sb.before(n, 2))
                    ln.transpose(pe, n, n, ps_x[:, n % 2], x_mm)
                for n in range(NH):
                    pe.wait_ge(x_sb.sem, x_sb.now(n))
                    if n >= 2:
                        pe.wait_ge(r_sb, n - 1)
                    for t in range(NT):
                        last = nc.tensor.matmul(ps_r[:, n % 2, DH * t:DH * t + DH], xT[n][:, P * t:P * t + P],
                                                tw.hw("hlres", lo=DH * n, n=DH), start=True, stop=True)
                    last.then_inc(r_mm, 1)

            @block.scalar
            def _(act):
                prime(act, [ln.sqr, x_sb])
                for n in range(NH):
                    ln.square(act, n, n)
                act.wait_ge(loaded, 16)
                nc.scalar.copy(wm[0][:, :, :], tw.hw("hlmask").rearrange("p (n m) -> p n m", m=P)).then_inc(m_hi, 1)
                act.wait_ge(b_mm, 1)
                nc.scalar.copy(wb[0:96, :, :], ps_b[0:96, 0:3 * NH].rearrange("p (n m) -> p n m", m=3))
                nc.scalar.copy(wb[96:98, :, 2:3], ps_b[96:98, 0:3 * NH].rearrange("p (n m) -> p n m", m=3)[:, :, 2:3])
                nc.scalar.copy(v_bias[:, :, :], ps_b[:, 128:256].rearrange("p (n f) -> p n f", f=32)).then_inc(b_sb, 1)
                for n in range(NH):
                    act.wait_ge(w_mm, n + 1)
                    nc.scalar.copy(wx[0][:, n, :], ps_w[:, 0:322]).then_inc(w_hi, 1)
                for n in range(NH):
                    act.wait_ge(x_mm.sem, x_mm.now(n))
                    ln.features(act, xT[n], ps_x[:, n % 2], x_sb)

            @block.vector
            def _(dve):
                prime(dve, ln.dve_steps)
                for n in range(NH):
                    ln.center(dve, n, n, ln.out)
                for n in range(NH):
                    ln.variance(dve, n, n)
                for n in range(NH):
                    last = nc.vector.memset(xT[n][64:65, :], 1.0)
                last.then_inc(ones, 1)
                for n in range(NH):
                    ln.scale(dve, n, n)
                dve.wait_ge(m_hi, 1)
                nc.vector.tensor_tensor(wm[1][:, :, :], tw.hw("hlmask").rearrange("p (n m) -> p n m", m=P),
                                        wm[0][:, :, :], ALU.subtract)
                nc.vector.tensor_scalar(no_feature[:, :], tw.hw("hlmask_b"), -1.0, None, ALU.mult)
                for n in range(NH):
                    dve.wait_ge(w_hi, n + 1)
                    nc.vector.tensor_tensor(wx[1][:, n, :], ps_w[:, 0:322], wx[0][:, n, :], ALU.subtract
                                            ).then_inc(w_lo, 1)
                for n in range(NH):
                    dve.wait_ge(r_mm, n + 1)
                    nc.vector.tensor_copy(resid[:, n], ps_r[:, n % 2, 0:NT * DH].rearrange("p (t f) -> p t f", f=DH)
                                          ).then_inc(r_sb, 1)

            @block.gpsimd
            def _(pool):
                prime(pool, [ln.rstd])
                for n in range(NH):
                    ln.inverse_root(pool, n, n)


def causal_heads(st, ln, xn2, wx, wm, wb, v_bias, no_feature, resid, out):
    nc, tw = st.nc, st.tw
    xs = st.sb("xs", [P, S], F32R)
    q_in = [[st.sb(f"q{n}{j}", [98, S], F32R) for j in range(2)] for n in range(NH)]
    k_in = [[st.sb(f"k{n}{e}", [98, S], F32R) for e in range(2)] for n in range(NH)]
    live = [st.sb(f"live{n}", [P, S], BF16) for n in range(NH)]
    v = st.sb("v", [P, NT, NH, 32])
    neg_max = st.sb("neg_max", [P, 2, NE, NT])
    m_cols = st.sb("m_cols", [P, 4, 2, 64], F32R)
    ident_r = st.sb("ident_r", [P, P], F32R)
    probs = st.sb("probs", [P, 3, NE, 512])
    oT = st.sb("oT", [P, 2, 512])
    r = st.sb("r", [P, 2, NT, 84])
    ident_b = st.sb("ident_b", [P, P], BF16)
    mask_q = st.sb("mask_q", [P, P], BF16)
    mask_k = st.sb("mask_k", [P, P], BF16)
    tri = st.sb("tri", [P, P])
    inv = st.sb("inv", [P, NT, NE])
    gl = st.sb("gl", [P, NT, NE, NE])
    lg = st.sb("lg", [P, 3, NT, NE])
    gz = st.sb("gz", [P, 3, NT])
    cf = st.sb("cf", [P, 2, NT, NE])
    weighed = st.sb("weighed", [P, NT, NE, DH])
    mix = st.sb("mix", [P, NT, NH, DH])
    t_stat = st.sb("t_stat", [P, 2, 4, NT * NH])
    t_half = st.sb("t_half", [P, NT * NH])
    t_c = st.sb("t_c", [P, NT, D])
    t_sq = st.sb("t_sq", [P, NT, D])
    fx = st.sb("fx", [P, NT, D])
    y = st.sb("y", [P, NT, D])
    fT = st.sb("fT", [64, S])
    hx = st.sb("hx", [65, S])
    fg = st.sb("fg", [P, 3, NT, NH])
    fz = st.sb("fz", [P, 2, NT])
    o = st.sb("o", [P, NT, D])
    ring = [st.ps(f"ring{i}", [P, 2, 512]) for i in range(3)]
    ps_o = st.ps("ps_o", [P, 512])
    ps_m = st.ps("ps_m", [P, 512])

    early_banks = [ps_m[:, :]] + [ring[i][:, j, :] for i in range(3) for j in range(2)]
    early_items = [(g, kind, j) for g in range(2) for kind, j in
                   [("k", 0), ("k", 1), ("q", 0), ("q", 1), ("q", 2), ("q", 3), ("mask", 0), ("mask", 1)]]

    names = ("x_mm x_hi x_lo s1_mm s2_mm pv_mm k_mm q_mm mask_mm m_mm r_mm v_mm fxT_mm f1_mm f2_mm foT_mm fg_mm "
             "s1_max k_lo q_lo mask_sb m_cols o_sb y_sb fg_sub "
             "s2_exp k_hi q_hi m_sb r_sb v_sb fxT_sb f1_sb foT_sb "
             "k_in0 k_in1 k_one stored consts_v consts_p n_tri "
             "g_inv g_mul g_sum g_bias g_max g_sub g_exp g_z g_rz g_cf g_cfz g_w g_mix g_res "
             "n_sum n_mean n_cent n_sq n_var n_eps n_root n_out n_g n_b f1_live y_add "
             "z_max z_sum z_rec z_exp z_w z_o z_add")
    s = {name: st.sem(name) for name in names.split()}

    def wait(engine, name, value):
        if isinstance(value, int) and value <= 0:
            return
        engine.wait_ge(s[name], value)

    def heads(tile):
        return tile[:, :, :].rearrange("p t (n f) -> p (t n) f", f=DH)

    def read(engine, n, b, item):
        kind, j = item
        g = NH * b + n
        if kind == "m":
            wait(engine, "m_sb", 2 * (g + 1) + (0 if j else 1))
        elif kind == "r":
            wait(engine, "r_sb", 2 * (g if j else g + 1) - (0 if j else 1))
        elif kind == "k":
            wait(engine, "k_lo", 2 * (g + 2) + j + 1)
        elif kind == "q":
            wait(engine, "q_lo", 4 * (g + 2) + j + 1)
        elif kind == "mask":
            wait(engine, "mask_sb", 2 * (g + 2) + j + 1)
        elif kind == "v":
            wait(engine, "v_sb", 2 * b + j + 1)
        elif kind == "x":
            wait(engine, "x_lo", 2 * (b + 1) + j + 1)
        elif kind == "fxT":
            wait(engine, "fxT_sb", b)
        elif kind == "f1":
            wait(engine, "f1_sb", 2 * (b - 1) + j + 1)
        elif kind == "f2":
            wait(engine, "y_sb", b)
        elif kind == "foT":
            wait(engine, "foT_sb", b)
        elif kind == "fg":
            wait(engine, "fg_sub", b)

    with nc.Block() as block:
        @block.sync
        def _(sp):
            wait(sp, "consts_v", 1)
            for n in range(NH):
                sp.dma_start(k_in[n][1][97:98, :].bitcast(F32), hx[64:65, :]).then_inc(s["k_one"], 16)
            wait(sp, "k_one", 16 * NH)

            def second_keys(g, n):
                wait(sp, "k_lo", 2 * (g + 1))
                sp.dma_start(k_in[n][1][16:96, :].bitcast(F32), k_in[n][0][0:80, :].bitcast(F32)
                             ).then_inc(s[f"k_in{n % 2}"], 16)

            def results(b):
                wait(sp, "z_add", b + 1)
                sp.dma_start(out[bass.ds(b, 1)].rearrange("a (t p) f -> p (a t) f", p=P), o[:, :, :]
                             ).then_inc(s["stored"], 16)

            second_keys(0, 0)
            second_keys(1, 1)

            def body(b, first, last):
                for n in range(NH):
                    g = NH * b + n
                    items = items_of(n, first, last)
                    for p in sorted(items):
                        if items[p] == ("k", 1):
                            second_keys(g + 2, (n + 2) % NH)
                if not first:
                    results(b - 1)

            body(0, True, False)
            with sp.Fori(1, B - 1) as b:
                body(b, False, False)
            body(B - 1, False, True)
            results(B - 1)
            wait(sp, "stored", 16 * B)

        @block.tensor
        def _(pe):
            def query_tile(g, n, p):
                (qb, c), j = QUERY_STEPS[p // 2], p % 2
                w = min(512, P * (qb + 1) - 512 * c)
                slot = ring[(2 * p + 1) % 3]
                diagonal = P * qb < 512 * c + w
                for e in range(2):
                    last = nc.tensor.matmul(slot[:, e, 0:w], q_in[n][j][0:96, P * qb:P * qb + P],
                                            k_in[n][e][0:96, 512 * c:512 * c + w], start=True, stop=not diagonal)
                if diagonal:
                    for e in range(2):
                        last = nc.tensor.matmul(slot[:, e, w - P:w], ident_b[:, :], mask_q[:, :],
                                                start=False, stop=True)
                last.then_inc(s["s1_mm"], 1)

            def key_tile(g, n, p):
                (c, kb), j = KEY_STEPS[p // 2], p % 2
                q0 = max(512 * c, P * kb)
                w = 512 * (c + 1) - q0
                slot = ring[(2 * p) % 3]
                diagonal = q0 == P * kb
                for e in range(2):
                    last = nc.tensor.matmul(slot[:, e, 0:w], k_in[n][e][:, P * kb:P * kb + P],
                                            q_in[n][j][:, q0:q0 + w], start=True, stop=not diagonal)
                if diagonal:
                    for e in range(2):
                        last = nc.tensor.matmul(slot[:, e, 0:P], ident_b[:, :], mask_k[:, :],
                                                start=False, stop=True)
                last.then_inc(s["s2_mm"], 1)

            def values(g, n, step):
                c, kb = KEY_STEPS[step]
                q0 = max(512 * c, P * kb)
                w = 512 * (c + 1) - q0
                wait(pe, "s2_exp", NTILE * g + 2 * step + 2)
                if kb == 0:
                    wait(pe, "o_sb", 2 * g + c)
                for e in range(NE):
                    last = nc.tensor.matmul(ps_o[32 * e:32 * e + 32, q0 - 512 * c:512], v[:, kb, n, :],
                                            probs[:, step % 3, e, 0:w], start=kb == 0, stop=step in (3, NSTEP - 1),
                                            tile_position=(0, 32 * e))
                last.then_inc(s["pv_mm"], 1)

            def project(kind, g, n, j, bank=ps_m):
                c = j % 2
                if kind == "k":
                    w, rows, done = [x[:, n, 192:290] for x in wx], 98, "k_mm"
                elif kind == "q":
                    w, rows, done = [x[:, n, 96 * (j // 2):96 * (j // 2) + 96] for x in wx], 96, "q_mm"
                else:
                    w, rows, done = [x[:, n, :] for x in wm], P, "mask_mm"
                for k in range(2):
                    last = nc.tensor.matmul(bank[0:rows, :], w[k], xs[:, 512 * c:512 * c + 512],
                                            start=k == 0, stop=k == 1)
                last.then_inc(s[done], 1)

            def maxima(g, half):
                wait(pe, "m_cols", 2 * g + half + 1)
                for t in range(4):
                    last = nc.tensor.matmul(ps_m[0:66, P * t:P * t + P],
                                            m_cols[:, t].rearrange("p j c -> p (j c)")[:, 0:66], ident_r[:, :],
                                            start=True, stop=True)
                last.then_inc(s["m_mm"], 1)

            def token_rows(g, n, c):
                wait(pe, "o_sb", 2 * g + c + 1)
                for t in range(4):
                    last = nc.tensor.matmul(ps_m[:, 84 * t:84 * t + 84], oT[:, c, P * t:P * t + P],
                                            tw.fw("gate", lo=84 * n, n=84), start=True, stop=True)
                last.then_inc(s["r_mm"], 1)

            def turn(src, done):
                for t in range(NT // 2):
                    last = nc.tensor.transpose(ps_m[:, P * t:P * t + P], src[:, 2 * t:2 * t + 2, :], tw.ct("ident"))
                last.then_inc(s[done], 1)

            def tail(kind, b, j):
                if kind == "fxT":
                    wait(pe, "n_b", 2 * b + 1)
                    turn(fx, "fxT_mm")
                elif kind == "f1":
                    wait(pe, "fxT_sb", b + 1)
                    nc.tensor.matmul(ps_m[:, :], tw.fw("fc1"), fT[:, 512 * j:512 * j + 512],
                                     start=True, stop=True).then_inc(s["f1_mm"], 1)
                elif kind == "f2":
                    wait(pe, "f1_live", b + 1)
                    for t in range(NT):
                        last = nc.tensor.matmul(ps_m[:, D * t:D * t + D], hx[:, P * t:P * t + P], tw.fw("fc2"),
                                                start=True, stop=True)
                    last.then_inc(s["f2_mm"], 1)
                elif kind == "foT":
                    wait(pe, "n_b", 2 * b + 2)
                    turn(y, "foT_mm")
                else:
                    wait(pe, "foT_sb", b + 1)
                    for t in range(NT):
                        last = nc.tensor.matmul(ps_m[:, NH * t:NH * t + NH], fT[:, P * t:P * t + P],
                                                tw.fw("fgate"), start=True, stop=True)
                    last.then_inc(s["fg_mm"], 1)

            def image_features(b, j):
                pe.wait_ge(ln.out.sem, ln.out.now(b))
                for t in range(4):
                    last = nc.tensor.transpose(ps_m[:, P * t:P * t + P], xn2[:, 4 * j + t], tw.ct("ident"))
                last.then_inc(s["x_mm"], 1)

            def small(b, n, item):
                kind, j = item
                g = NH * b + n
                if kind in ("k", "q", "mask"):
                    if kind == "k" and n == 2:
                        wait(pe, "x_lo", 2 * (b + 1) + j + 1)
                    project(kind, g + 2, (n + 2) % NH, j)
                elif kind == "m":
                    maxima(g if j else g + 1, j)
                elif kind == "r":
                    token_rows(g - 1 if j else g, (n - 1) % NH if j else n, j)
                elif kind == "v":
                    for t in range(4):
                        for k in range(2):
                            last = nc.tensor.matmul(ps_m[:, P * t:P * t + P],
                                                    xs[:, P * (4 * j + t):P * (4 * j + t) + P],
                                                    wx[k][:, :, 290:322], start=k == 0, stop=k == 1)
                    last.then_inc(s["v_mm"], 1)
                elif kind == "x":
                    image_features(b + 1, j)
                else:
                    tail(kind, b - 1, j)

            wait(pe, "consts_v", 1)
            wait(pe, "consts_p", 1)
            wait(pe, "k_one", 16 * NH)
            image_features(0, 0)
            wait(pe, "x_lo", 1)
            image_features(0, 1)
            wait(pe, "x_lo", 2)
            for i, (g, kind, j) in enumerate(early_items):
                if i >= len(early_banks):
                    before = early_items[i - len(early_banks)]
                    read(pe, before[0] - 2, 0, before[1:])
                project(kind, g, g, j, early_banks[i % len(early_banks)])
            for g, kind, j in early_items[-len(early_banks):]:
                read(pe, g - 2, 0, (kind, j))
            wait(pe, "k_in0", 16)
            for p in range(NTILE):
                wait(pe, "s1_max", p - 2)
                query_tile(0, 0, p)
            maxima(0, 0)
            prev = (-1, 0, ("m", 0))

            def body(b, first, last, prev):
                for n in range(NH):
                    g = NH * b + n
                    items = items_of(n, first, last)
                    more = not (last and n == NH - 1)
                    for p in range(NTILE):
                        if p == 0:
                            wait(pe, "m_sb", 2 * g + 1)
                        elif p == 8:
                            wait(pe, "m_sb", 2 * g + 2)
                        if more:
                            wait(pe, "s1_max", NTILE * (g + 1) + p - 1)
                        else:
                            if p < 2:
                                wait(pe, "s1_max", NTILE * (g + 1) + p - 1 if p == 0 else NTILE * (g + 1))
                            wait(pe, "s2_exp", NTILE * g + max(p - 2, 0))
                        key_tile(g, n, p)
                        if more:
                            if p == 0:
                                wait(pe, f"k_in{(n + 1) % 2}", 16 * (2 * b + (n + 1) // 2 + 1))
                                wait(pe, "q_lo", 4 * (g + 2))
                            wait(pe, "s2_exp", NTILE * g + p)
                            query_tile(g + 1, (n + 1) % NH, p)
                        if p % 2 == 0:
                            if p > 0:
                                if n == 0 and p == 2:
                                    wait(pe, "v_sb", 2 * b + 1)
                                if n == 0 and p == 18:
                                    wait(pe, "v_sb", 2 * b + 2)
                                values(g, n, p // 2 - 1)
                            elif not (first and n == 0):
                                values(g - 1, (n - 1) % NH, NSTEP - 1)
                        if p in items:
                            read(pe, *prev)
                            small(b, n, items[p])
                            prev = (n, b, items[p])
                return prev

            body(0, True, False, prev)
            with pe.Fori(1, B - 1) as b:
                body(b, False, False, (NH - 1, b - 1, ("mask", 1)))
            prev = body(B - 1, False, True, (NH - 1, B - 2, ("mask", 1)))
            g = NH * B - 1
            values(g, NH - 1, NSTEP - 1)
            for item in [("r", 1), ("fxT", 0), ("f1", 0), ("f1", 1), ("f2", 0), ("foT", 0), ("fg", 0)]:
                read(pe, *prev)
                small(B, 0, item)
                prev = (0, B, item)

        @block.scalar
        def _(act):
            def probabilities(g, p):
                (c, kb), j, step = KEY_STEPS[p // 2], p % 2, p // 2
                w = 512 * (c + 1) - max(512 * c, P * kb)
                wait(act, "s2_mm", NTILE * g + p + 1)
                if j == 0:
                    wait(act, "pv_mm", NSTEP * g + step - 2)
                nc.scalar.activation(probs[:, step % 3, 2 * j:2 * j + 2, 0:w], ring[(2 * p) % 3][:, :, 0:w], ACT.Exp,
                                     scale=float(DH) ** 0.5).then_inc(s["s2_exp"], 1)

            def high(kind, g, n, j, bank=ps_m):
                cols = slice(512 * (j % 2), 512 * (j % 2) + 512)
                if kind == "k":
                    wait(act, "k_mm", 2 * g + j + 1)
                    nc.scalar.activation(k_in[n][0][:, cols], bank[0:98, :], ACT.Identity, bias=wb[:, n, 2:3]
                                         ).then_inc(s["k_hi"], 1)
                else:
                    wait(act, "q_mm", 4 * g + j + 1)
                    nc.scalar.activation(q_in[n][j // 2][0:96, cols], bank[0:96, :], ACT.Identity,
                                         bias=wb[0:96, n, j // 2:j // 2 + 1]).then_inc(s["q_hi"], 1)

            def maxima(g, n, half):
                wait(act, "m_mm", 2 * g + half + 1)
                for j in range(2):
                    last = nc.scalar.copy(q_in[n][j][96:98, 512 * half:512 * half + 512], ps_m[64 * j:64 * j + 2, :])
                last.then_inc(s["m_sb"], 1)

            def token_rows(g, n, c):
                wait(act, "r_mm", 2 * g + c + 1)
                wait(act, "g_w", g - 1)
                nc.scalar.copy(r[:, n % 2, 4 * c:4 * c + 4, :], ps_m[:, 0:336].rearrange("p (t f) -> p t f", f=84)
                               ).then_inc(s["r_sb"], 1)

            def gate_exp(g):
                wait(act, "g_sub", g + 1)
                nc.scalar.activation(lg[:, 2], lg[:, 1], ACT.Exp).then_inc(s["g_exp"], 1)

            def turned(name, b):
                wait(act, name + "_mm", b + 1)
                for par in range(2):
                    last = nc.scalar.copy(fT[:, :].rearrange("p (t e n) -> p e t n", e=2, n=P)[:, par],
                                          ps_m[D * par:D * par + D, :].rearrange("p (t n) -> p t n", n=P))
                last.then_inc(s[name + "_sb"], 1)

            def hidden(b, j):
                wait(act, "f1_mm", 2 * b + j + 1)
                nc.scalar.activation(hx[0:64, 512 * j:512 * j + 512], ps_m[0:64, :], ACT.Relu,
                                     bias=tw.fw("fc1_b")).then_inc(s["f1_sb"], 1)

            def head_gate_exp(b):
                wait(act, "fg_sub", b + 1)
                nc.scalar.activation(fg[:, 1], fg[:, 0], ACT.Exp).then_inc(s["z_exp"], 1)

            def image_features(b, j):
                wait(act, "x_mm", 2 * b + j + 1)
                nc.scalar.copy(xs[:, 512 * j:512 * j + 512], ps_m[:, :]).then_inc(s["x_hi"], 1)

            def small(b, n, item):
                kind, j = item
                g = NH * b + n
                if kind in ("k", "q"):
                    high(kind, g + 2, (n + 2) % NH, j)
                elif kind == "m":
                    maxima(g if j else g + 1, n if j else (n + 1) % NH, j)
                elif kind == "r":
                    token_rows(g - 1 if j else g, (n - 1) % NH if j else n, j)
                elif kind == "x":
                    image_features(b + 1, j)
                elif kind in ("fxT", "foT"):
                    turned(kind, b - 1)
                elif kind == "f1":
                    hidden(b - 1, j)

            prime(act, [ln.sqr])
            ln.square(act, 0, 0)
            image_features(0, 0)
            image_features(0, 1)
            for i, (g, kind, j) in enumerate(early_items):
                if kind != "mask":
                    high(kind, g, g, j, early_banks[i % len(early_banks)])
            maxima(0, 0, 0)

            def body(b, first, last):
                for n in range(NH):
                    g = NH * b + n
                    items = items_of(n, first, last)
                    for p in range(NTILE):
                        probabilities(g, p)
                        if p in items:
                            small(b, n, items[p])
                        if p == 16 and not (first and n == 0):
                            gate_exp(g - 1)
                        if n == 0 and p == 5 and not last:
                            ln.square(act, b + 1, 0)
                        if n == 3 and p == 22 and not first:
                            head_gate_exp(b - 1)

            body(0, True, False)
            with act.Fori(1, B - 1) as b:
                body(b, False, False)
            body(B - 1, False, True)
            token_rows(NH * B - 1, NH - 1, 1)
            gate_exp(NH * B - 1)
            turned("fxT", B - 1)
            hidden(B - 1, 0)
            hidden(B - 1, 1)
            turned("foT", B - 1)
            head_gate_exp(B - 1)

        @block.vector
        def _(dve):
            def then(name, count, op):
                op.then_inc(s[name], 1)
                wait(dve, name, count)

            def maximum(g, p):
                (qb, c), j = QUERY_STEPS[p // 2], p % 2
                w = min(512, P * (qb + 1) - 512 * c)
                wait(dve, "s1_mm", NTILE * g + p + 1)
                nc.vector.tensor_reduce(neg_max[:, c, 2 * j:2 * j + 2, qb], ring[(2 * p + 1) % 3][:, :, 0:w],
                                        axis=AX_X, op=ALU.max, negate=True).then_inc(s["s1_max"], 1)

            def columns_of(x):
                return x.rearrange("p (j e) t -> p t j e", e=2)

            def early_maxima(g):
                wait(dve, "s1_max", NTILE * g + EARLY)
                wait(dve, "m_mm", 2 * g)
                nc.vector.tensor_copy(m_cols[:, :, :, 0:2], columns_of(neg_max[:, 0, :, 0:4])).then_inc(s["m_cols"], 1)

            def late_maxima(g):
                wait(dve, "s1_max", NTILE * (g + 1))
                wait(dve, "m_mm", 2 * g + 1)
                nc.vector.tensor_tensor(m_cols[:, :, :, 0:2], columns_of(neg_max[:, 0, :, 4:8]),
                                        columns_of(neg_max[:, 1, :, 4:8]), ALU.min).then_inc(s["m_cols"], 1)

            def outputs(g, n, c):
                wait(dve, "pv_mm", NSTEP * g + (4 if c == 0 else NSTEP))
                wait(dve, "r_mm", 2 * (g - 1) + c + 1)
                nc.vector.tensor_tensor(oT[:, c, :], ps_o[:, :], live[n][:, 512 * c:512 * c + 512],
                                        ALU.mult).then_inc(s["o_sb"], 1)

            def rest(kind, g, n, j, bank=ps_m):
                cols = slice(512 * (j % 2), 512 * (j % 2) + 512)
                if kind == "k":
                    wait(dve, "k_hi", 2 * g + j + 1)
                    part = k_in[n][0][64:96, cols]
                    nc.vector.scalar_tensor_tensor(part, bank[64:96, :], wb[64:96, n, 2:3], part, ALU.add,
                                                   ALU.subtract).then_inc(s["k_lo"], 1)
                elif kind == "q":
                    wait(dve, "q_hi", 4 * g + j + 1)
                    part = q_in[n][j // 2][32:64, cols]
                    nc.vector.scalar_tensor_tensor(part, bank[32:64, :], wb[32:64, n, j // 2:j // 2 + 1], part, ALU.add,
                                                   ALU.subtract).then_inc(s["q_lo"], 1)
                else:
                    wait(dve, "mask_mm", 2 * g + j + 1)
                    nc.vector.tensor_scalar(live[n][:, cols], bank[:, :], no_feature[:, n:n + 1], None, ALU.not_equal
                                            ).then_inc(s["mask_sb"], 1)

            def rest_of_features(b, j):
                wait(dve, "x_hi", 2 * b + j + 1)
                part = xs[64:128, 512 * j:512 * j + 512]
                nc.vector.tensor_tensor(part, ps_m[64:128, :], part, ALU.subtract).then_inc(s["x_lo"], 1)

            def gate_inverse(g, n):
                wait(dve, "r_sb", 2 * g + 2)
                nc.vector.reciprocal(inv[:, :, :], r[:, n % 2, :, 64:68]).then_inc(s["g_inv"], 1)

            def gate_step(g, n, k):
                if k == 0:
                    wait(dve, "g_mul", g + 1)
                    nc.vector.reduce_sum(lg[:, 0], gl[:, :, :, :], axis=AX_X).then_inc(s["g_sum"], 1)
                elif k == 1:
                    wait(dve, "g_sum", g + 1)
                    bias = tw.fw("gate_b", lo=NE * n, n=NE).unsqueeze(1).to_broadcast([P, NT, NE])
                    nc.vector.tensor_tensor(lg[:, 0], lg[:, 0], bias, ALU.add).then_inc(s["g_bias"], 1)
                elif k == 2:
                    wait(dve, "g_bias", g + 1)
                    nc.vector.reduce_max(gz[:, 0, :], lg[:, 0], axis=AX_X).then_inc(s["g_max"], 1)
                elif k == 3:
                    wait(dve, "g_max", g + 1)
                    nc.vector.tensor_tensor(lg[:, 1], lg[:, 0], bc(gz[:, 0, :], NE), ALU.subtract
                                            ).then_inc(s["g_sub"], 1)
                elif k == 4:
                    wait(dve, "g_exp", g + 1)
                    nc.vector.reduce_sum(gz[:, 1, :], lg[:, 2], axis=AX_X).then_inc(s["g_z"], 1)
                else:
                    wait(dve, "g_z", g + 1)
                    nc.vector.reciprocal(gz[:, 2, :], gz[:, 1, :]).then_inc(s["g_rz"], 1)

            def gate_mix(g, n, b):
                wait(dve, "g_w", g + 1)
                if n == 0:
                    wait(dve, "n_cent", 2 * b - 1)
                nc.vector.reduce_sum(mix[:, :, n, :], weighed[:, :, :, :].rearrange("p t e f -> p t f e"),
                                     axis=AX_X).then_inc(s["g_mix"], 1)

            def norm_step(src, k, step):
                if step == 0:
                    nc.vector.reduce_sum(t_stat[:, 0, 0, :], src, axis=AX_X).then_inc(s["n_sum"], 1)
                elif step == 1:
                    wait(dve, "n_sum", k + 1)
                    nc.vector.tensor_scalar(t_stat[:, 0, 1, :], t_stat[:, 0, 0, :], 1.0 / DH, None, ALU.mult
                                            ).then_inc(s["n_mean"], 1)
                elif step == 2:
                    wait(dve, "n_sq", k + 1)
                    nc.vector.reduce_sum(t_stat[:, 1, 0, :], heads(t_sq), axis=AX_X).then_inc(s["n_var"], 1)
                else:
                    wait(dve, "n_var", k + 1)
                    nc.vector.tensor_scalar(t_stat[:, 1, 1, :], t_stat[:, 1, 0, :], 1.0 / DH, 1e-8, ALU.mult,
                                            ALU.add).then_inc(s["n_eps"], 1)

            def live_hidden(b):
                wait(dve, "f1_sb", 2 * b + 2)
                nc.vector.scalar_tensor_tensor(hx[0:64, :], fT[:, :], 0.0, hx[0:64, :], ALU.not_equal,
                                               ALU.mult).then_inc(s["f1_live"], 1)

            def live_out(b):
                wait(dve, "f2_mm", b + 1)
                wait(dve, "z_o", b)
                nc.vector.scalar_tensor_tensor(y[:, :, :].rearrange("p t f -> p (t f)"),
                                               fx[:, :, :].rearrange("p t f -> p (t f)"), 0.0, ps_m[:, :],
                                               ALU.not_equal, ALU.mult).then_inc(s["y_sb"], 1)

            def head_gate(b):
                wait(dve, "fg_mm", b + 1)
                logits = ps_m[:, 0:NT * NH].rearrange("p (t n) -> p t n", n=NH)
                then("z_max", b + 1, nc.vector.reduce_max(fz[:, 0, :], logits, axis=AX_X))
                nc.vector.tensor_tensor(fg[:, 0], logits, bc(fz[:, 0, :], NH), ALU.subtract).then_inc(s["fg_sub"], 1)

            def head_gate_norm(b):
                wait(dve, "z_exp", b + 1)
                then("z_sum", b + 1, nc.vector.reduce_sum(fz[:, 0, :], fg[:, 1], axis=AX_X))
                nc.vector.reciprocal(fz[:, 1, :], fz[:, 0, :]).then_inc(s["z_rec"], 1)

            def small(b, n, item):
                kind, j = item
                if kind in ("k", "q", "mask"):
                    rest(kind, NH * b + n + 2, (n + 2) % NH, j)
                elif kind == "x":
                    rest_of_features(b + 1, j)
                elif kind == "v":
                    wait(dve, "v_mm", 2 * b + j + 1)
                    nc.vector.tensor_tensor(
                        v[:, 4 * j:4 * j + 4, :, :], ps_m[:, :].rearrange("p (t n f) -> p t n f", n=NH, f=32),
                        v_bias[:, :, :].unsqueeze(1).to_broadcast([P, 4, NH, 32]), ALU.add).then_inc(s["v_sb"], 1)
                elif kind == "f2":
                    live_out(b - 1)
                elif kind == "fg":
                    head_gate(b - 1)

            prime(dve, ln.dve_steps[:-1])
            ln.center(dve, 0, 0, ln.out, b=0)
            mixed = mix[:, :, :, :].rearrange("p t n f -> p (t n) f")
            for n in range(NH):
                nc.vector.memset(k_in[n][1][:, :].bitcast(F32), 0.0)
            nc.vector.memset(t_half[:, :], -0.5)
            nc.vector.memset(hx[64:65, :], 1.0)
            nc.vector.memset(m_cols[:, :, :, :].bitcast(F32), 0.0)
            nc.vector.tensor_copy(ident_r[:, :], tw.ct("ident"))
            nc.vector.tensor_copy(ident_b[:, :], tw.ct("ident")).then_inc(s["consts_v"], 1)
            ln.variance(dve, 0, 0)
            rest_of_features(0, 0)
            rest_of_features(0, 1)
            for i, (g, kind, j) in enumerate(early_items):
                rest(kind, g, g, j, early_banks[i % len(early_banks)])
            for p in range(NTILE):
                maximum(0, p)
            early_maxima(0)
            late_maxima(0)

            def body(b, first, last):
                for n in range(NH):
                    g = NH * b + n
                    head_before = not (first and n == 0)
                    items = items_of(n, first, last)
                    more = not (last and n == NH - 1)
                    for p in range(NTILE):
                        if more:
                            maximum(g + 1, p)
                        if p == 8:
                            outputs(g, n, 0)
                        if p == EARLY and more:
                            early_maxima(g + 1)
                        if p in items:
                            small(b, n, items[p])
                        if p == 0 and head_before:
                            outputs(g - 1, (n - 1) % NH, 1)
                        if head_before:
                            if p == 6:
                                gate_inverse(g - 1, (n - 1) % NH)
                            elif p in GATE_AT:
                                gate_step(g - 1, (n - 1) % NH, GATE_AT.index(p))
                            elif p == 22:
                                gate_mix(g - 1, (n - 1) % NH, b)
                        if n == 0 and not last:
                            if p == 2:
                                ln.center(dve, b + 1, 0, ln.out, b=b + 1)
                            elif p == 8:
                                ln.variance(dve, b + 1, 0)
                        if not first:
                            if n == 1 and p in MIXED_AT:
                                if p == MIXED_AT[0]:
                                    wait(dve, "g_res", NH * b)
                                norm_step(mixed, 2 * (b - 1), MIXED_AT.index(p))
                            elif (n, p) == (2, 22):
                                live_hidden(b - 1)
                            elif n == 3 and p in OUT_AT:
                                if p == OUT_AT[0]:
                                    wait(dve, "y_add", b)
                                norm_step(heads(y), 2 * (b - 1) + 1, OUT_AT.index(p))
                            elif (n, p) == (3, 23):
                                head_gate_norm(b - 1)
                    if more:
                        late_maxima(g + 1)

            body(0, True, False)
            with dve.Fori(1, B - 1) as b:
                body(b, False, False)
            body(B - 1, False, True)
            g, b = NH * B - 1, B - 1
            outputs(g, NH - 1, 1)
            gate_inverse(g, NH - 1)
            for k in range(len(GATE_AT)):
                gate_step(g, NH - 1, k)
            gate_mix(g, NH - 1, b)
            wait(dve, "g_res", NH * B)
            for k in range(4):
                norm_step(mixed, 2 * b, k)
            live_hidden(b)
            live_out(b)
            wait(dve, "y_add", B)
            for k in range(4):
                norm_step(heads(y), 2 * b + 1, k)
            head_gate(b)
            head_gate_norm(b)

        @block.gpsimd
        def _(pool):
            def then(name, count, op):
                op.then_inc(s[name], 1)
                wait(pool, name, count)

            def normalise(b):
                ln.inverse_root(pool, b, 0)
                wait(pool, "x_mm", 2 * b)
                ln.scale_twice(pool, b, 0, xn2)

            def gate_products(g, n):
                wait(pool, "g_inv", g + 1)
                nc.gpsimd.tensor_tensor(
                    gl[:, :, :, :], r[:, n % 2, :, 68:84].rearrange("p t (e f) -> p t e f", f=NE),
                    inv[:, :, :].unsqueeze(2).to_broadcast([P, NT, NE, NE]), ALU.mult).then_inc(s["g_mul"], 1)

            def gate_weights(g, n):
                wait(pool, "g_exp", g + 1)
                then("g_cf", g + 1, nc.gpsimd.tensor_tensor(cf[:, 0], lg[:, 2], inv[:, :, :], ALU.mult))
                wait(pool, "g_rz", g + 1)
                then("g_cfz", g + 1, nc.gpsimd.tensor_tensor(cf[:, 1], cf[:, 0], bc(gz[:, 2, :], NE), ALU.mult))
                nc.gpsimd.tensor_tensor(
                    weighed[:, :, :, :], r[:, n % 2, :, 0:64].rearrange("p t (e f) -> p t e f", f=DH),
                    cf[:, 1].unsqueeze(3).to_broadcast([P, NT, NE, DH]), ALU.mult).then_inc(s["g_w"], 1)

            def gate_residual(g, n):
                wait(pool, "g_mix", g + 1)
                nc.gpsimd.tensor_tensor(mix[:, :, n, :], mix[:, :, n, :], resid[:, n], ALU.add).then_inc(s["g_res"], 1)

            def norm(src, dst, gain, bias, k, ready):
                ready()
                wait(pool, "n_mean", k + 1)
                then("n_cent", k + 1, nc.gpsimd.tensor_tensor(heads(t_c), src, bc(t_stat[:, 0, 1, :], DH), ALU.subtract))
                nc.gpsimd.tensor_tensor(t_sq[:, :, :], t_c[:, :, :], t_c[:, :, :], ALU.mult).then_inc(s["n_sq"], 1)
                wait(pool, "n_eps", k + 1)
                then("n_root", k + 1, nc.gpsimd.tensor_tensor(t_stat[:, 1, 2, :], t_stat[:, 1, 1, :], t_half[:, :], ALU.pow))
                then("n_out", k + 1, nc.gpsimd.tensor_tensor(heads(dst), heads(t_c), bc(t_stat[:, 1, 2, :], DH), ALU.mult))
                for name, w, op in (("n_g", gain, ALU.mult), ("n_b", bias, ALU.add)):
                    then(name, k + 1, nc.gpsimd.tensor_tensor(
                        dst[:, :, :], dst[:, :, :], tw.fw(w).unsqueeze(1).to_broadcast([P, NT, D]), op))

            def norm_mixed(b):
                norm(mix[:, :, :, :].rearrange("p t n f -> p (t n) f"), fx, "ln_g", "ln_b", 2 * b,
                     lambda: wait(pool, "y_sb", b))

            def add_mixed(b):
                wait(pool, "y_sb", b + 1)
                then("y_add", b + 1, nc.gpsimd.tensor_tensor(y[:, :, :], y[:, :, :], fx[:, :, :], ALU.add))

            def norm_out(b):
                norm(heads(y), y, "fn_g", "fn_b", 2 * b + 1, lambda: None)

            def finish(b):
                wait(pool, "z_rec", b + 1)
                then("z_w", b + 1, nc.gpsimd.tensor_tensor(fg[:, 2], fg[:, 1], bc(fz[:, 1, :], NH), ALU.mult))
                wait(pool, "stored", 16 * b)
                then("z_o", b + 1, nc.gpsimd.tensor_tensor(
                    heads(o), heads(y), bc(fg[:, 2].rearrange("p t n -> p (t n)"), DH), ALU.mult))
                nc.gpsimd.tensor_tensor(o[:, :, :], o[:, :, :], tw.h_at(b), ALU.add).then_inc(s["z_add"], 1)

            prime(pool, [ln.rstd, ln.out])
            nc.gpsimd.memset(tri[:, :], 0.0).then_inc(s["n_tri"], 1)
            wait(pool, "n_tri", 1)
            nc.gpsimd.affine_select(out=mask_q[:, :], in_=tri[:, :], pattern=[[-1, P]], compare_op=ALU.is_ge,
                                    fill=NEG, base=0, channel_multiplier=1)
            nc.gpsimd.affine_select(out=mask_k[:, :], in_=tri[:, :], pattern=[[1, P]], compare_op=ALU.is_ge,
                                    fill=NEG, base=0, channel_multiplier=-1).then_inc(s["consts_p"], 1)
            normalise(0)

            def body(b, first, last):
                for n in range(NH):
                    g = NH * b + n
                    head_before = not (first and n == 0)
                    if n == 1 and not first:
                        norm_mixed(b - 1)
                    if n == 3 and not first:
                        add_mixed(b - 1)
                    if head_before:
                        gate_products(g - 1, (n - 1) % NH)
                    if n == 0 and not last:
                        normalise(b + 1)
                    if n == 3 and not first:
                        norm_out(b - 1)
                    if head_before:
                        gate_weights(g - 1, (n - 1) % NH)
                        gate_residual(g - 1, (n - 1) % NH)
                    if n == 3 and not first:
                        finish(b - 1)

            body(0, True, False)
            with pool.Fori(1, B - 1) as b:
                body(b, False, False)
            body(B - 1, False, True)
            gate_products(NH * B - 1, NH - 1)
            gate_weights(NH * B - 1, NH - 1)
            gate_residual(NH * B - 1, NH - 1)
            norm_mixed(B - 1)
            add_mixed(B - 1)
            norm_out(B - 1)
            finish(B - 1)


def program(nc, x, tok_w, weights, f_weights, h_weights, consts, out):
    with ExitStack() as ctx:
        tw = Tower(nc, ctx)
        tw.head_weights = h_weights
        with nc.sbuf_tensor("w", [P, W_COLS], F32) as tw.w:
            load_inputs(tw, weights, f_weights, consts)
            tokens(tw, x, tok_w)
            linear_attention(tw)
            routed_ffn(tw)
            softmax_attention(tw)
        expert_attention(tw, out)


def pack(x):
    tables = (WEIGHTS, F_WEIGHTS, H_WEIGHTS)
    packed = [np.zeros((P, cols), np.float32) for cols in (W_COLS, F_COLS, H_COLS)]

    def put(name, a, lo=0, row=0):
        a = np.asarray(a, np.float32)
        k = [name in t for t in tables].index(True)
        out, table = packed[k], tables[k]
        at = table[name][1] + lo
        out[row:row + a.shape[0], at:at + a.shape[1]] = a

    qkv = np.asarray(x["L0_attn_W_qkv"]).reshape(16, 12, D)
    qkv_b = np.asarray(x["L0_attn_b_qkv"]).reshape(16, 12)
    part = [qkv[:, 4 * j:4 * j + 4].reshape(64, D) for j in range(3)]
    part_b = [qkv_b[:, 4 * j:4 * j + 4].reshape(64, 1) for j in range(3)]
    put("kvT", np.concatenate([part[1], part[2]]))
    put("kvT", np.concatenate([part_b[1], part_b[2]]), lo=64)
    for name, w, b in (("ak", "L0_attn_kln_w", "L0_attn_kln_b"), ("av", "L0_attn_vln_w", "L0_attn_vln_b")):
        for j, v in enumerate(np.asarray(x[w]).reshape(64)):
            put(name, v.reshape(1, 1), lo=j, row=j)
        put(name, np.asarray(x[b]).reshape(1, 64), row=64)
    put("wqT", part[0])
    put("wqT", part_b[0], lo=64)
    put("wpT", np.asarray(x["L0_attn_W_proj"]).T)
    put("bp", np.asarray(x["L0_attn_b_proj"]).reshape(1, 64), row=64)
    for k in range(2):
        put("rw1", x["L0_ffn_router_w1"], row=64 * k)
        put("eb3", x["L0_ffn_expert_b3"], row=32 * k)
    put("rb1", np.asarray(x["L0_ffn_router_b1"]).reshape(32, 1))
    put("rb1", np.ones((1, 1)), row=32)
    put("rw2", x["L0_ffn_router_w2"])
    put("rw2", np.asarray(x["L0_ffn_router_b2"]).reshape(1, E6), row=32)
    for e in range(E6):
        for k in range(2):
            put("ew1", x["L0_ffn_expert_w1"][e], lo=64 * e, row=64 * k)
        put("eb1", np.asarray(x["L0_ffn_expert_b1"][e]).reshape(64, 1), lo=e // 2, row=64 * (e % 2))
        put("ew2", x["L0_ffn_expert_w2"][e], lo=64 * e, row=64 * (e % 2))
        put("eb2", np.asarray(x["L0_ffn_expert_b2"][e]).reshape(64, 1), lo=e // 2, row=64 * (e % 2))
        put("ew3", x["L0_ffn_expert_w3"][e], lo=64 * (e // 2), row=64 * (e % 2))
    for j in range(2):
        for k in range(2):
            put("wqq", np.asarray(x["L1_attn_Wq"]).T, lo=64 * j, row=64 * k)
            put("wkk", np.asarray(x["L1_attn_Wk"]).T, lo=64 * j, row=64 * k)
        put("wv1", np.asarray(x["L1_attn_Wv"]).T, row=64 * j)
    one = np.ones((1, 1))
    for n in range(NH):
        hl_w, hl_b = np.asarray(x["L1_ffn_hl_w"][n]), np.asarray(x["L1_ffn_hl_b"][n])
        for k in range(2):
            put("hl_w", hl_w, lo=128 * n + 64 * k)
        put("hl_b", np.broadcast_to(hl_b.reshape(DH, 1), (DH, P)), lo=128 * n)
        put("hl_b", np.ones((1, P)), lo=128 * n, row=DH)
        put("hlres", hl_w.T, lo=DH * n)
        put("hlres", hl_b.reshape(1, DH), lo=DH * n, row=64)
        at = 322 * n
        for e in range(NE):
            for k in range(2):
                put("hlmask", hl_w.T, lo=128 * n + 32 * e, row=64 * k)
            put("hlmask_b", hl_b.reshape(DH, 1), lo=n, row=32 * e)
            put("hlmask_b", one, lo=n, row=32 * e + DH)
            for g in range(3):
                put("proj", np.asarray(x["L1_ffn_wq"][n, e]).T, lo=at + 96 * (e // 2) + 32 * g + DH * (e % 2))
        for g in range(3):
            put("proj", np.asarray(x["L1_ffn_wk"][n]).T, lo=at + 192 + 32 * g)
        put("proj", one, lo=at + 192 + 96, row=DH)
        put("proj", np.asarray(x["L1_ffn_wv"][n]).T, lo=at + 290)
        put("proj", one, lo=at + 290 + DH, row=DH)
        for e in range(NE):
            put("gate", np.eye(DH), lo=84 * n + DH * e, row=32 * e)
            put("gate", one, lo=84 * n + 64 + e, row=32 * e + DH)
            for f in range(NE):
                put("gate", np.asarray(x["L1_ffn_gate_w"][n, e, DH * f:DH * f + DH]).reshape(DH, 1),
                    lo=84 * n + 68 + NE * e + f, row=32 * f)
        put("fgate", np.asarray(x["L1_ffn_fgate_w"]).T)
        put("fc1", np.asarray(x["L1_ffn_fc1_w"]).T, lo=DH * n, row=DH * n)
        put("fc1_b", np.asarray(x["L1_ffn_fc1_b"]).reshape(DH, 1), row=DH * n)
        put("fc2", np.asarray(x["L1_ffn_fc2_w"]).T, lo=DH * n, row=DH * n)
        put("fc2", np.asarray(x["L1_ffn_fc2_b"]).reshape(1, DH), lo=DH * n, row=64)
        for name, w in (("ln_g", "ln_g"), ("ln_b", "ln_b"), ("fn_g", "fnorm_g"), ("fn_b", "fnorm_b")):
            put(name, np.broadcast_to(np.asarray(x["L1_ffn_" + w]), (P, DH)), lo=DH * n)
    put("gate_b", np.broadcast_to(np.asarray(x["L1_ffn_gate_b"]).reshape(NH * NE), (P, NH * NE)))
    return packed


def kernel(**inputs):
    import concourse.bacc as bacc
    from concourse.bass_utils import run_bass_kernel_spmd

    nc = bacc.Bacc("TRN2", target_bir_lowering=False, num_devices=1)
    weights, f_weights, h_weights = pack(inputs)
    arrays = {
        "x": np.ascontiguousarray(inputs["x"]),
        "tok_w": np.ascontiguousarray(
            np.asarray(inputs["L0_tok_W"]).reshape(D, 2 * NF, C).transpose(1, 0, 2).reshape(2 * NF, D * C)),
        "weights": weights,
        "f_weights": f_weights,
        "h_weights": h_weights,
        "consts": constants(),
    }
    args = {n: nc.dram_tensor(n, a.shape, mybir.dt.from_np(a.dtype), kind="ExternalInput").ap()
            for n, a in arrays.items()}
    out = nc.dram_tensor("out", (B, S, D), F32, kind="ExternalOutput").ap()
    program(nc, out=out, **args)
    return run_bass_kernel_spmd(nc, [arrays], core_ids=[0]).results[0]["out"]
```
